# Optimizing a Trainium2 kernel written in Bass

```python
import numpy as np
import jax
import jax.numpy as jnp

def _softmax(x, axis=-1):
    return jax.nn.softmax(x, axis=axis)

def _gelu(x):
    return jax.nn.gelu(x, approximate=True)

def _silu(x):
    return jax.nn.silu(x)

def _sigmoid(x):
    return jax.nn.sigmoid(x)

def _layernorm(x, axis=-1, eps=1e-05):
    m = jnp.mean(x, axis=axis, keepdims=True)
    v = jnp.var(x, axis=axis, keepdims=True)
    return (x - m) / jnp.sqrt(v + eps)

def _scatter_add(tgt, idx, src, axis=0):
    return tgt.at[idx].add(src)

def _segment_sum(src, seg, n):
    return jax.ops.segment_sum(src, seg, n)
kernel_name = 'mk_hybrid_d2_jaxref_r8_eb51c3'

def setup_inputs(seed: int=0):
    np.random.seed(seed)
    _w = jnp.asarray

    def _L0_attn_a_setup():
        import jax, jax.numpy as jnp
        import numpy as np
        EMB_DIM = 128
        B, T = (4, 256)
        key = jax.random.key(seed)
        kx, kq, kk, kv = jax.random.split(key, 4)
        s = 1.0 / np.sqrt(EMB_DIM)
        return {'x': jax.random.normal(kx, (B, T, EMB_DIM), dtype=jnp.float32), 'Wq': jax.random.normal(kq, (EMB_DIM, EMB_DIM), dtype=jnp.float32) * s, 'Wk': jax.random.normal(kk, (EMB_DIM, EMB_DIM), dtype=jnp.float32) * s, 'Wv': jax.random.normal(kv, (EMB_DIM, EMB_DIM), dtype=jnp.float32) * s}
    _L0_attn_a_in = _L0_attn_a_setup()

    def _L0_attn_b_setup():
        import jax, jax.numpy as jnp
        import numpy as np
        NUM_HEADS = 16
        key = jax.random.key(seed)
        ks = jax.random.split(key, 6)
        B, S, D = (2, 256, 128)
        x = jax.random.normal(ks[0], (B, S, D), dtype=jnp.float32)
        s = 1.0 / np.sqrt(D)
        Wq = jax.random.normal(ks[1], (D, D), dtype=jnp.float32) * s
        Wk = jax.random.normal(ks[2], (D, D), dtype=jnp.float32) * s
        Wv = jax.random.normal(ks[3], (D, D), dtype=jnp.float32) * s
        Wff = jax.random.normal(ks[4], (D, D), dtype=jnp.float32) * s
        bff = jax.random.normal(ks[5], (D,), dtype=jnp.float32) * 0.01
        return {'x': x, 'Wq': Wq, 'Wk': Wk, 'Wv': Wv, 'Wff': Wff, 'bff': bff}
    _L0_attn_b_in = _L0_attn_b_setup()

    def _L0_ffn_setup():
        import jax, jax.numpy as jnp
        import numpy as np
        B, T, D, E, H = (4, 256, 128, 4, 8)
        EPS = 1e-05

        def _uniform(k, shape, bound):
            return jax.random.uniform(k, shape, jnp.float32, -bound, bound)

        def _layernorm(x, w, b):
            mu = jnp.mean(x, axis=-1, keepdims=True)
            var = jnp.mean(jnp.square(x - mu), axis=-1, keepdims=True)
            return (x - mu) * jax.lax.rsqrt(var + EPS) * w + b
        key = jax.random.key(seed)
        ks = jax.random.split(key, 12)
        wb = np.sqrt(6.0 / D) / np.sqrt(6.0)
        wb = 1.0 / np.sqrt(D)
        return {'x': jax.random.normal(ks[0], (B, T, D), jnp.float32), 'router_prob': jax.random.uniform(ks[1], (B, T, E), jnp.float32), 'norm_w': jnp.ones((D,), jnp.float32), 'norm_b': jnp.zeros((D,), jnp.float32), 'q_w': _uniform(ks[2], (D, D), wb), 'q_b': _uniform(ks[3], (D,), wb), 'k_w': _uniform(ks[4], (D, D), wb), 'k_b': _uniform(ks[5], (D,), wb), 'v_w': _uniform(ks[6], (D, D), wb), 'v_b': _uniform(ks[7], (D,), wb), 'o_w': _uniform(ks[8], (D, D), wb), 'o_b': _uniform(ks[9], (D,), wb)}
    _L0_ffn_in = _L0_ffn_setup()

    def _L1_attn_a_setup():
        import jax, jax.numpy as jnp
        import numpy as np
        B, N, DIM = (2, 512, 128)
        H, DH, F = (16, 64, 32)
        key = jax.random.key(seed)
        ks = jax.random.split(key, 12)
        s = 1.0 / np.sqrt(DIM)
        inp = {'x': jax.random.normal(ks[0], (B, N, DIM), jnp.float32), 'Wq': jax.random.normal(ks[1], (DIM, H * DH), jnp.float32) * s, 'bq': jax.random.normal(ks[2], (H * DH,), jnp.float32) * 0.02, 'Wk': jax.random.normal(ks[3], (DIM, H * DH), jnp.float32) * s, 'bk': jax.random.normal(ks[4], (H * DH,), jnp.float32) * 0.02, 'Wv': jax.random.normal(ks[5], (DIM, H * DH), jnp.float32) * s, 'bv': jax.random.normal(ks[6], (H * DH,), jnp.float32) * 0.02, 'Wproj': jax.random.normal(ks[7], (H * DH, DIM), jnp.float32) * s, 'bproj': jax.random.normal(ks[8], (DIM,), jnp.float32) * 0.02, 'wq_feat': jax.random.normal(ks[9], (DH, F), jnp.float32) / np.sqrt(DH), 'wk_feat': jax.random.normal(ks[10], (DH, F), jnp.float32) / np.sqrt(DH)}
        return inp
    _L1_attn_a_in = _L1_attn_a_setup()

    def _L1_attn_b_setup():
        import jax, jax.numpy as jnp
        import numpy as np
        B, L, HID = (2, 256, 128)
        H = 16
        D = HID // H
        LR = 16
        EPS = 1e-05
        GLN = 16.0
        SCALE = D ** (-0.5)

        def _reference_tuple_inner(x, Wq, Wk, Wv, Wg1, Wg2, bg2, Wg, g_norm_w, Wo):
            Bb, Ll, Hid = x.shape
            q = (x @ Wq).reshape(Bb, Ll, H, D)
            k = (x @ Wk).reshape(Bb, Ll, H, D)
            v = (x @ Wv).reshape(Bb, Ll, H, D)
            gk = jax.nn.log_sigmoid(x @ Wg1 @ Wg2 + bg2).reshape(Bb, Ll, H, D) / GLN

            def step(S, inp):
                q_t, k_t, v_t, gk_t = inp
                S = jnp.exp(gk_t)[..., None] * S + k_t[..., None] * v_t[..., None, :]
                o_t = jnp.einsum('bhdv,bhd->bhv', S, q_t) * SCALE
                return (S, o_t)
            S0 = jnp.zeros((Bb, H, D, D), x.dtype)
            scan_in = tuple((jnp.moveaxis(t, 1, 0) for t in (q, k, v, gk)))
            S, o = jax.lax.scan(step, S0, scan_in)
            o = jnp.moveaxis(o, 0, 1)
            o = o * jax.lax.rsqrt(jnp.mean(o * o, axis=-1, keepdims=True) + EPS) * g_norm_w
            o = o.reshape(Bb, Ll, Hid)
            g = x @ Wg
            o = o * (g * jax.nn.sigmoid(g))
            o = o @ Wo
            return (o, S[:, None])
        key = jax.random.key(seed)
        ks = jax.random.split(key, 9)
        s = 0.02
        return {'x': jax.random.normal(ks[0], (B, L, HID), jnp.float32), 'Wq': jax.random.normal(ks[1], (HID, HID), jnp.float32) * s, 'Wk': jax.random.normal(ks[2], (HID, HID), jnp.float32) * s, 'Wv': jax.random.normal(ks[3], (HID, HID), jnp.float32) * s, 'Wg1': jax.random.normal(ks[4], (HID, LR), jnp.float32) * s, 'Wg2': jax.random.normal(ks[5], (LR, HID), jnp.float32) * s, 'bg2': jnp.zeros((HID,), jnp.float32), 'Wg': jax.random.normal(ks[6], (HID, HID), jnp.float32) * s, 'g_norm_w': jnp.ones((D,), jnp.float32), 'Wo': jax.random.normal(ks[7], (HID, HID), jnp.float32) * s}
    _L1_attn_b_in = _L1_attn_b_setup()

    def _L1_ffn_setup():
        import jax, jax.numpy as jnp
        import numpy as np
        B, S, D, E, H, K = (4, 256, 128, 8, 512, 2)
        EPS = 1e-06

        def _ln(x, scale, bias):
            m = jnp.mean(x, axis=-1, keepdims=True)
            v = jnp.mean(jnp.square(x - m), axis=-1, keepdims=True)
            return (x - m) * jax.lax.rsqrt(v + EPS) * scale + bias
        key = jax.random.key(seed)
        ks = jax.random.split(key, 4)
        s1 = 1.0 / np.sqrt(D)
        s2 = 1.0 / np.sqrt(H)
        return {'x': jax.random.normal(ks[0], (B, S, D), jnp.float32), 'router_ln_scale': jnp.ones((D,), jnp.float32), 'router_ln_bias': jnp.zeros((D,), jnp.float32), 'router_w': jax.random.normal(ks[1], (E, D), jnp.float32) * s1, 'router_b': jnp.zeros((E,), jnp.float32), 'expert_ln_scale': jnp.ones((E, D), jnp.float32), 'expert_ln_bias': jnp.zeros((E, D), jnp.float32), 'w1': jax.random.normal(ks[2], (E, H, D), jnp.float32) * s1, 'b1': jnp.zeros((E, H), jnp.float32), 'w2': jax.random.normal(ks[3], (E, D, H), jnp.float32) * s2, 'b2': jnp.zeros((E, D), jnp.float32)}
    _L1_ffn_in = _L1_ffn_setup()
    _d = {'L0_attn_a_x': _L0_attn_a_in['x'], 'L0_attn_a_Wq': _L0_attn_a_in['Wq'], 'L0_attn_a_Wk': _L0_attn_a_in['Wk'], 'L0_attn_a_Wv': _L0_attn_a_in['Wv'], 'L0_attn_b_Wq': _L0_attn_b_in['Wq'], 'L0_attn_b_Wk': _L0_attn_b_in['Wk'], 'L0_attn_b_Wv': _L0_attn_b_in['Wv'], 'L0_attn_b_Wff': _L0_attn_b_in['Wff'], 'L0_attn_b_bff': _L0_attn_b_in['bff'], 'L0_ffn_router_prob': _L0_ffn_in['router_prob'], 'L0_ffn_norm_w': _L0_ffn_in['norm_w'], 'L0_ffn_norm_b': _L0_ffn_in['norm_b'], 'L0_ffn_q_w': _L0_ffn_in['q_w'], 'L0_ffn_q_b': _L0_ffn_in['q_b'], 'L0_ffn_k_w': _L0_ffn_in['k_w'], 'L0_ffn_k_b': _L0_ffn_in['k_b'], 'L0_ffn_v_w': _L0_ffn_in['v_w'], 'L0_ffn_v_b': _L0_ffn_in['v_b'], 'L0_ffn_o_w': _L0_ffn_in['o_w'], 'L0_ffn_o_b': _L0_ffn_in['o_b'], 'L1_attn_a_Wq': _L1_attn_a_in['Wq'], 'L1_attn_a_bq': _L1_attn_a_in['bq'], 'L1_attn_a_Wk': _L1_attn_a_in['Wk'], 'L1_attn_a_bk': _L1_attn_a_in['bk'], 'L1_attn_a_Wv': _L1_attn_a_in['Wv'], 'L1_attn_a_bv': _L1_attn_a_in['bv'], 'L1_attn_a_Wproj': _L1_attn_a_in['Wproj'], 'L1_attn_a_bproj': _L1_attn_a_in['bproj'], 'L1_attn_a_wq_feat': _L1_attn_a_in['wq_feat'], 'L1_attn_a_wk_feat': _L1_attn_a_in['wk_feat'], 'L1_attn_b_Wq': _L1_attn_b_in['Wq'], 'L1_attn_b_Wk': _L1_attn_b_in['Wk'], 'L1_attn_b_Wv': _L1_attn_b_in['Wv'], 'L1_attn_b_Wg1': _L1_attn_b_in['Wg1'], 'L1_attn_b_Wg2': _L1_attn_b_in['Wg2'], 'L1_attn_b_bg2': _L1_attn_b_in['bg2'], 'L1_attn_b_Wg': _L1_attn_b_in['Wg'], 'L1_attn_b_g_norm_w': _L1_attn_b_in['g_norm_w'], 'L1_attn_b_Wo': _L1_attn_b_in['Wo'], 'L1_ffn_router_ln_scale': _L1_ffn_in['router_ln_scale'], 'L1_ffn_router_ln_bias': _L1_ffn_in['router_ln_bias'], 'L1_ffn_router_w': _L1_ffn_in['router_w'], 'L1_ffn_router_b': _L1_ffn_in['router_b'], 'L1_ffn_expert_ln_scale': _L1_ffn_in['expert_ln_scale'], 'L1_ffn_expert_ln_bias': _L1_ffn_in['expert_ln_bias'], 'L1_ffn_w1': _L1_ffn_in['w1'], 'L1_ffn_b1': _L1_ffn_in['b1'], 'L1_ffn_w2': _L1_ffn_in['w2'], 'L1_ffn_b2': _L1_ffn_in['b2']}
    _x0 = _d['L0_attn_a_x']
    _d['L0_attn_a_x'] = jax.random.normal(jax.random.fold_in(jax.random.key(seed), 1), (4, 1024, 128), dtype=_x0.dtype)
    del _x0
    return _d

def reference(L0_attn_a_x, L0_attn_a_Wq, L0_attn_a_Wk, L0_attn_a_Wv, L0_attn_b_Wq, L0_attn_b_Wk, L0_attn_b_Wv, L0_attn_b_Wff, L0_attn_b_bff, L0_ffn_router_prob, L0_ffn_norm_w, L0_ffn_norm_b, L0_ffn_q_w, L0_ffn_q_b, L0_ffn_k_w, L0_ffn_k_b, L0_ffn_v_w, L0_ffn_v_b, L0_ffn_o_w, L0_ffn_o_b, L1_attn_a_Wq, L1_attn_a_bq, L1_attn_a_Wk, L1_attn_a_bk, L1_attn_a_Wv, L1_attn_a_bv, L1_attn_a_Wproj, L1_attn_a_bproj, L1_attn_a_wq_feat, L1_attn_a_wk_feat, L1_attn_b_Wq, L1_attn_b_Wk, L1_attn_b_Wv, L1_attn_b_Wg1, L1_attn_b_Wg2, L1_attn_b_bg2, L1_attn_b_Wg, L1_attn_b_g_norm_w, L1_attn_b_Wo, L1_ffn_router_ln_scale, L1_ffn_router_ln_bias, L1_ffn_router_w, L1_ffn_router_b, L1_ffn_expert_ln_scale, L1_ffn_expert_ln_bias, L1_ffn_w1, L1_ffn_b1, L1_ffn_w2, L1_ffn_b2):

    def _L0_attn_a_ref(x, Wq, Wk, Wv):
        import jax, jax.numpy as jnp
        import numpy as np
        EMB_DIM = 128
        B, T = (4, 256)
        B_, T_, C = x.shape
        q = jnp.einsum('btc,dc->btd', x, Wq)
        k = jnp.einsum('btc,dc->btd', x, Wk)
        v = jnp.einsum('btc,dc->btd', x, Wv)
        scale = jnp.asarray(C, x.dtype) ** (-0.5)
        wei = jnp.einsum('btd,bsd->bts', q, k) * scale
        causal = jnp.tril(jnp.ones((T_, T_), dtype=bool))
        wei = jnp.where(causal, wei, jnp.asarray(-jnp.inf, x.dtype))
        wei = jax.nn.softmax(wei, axis=-1)
        out = jnp.einsum('bts,bsd->btd', wei, v)
        return out

    def _L0_attn_b_ref(x, Wq, Wk, Wv, Wff, bff):
        import jax, jax.numpy as jnp
        import numpy as np
        NUM_HEADS = 16
        B, S, D = x.shape
        H = NUM_HEADS
        Dh = D // H
        q = x @ Wq.T * (1.0 / jnp.sqrt(jnp.asarray(D, x.dtype)))
        k = x @ Wk.T
        v = x @ Wv.T
        q = q.reshape(B, S, H, Dh)
        k = k.reshape(B, S, H, Dh)
        v = v.reshape(B, S, H, Dh)
        scores = jnp.einsum('bqhd,bkhd->bhqk', q, k)
        attn = jax.nn.softmax(scores, axis=-1)
        out = jnp.einsum('bhqk,bkhd->bqhd', attn, v).reshape(B, S, D)
        return out @ Wff.T + bff

    def _L0_ffn_ref(x, router_prob, norm_w, norm_b, q_w, q_b, k_w, k_b, v_w, v_b, o_w, o_b):
        import jax, jax.numpy as jnp
        import numpy as np
        B, T, D, E, H = (4, 256, 128, 4, 8)
        EPS = 1e-05

        def _uniform(k, shape, bound):
            return jax.random.uniform(k, shape, jnp.float32, -bound, bound)

        def _layernorm(x, w, b):
            mu = jnp.mean(x, axis=-1, keepdims=True)
            var = jnp.mean(jnp.square(x - mu), axis=-1, keepdims=True)
            return (x - mu) * jax.lax.rsqrt(var + EPS) * w + b
        e_cnt = router_prob.shape[2]
        b, t, d = x.shape
        n = t // e_cnt
        h = H
        scale = d ** (-0.5)
        qs, ks_, vs = ([], [], [])
        for e in range(e_cnt):
            xe = x[:, e * n:(e + 1) * n, :]
            xn = _layernorm(xe, norm_w, norm_b)
            m = d // 2 ** e
            xm = xn[..., :m]
            qs.append(jnp.einsum('bnm,dm->bnd', xm, q_w[:, :m]) + q_b)
            ks_.append(jnp.einsum('bnm,dm->bnd', xm, k_w[:, :m]) + k_b)
            vs.append(jnp.einsum('bnm,dm->bnd', xm, v_w[:, :m]) + v_b)
        q = jnp.concatenate(qs, axis=1)
        k = jnp.concatenate(ks_, axis=1)
        v = jnp.concatenate(vs, axis=1)
        dh = d // h
        q = q.reshape(b, t, h, dh).transpose(0, 2, 1, 3)
        k = k.reshape(b, t, h, dh).transpose(0, 2, 1, 3)
        v = v.reshape(b, t, h, dh).transpose(0, 2, 1, 3)
        attn = jnp.einsum('bhqd,bhkd->bhqk', q, k) * scale
        attn = jax.nn.softmax(attn, axis=-1)
        attn_out = jnp.einsum('bhqk,bhkd->bhqd', attn, v)
        attn_out = attn_out.transpose(0, 2, 1, 3).reshape(b, t, d)
        outs = []
        for e in range(e_cnt):
            sl = slice(e * n, (e + 1) * n)
            m = d // 2 ** e
            xm = attn_out[:, sl, :m]
            out = jnp.einsum('bnm,om->bno', xm, o_w[:m, :m]) + o_b[:m]
            pad = d - m
            if pad:
                out = jnp.pad(out, ((0, 0), (0, 0), (0, pad)))
            outs.append(out + x[:, sl, :])
        return jnp.concatenate(outs, axis=1)

    def _L1_attn_a_ref(x, Wq, bq, Wk, bk, Wv, bv, Wproj, bproj, wq_feat, wk_feat):
        import jax, jax.numpy as jnp
        import numpy as np
        B, N, DIM = (2, 512, 128)
        H, DH, F = (16, 64, 32)
        b, n, _ = x.shape
        q = (x @ Wq + bq).reshape(b, n, H, DH)
        k = (x @ Wk + bk).reshape(b, n, H, DH)
        v = (x @ Wv + bv).reshape(b, n, H, DH)
        q_prime = jnp.exp(jnp.einsum('bnhd,df->bnhf', q, wq_feat))
        k_prime = jnp.exp(jnp.einsum('bnhd,df->bnhf', k, wk_feat))
        k_sum = k_prime.sum(axis=1)
        D_inv = 1.0 / (jnp.einsum('bnhf,bhf->bnh', q_prime, k_sum) + 1e-06)
        context = jnp.einsum('bnhf,bnhd->bhfd', k_prime, v)
        out = jnp.einsum('bnhf,bhfd,bnh->bnhd', q_prime, context, D_inv)
        out = out.reshape(b, n, H * DH)
        return out @ Wproj + bproj

    def _L1_attn_b_ref(x, Wq, Wk, Wv, Wg1, Wg2, bg2, Wg, g_norm_w, Wo):
        import jax, jax.numpy as jnp
        import numpy as np
        B, L, HID = (2, 256, 128)
        H = 16
        D = HID // H
        LR = 16
        EPS = 1e-05
        GLN = 16.0
        SCALE = D ** (-0.5)

        def _reference_tuple_inner(x, Wq, Wk, Wv, Wg1, Wg2, bg2, Wg, g_norm_w, Wo):
            Bb, Ll, Hid = x.shape
            q = (x @ Wq).reshape(Bb, Ll, H, D)
            k = (x @ Wk).reshape(Bb, Ll, H, D)
            v = (x @ Wv).reshape(Bb, Ll, H, D)
            gk = jax.nn.log_sigmoid(x @ Wg1 @ Wg2 + bg2).reshape(Bb, Ll, H, D) / GLN

            def step(S, inp):
                q_t, k_t, v_t, gk_t = inp
                S = jnp.exp(gk_t)[..., None] * S + k_t[..., None] * v_t[..., None, :]
                o_t = jnp.einsum('bhdv,bhd->bhv', S, q_t) * SCALE
                return (S, o_t)
            S0 = jnp.zeros((Bb, H, D, D), x.dtype)
            scan_in = tuple((jnp.moveaxis(t, 1, 0) for t in (q, k, v, gk)))
            S, o = jax.lax.scan(step, S0, scan_in)
            o = jnp.moveaxis(o, 0, 1)
            o = o * jax.lax.rsqrt(jnp.mean(o * o, axis=-1, keepdims=True) + EPS) * g_norm_w
            o = o.reshape(Bb, Ll, Hid)
            g = x @ Wg
            o = o * (g * jax.nn.sigmoid(g))
            o = o @ Wo
            return (o, S[:, None])
        return _reference_tuple_inner(x, Wq, Wk, Wv, Wg1, Wg2, bg2, Wg, g_norm_w, Wo)[0]

    def _L1_ffn_ref(x, router_ln_scale, router_ln_bias, router_w, router_b, expert_ln_scale, expert_ln_bias, w1, b1, w2, b2):
        import jax, jax.numpy as jnp
        import numpy as np
        B, S, D, E, H, K = (4, 256, 128, 8, 512, 2)
        EPS = 1e-06

        def _ln(x, scale, bias):
            m = jnp.mean(x, axis=-1, keepdims=True)
            v = jnp.mean(jnp.square(x - m), axis=-1, keepdims=True)
            return (x - m) * jax.lax.rsqrt(v + EPS) * scale + bias
        orig_shape = x.shape
        xf = x.reshape(-1, D)
        T = xf.shape[0]
        logits = _ln(xf, router_ln_scale, router_ln_bias) @ router_w.T + router_b
        probs = jax.nn.softmax(logits, axis=-1)
        topw, topi = jax.lax.top_k(probs, K)
        topw = topw / jnp.sum(topw, axis=-1, keepdims=True)
        gates = jnp.zeros((T, E), xf.dtype).at[jnp.arange(T)[:, None], topi].set(topw)

        def expert(ls, lb, W1, B1, W2, B2):
            h = jax.nn.gelu(_ln(xf, ls, lb) @ W1.T + B1, approximate=False)
            return h @ W2.T + B2
        ys = jax.vmap(expert)(expert_ln_scale, expert_ln_bias, w1, b1, w2, b2)
        out = jnp.einsum('te,etd->td', gates, ys)
        return out.reshape(orig_shape)
    x = L0_attn_a_x
    x = x + _L0_attn_a_ref(_layernorm(x, axis=-1), L0_attn_a_Wq, L0_attn_a_Wk, L0_attn_a_Wv)
    x = x + _L0_ffn_ref(_layernorm(x, axis=-1), L0_ffn_router_prob, L0_ffn_norm_w, L0_ffn_norm_b, L0_ffn_q_w, L0_ffn_q_b, L0_ffn_k_w, L0_ffn_k_b, L0_ffn_v_w, L0_ffn_v_b, L0_ffn_o_w, L0_ffn_o_b)
    x = x + _L0_attn_b_ref(_layernorm(x, axis=-1), L0_attn_b_Wq, L0_attn_b_Wk, L0_attn_b_Wv, L0_attn_b_Wff, L0_attn_b_bff)
    x = x + _L0_ffn_ref(_layernorm(x, axis=-1), L0_ffn_router_prob, L0_ffn_norm_w, L0_ffn_norm_b, L0_ffn_q_w, L0_ffn_q_b, L0_ffn_k_w, L0_ffn_k_b, L0_ffn_v_w, L0_ffn_v_b, L0_ffn_o_w, L0_ffn_o_b)
    x = x + _L1_attn_a_ref(_layernorm(x, axis=-1), L1_attn_a_Wq, L1_attn_a_bq, L1_attn_a_Wk, L1_attn_a_bk, L1_attn_a_Wv, L1_attn_a_bv, L1_attn_a_Wproj, L1_attn_a_bproj, L1_attn_a_wq_feat, L1_attn_a_wk_feat)
    x = x + _L1_ffn_ref(_layernorm(x, axis=-1), L1_ffn_router_ln_scale, L1_ffn_router_ln_bias, L1_ffn_router_w, L1_ffn_router_b, L1_ffn_expert_ln_scale, L1_ffn_expert_ln_bias, L1_ffn_w1, L1_ffn_b1, L1_ffn_w2, L1_ffn_b2)
    x = x + _L1_attn_b_ref(_layernorm(x, axis=-1), L1_attn_b_Wq, L1_attn_b_Wk, L1_attn_b_Wv, L1_attn_b_Wg1, L1_attn_b_Wg2, L1_attn_b_bg2, L1_attn_b_Wg, L1_attn_b_g_norm_w, L1_attn_b_Wo)
    x = x + _L1_ffn_ref(_layernorm(x, axis=-1), L1_ffn_router_ln_scale, L1_ffn_router_ln_bias, L1_ffn_router_w, L1_ffn_router_b, L1_ffn_expert_ln_scale, L1_ffn_expert_ln_bias, L1_ffn_w1, L1_ffn_b1, L1_ffn_w2, L1_ffn_b2)
    return x

_drawn_inputs = setup_inputs


def setup_inputs(seed=0):
    import zlib

    import numpy as np

    out = dict(_drawn_inputs(seed))
    spreads = {'L0_ffn_norm_w': (1.0, 0.6),
     'L0_ffn_norm_b': (0.0, 0.335),
     'L1_attn_b_bg2': (0.0, 0.8),
     'L1_attn_b_g_norm_w': (1.0, 0.6),
     'L1_ffn_router_ln_scale': (1.0, 0.2),
     'L1_ffn_router_ln_bias': (0.0, 0.1),
     'L1_ffn_router_b': (0.0, 0.1),
     'L1_ffn_expert_ln_scale': (1.0, 0.2),
     'L1_ffn_expert_ln_bias': (0.0, 0.1),
     'L1_ffn_b1': (0.0, 0.1),
     'L1_ffn_b2': (0.0, 0.1)}
    factors = {'L0_attn_b_Wq': 2.753,
     'L0_attn_b_bff': 3.704,
     'L0_ffn_q_w': 8.0,
     'L0_ffn_q_b': 8.0,
     'L0_ffn_k_w': 8.0,
     'L0_ffn_k_b': 64.0,
     'L1_attn_a_bq': 49.487,
     'L1_attn_a_bk': 46.06,
     'L1_attn_a_bproj': 3.802,
     'L1_attn_b_Wq': 4.46,
     'L1_attn_b_Wk': 4.692,
     'L1_attn_b_Wv': 4.628,
     'L1_attn_b_Wg1': 8.0,
     'L1_attn_b_Wg2': 8.0,
     'L1_attn_b_Wg': 4.659,
     'L1_attn_b_Wo': 4.273}
    for name, (base, spread) in spreads.items():
        noise = np.random.default_rng([zlib.crc32(name.encode()), seed]).standard_normal(out[name].shape)
        drawn = base * np.exp(spread * noise) if base else spread * noise
        out[name] = jnp.asarray(drawn.astype(out[name].dtype))
    for name, factor in factors.items():
        out[name] = (out[name] * factor).astype(out[name].dtype)
    return out
```

```python
from contextlib import ExitStack

import concourse.bass as bass
from concourse import mybir

F32 = mybir.dt.float32
F32R = mybir.dt.float32r
BF16 = mybir.dt.bfloat16
ALU = mybir.AluOpType
ACT = mybir.ActivationFunctionType
AX = mybir.AxisListType.X

P = 128
D = 128
B = 4
T = 1024
TILES = T // P
NT = B * TILES
BANK = 512
MASKED = -1.0e30
LN_EPS = 1e-5


class Core:

    def __init__(self, nc, ctx):
        self.nc, self.ctx = nc, ctx
        self.x = ctx.enter_context(nc.sbuf_tensor("x_resident", [P, NT, D], F32))
        self.ident = ctx.enter_context(nc.sbuf_tensor("ident", [P, P], F32))
        self.ident_bf = ctx.enter_context(nc.sbuf_tensor("ident_bf", [P, P], BF16))
        self.minus_half = ctx.enter_context(nc.sbuf_tensor("minus_half", [P, 2 * TILES], F32))
        self.bank = ctx.enter_context(nc.psum_tensor("banks", [P, 8, BANK], F32))
        self.passed = nc.alloc_semaphore(name="passed")
        self.stage = ""

    def sem(self, name):
        return self.nc.alloc_semaphore(name=f"{self.stage}_{name}")

    def sbuf(self, stage_ctx, name, shape, dtype=F32):
        return stage_ctx.enter_context(self.nc.sbuf_tensor(f"{self.stage}_{name}", shape, dtype))


def wait_past(engine, semaphore, value):
    if not (isinstance(value, int) and value <= 0):
        engine.wait_ge(semaphore, value)


def wait_apart(core, engine, semaphore, value):
    engine.wait_ge(semaphore, value)
    engine.sem_inc(core.passed, 1)


def tile_at(x, tile):
    return x[:, bass.ds(tile, 1), :].rearrange("p o d -> p (o d)")


def load_stage(core, x_dram):
    nc = core.nc
    core.stage = "load"
    x_in, filled, shaped = core.sem("x_in"), core.sem("filled"), core.sem("shaped")
    with nc.Block() as block:

        @block.sync
        def _(sp):
            for b in range(B):
                sp.dma_start(core.x[:, b * TILES:(b + 1) * TILES, :],
                             x_dram[b].rearrange("(i p) d -> p i d", p=P)).then_inc(x_in, 16)
            sp.wait_ge(x_in, 16 * B)

        @block.gpsimd
        def _(pool):
            pool.memset(core.ident[:], 0.0).then_inc(filled, 1)
            pool.wait_ge(filled, 1)
            pool.affine_select(out=core.ident[:], in_=core.ident[:], compare_op=ALU.not_equal, fill=1.0,
                               base=0, pattern=[[-1, P]], channel_multiplier=1).then_inc(shaped, 1)
            pool.memset(core.minus_half[:], -0.5).then_inc(filled, 1)
            pool.wait_ge(filled, 2)
            pool.wait_ge(shaped, 1)
            pool.tensor_copy(core.ident_bf[:], core.ident[:]).then_inc(shaped, 1)
            pool.wait_ge(shaped, 2)


def store_stage(core, out_dram):
    nc = core.nc
    core.stage = "store"
    stored = core.sem("stored")
    with nc.Block() as block:

        @block.sync
        def _(sp):
            for b in range(B):
                sp.dma_start(out_dram[b].rearrange("(i p) d -> p i d", p=P),
                             core.x[:, b * TILES:(b + 1) * TILES, :]).then_inc(stored, 16)
            sp.wait_ge(stored, 16 * B)


class LayerNorm:

    STEPS = 2 * TILES

    def __init__(self, core, ctx, name="ln"):
        self.core = core
        self.stats = core.sbuf(ctx, f"{name}_stats", [P, TILES, 6])
        self.moments = core.sbuf(ctx, f"{name}_moments", [P, TILES, 2])
        self.rstd = core.sbuf(ctx, f"{name}_rstd", [P, TILES])
        self.padded = core.sbuf(ctx, f"{name}_padded", [P, TILES])
        self.steps = core.sem(f"{name}_steps")
        self.padded_ready = core.sem(f"{name}_padded_ready")
        self.scaled = core.sem(f"{name}_scaled")

    def moments_of(self, dve, it):
        before = it * self.STEPS
        for i in range(TILES):
            dve.bn_stats(self.stats[:, i, :], tile_at(self.core.x, it * TILES + i)).then_inc(self.steps, 1)
        wait_apart(self.core, dve, self.steps, before + TILES)
        for i in range(TILES):
            dve.bn_aggr(self.moments[:, i, :], self.stats[:, i, :]).then_inc(self.steps, 1)

    def rstd_of(self, pool, it):
        wait_apart(self.core, pool, self.steps, (it + 1) * self.STEPS)
        pool.tensor_scalar(self.padded[:], self.moments[:, :, 1], LN_EPS, None, ALU.add).then_inc(self.padded_ready, 1)
        pool.wait_ge(self.padded_ready, it + 1)
        pool.tensor_tensor(self.rstd[:], self.padded[:], self.core.minus_half[:, 0:TILES], ALU.pow).then_inc(self.scaled, 1)


def causal_stage(core, wq_t, wk_t, wv_t):
    nc, x, bank = core.nc, core.x, core.bank
    core.stage = "causal"
    scale = float(D) ** -0.5
    s_ = core.sem
    w_in, mask_made = s_("w_in"), s_("mask_made")
    normed, turned, ht_copied, projected, qkv_copied = (
        s_("normed"), s_("turned"), s_("ht_copied"), s_("projected"), s_("qkv_copied"))
    scored, masked, maxed, shifted, probs = s_("scored"), s_("masked"), s_("maxed"), s_("shifted"), s_("probs")
    p_turned, pt_copied, mixed, inverted, added = (
        s_("p_turned"), s_("pt_copied"), s_("mixed"), s_("inverted"), s_("added"))
    chunks = T // BANK
    groups = [(qt, g) for qt in range(TILES) for g in range(qt // 4 + 1)]
    NG = len(groups)
    with ExitStack() as ctx:
        sb = lambda name, shape, dtype=F32: core.sbuf(ctx, name, shape, dtype)
        ln = LayerNorm(core, ctx)
        wq, wk, wv = sb("wq", [P, D]), sb("wk", [P, D]), sb("wv", [P, D])
        above = sb("above", [P, P])
        h = sb("h", [P, TILES, D])
        h_t = sb("h_t", [P, T])
        q_t, k_t, v = sb("q_t", [P, T]), sb("k_t", [P, T]), sb("v", [P, TILES, D])
        top, shift, total, inverse = (sb("top", [P, TILES]), sb("shift", [P, TILES]), sb("total", [P, TILES]),
                                      sb("inverse", [P, TILES]))
        p, p_t = sb("p", [P, 2, T]), sb("p_t", [P, 2, T])
        with nc.Block() as block:

            @block.sync
            def _(sp):
                sp.dma_start(wq[:], wq_t).then_inc(w_in, 16)
                sp.dma_start(wk[:], wk_t).then_inc(w_in, 16)
                sp.dma_start(wv[:], wv_t).then_inc(w_in, 16)

            @block.gpsimd
            def _(pool):
                pool.memset(above[:], 0.0).then_inc(mask_made, 1)
                pool.wait_ge(mask_made, 1)
                pool.affine_select(out=above[:], in_=above[:], compare_op=ALU.is_ge, fill=MASKED, base=0,
                                   pattern=[[-1, P]], channel_multiplier=1).then_inc(mask_made, 1)
                with pool.Fori(0, B) as it:
                    ln.rstd_of(pool, it)

            @block.vector
            def _(dve):
                dve.wait_ge(mask_made, 2)
                with dve.Fori(0, B) as it:
                    dve.wait_ge(added, it * TILES)
                    ln.moments_of(dve, it)
                    dve.wait_ge(ln.scaled, it + 1)
                    for i in range(TILES):
                        dve.tensor_scalar(h[:, i, :], tile_at(x, it * TILES + i), ln.moments[:, i, 0:1],
                                          ln.rstd[:, i:i + 1], ALU.subtract, ALU.mult).then_inc(normed, 1)
                    for c in range(chunks):
                        dve.wait_ge(projected, it * 6 + (3 + c))
                        dve.tensor_copy(k_t[:, c * BANK:(c + 1) * BANK], bank[:, 4 + c, :]).then_inc(qkv_copied, 1)
                    dve.wait_ge(projected, it * 6 + 6)
                    dve.tensor_copy(v[:, 4:8, :].rearrange("p i d -> p (i d)"), bank[:, 7, :]).then_inc(qkv_copied, 1)

                    def row_max(qt):
                        s = 2 * (qt % 2)
                        dve.wait_ge(scored, it * TILES + (qt + 1))
                        diag = bank[:, s + qt // 4, (qt % 4) * P:(qt % 4 + 1) * P]
                        dve.tensor_tensor(diag, diag, above[:], ALU.add).then_inc(masked, 1)
                        dve.wait_ge(masked, it * TILES + (qt + 1))
                        row = bank[:, s:s + 2, :].rearrange("p b n -> p (b n)")[:, 0:(qt + 1) * P]
                        dve.tensor_reduce(top[:, qt:qt + 1], row, AX, ALU.max).then_inc(maxed, 1)
                        dve.wait_ge(maxed, it * TILES + (qt + 1))
                        dve.tensor_scalar(shift[:, qt:qt + 1], top[:, qt:qt + 1], -scale, None,
                                          ALU.mult).then_inc(shifted, 1)

                    def copy_blocks(qt):
                        for n, (q, g) in enumerate(groups):
                            if q == qt:
                                w = min(4, qt + 1 - 4 * g)
                                dve.wait_ge(p_turned, it * NG + (n + 1))
                                dve.tensor_copy(p_t[:, qt % 2, g * BANK:g * BANK + w * P],
                                                bank[:, 4 + n % 2, 0:w * P]).then_inc(pt_copied, 1)

                    def finish(qt):
                        dve.wait_ge(probs, it * TILES + (qt + 1))
                        dve.reciprocal(inverse[:, qt:qt + 1], total[:, qt:qt + 1]).then_inc(inverted, 1)
                        dve.wait_ge(inverted, it * TILES + (qt + 1))
                        dve.wait_ge(mixed, it * TILES + (qt + 1))
                        row = tile_at(x, it * TILES + qt)
                        dve.scalar_tensor_tensor(row, bank[:, 6 + qt % 2, 0:D], inverse[:, qt:qt + 1], row,
                                                 ALU.mult, ALU.add).then_inc(added, 1)

                    row_max(0)
                    for qt in range(TILES):
                        if qt + 1 < TILES:
                            row_max(qt + 1)
                        copy_blocks(qt)
                        if qt:
                            finish(qt - 1)
                    finish(TILES - 1)

            @block.scalar
            def _(act):
                with act.Fori(0, B) as it:
                    for c in range(chunks):
                        act.wait_ge(turned, it * chunks + (c + 1))
                        act.activation(h_t[:, c * BANK:(c + 1) * BANK], bank[:, c, :], ACT.Copy).then_inc(ht_copied, 1)
                    for c in range(chunks):
                        act.wait_ge(projected, it * 6 + (1 + c))
                        act.activation(q_t[:, c * BANK:(c + 1) * BANK], bank[:, 2 + c, :],
                                       ACT.Copy).then_inc(qkv_copied, 1)
                    act.wait_ge(projected, it * 6 + 5)
                    act.activation(v[:, 0:4, :].rearrange("p i d -> p (i d)"), bank[:, 6, :],
                                   ACT.Copy).then_inc(qkv_copied, 1)
                    for qt in range(TILES):
                        s = 2 * (qt % 2)
                        act.wait_ge(shifted, it * TILES + (qt + 1))
                        if qt >= 2:
                            act.wait_ge(p_turned, it * NG + (1 + max(n for n, (q, _) in enumerate(groups)
                                                                     if q == qt - 2)))
                        row = bank[:, s:s + 2, :].rearrange("p b n -> p (b n)")[:, 0:(qt + 1) * P]
                        act.activation(p[:, qt % 2, 0:(qt + 1) * P], row, ACT.Exp, bias=shift[:, qt:qt + 1],
                                       scale=scale, accum_out=total[:, qt:qt + 1]).then_inc(probs, 1)

            @block.tensor
            def _(pe):
                pe.wait_ge(w_in, 48)
                with pe.Fori(0, B) as it:
                    for c in range(chunks):
                        pe.wait_ge(normed, it * TILES + 4 * (c + 1))
                        for i in range(4):
                            last = pe.transpose(bank[:, c, i * P:(i + 1) * P], h[:, 4 * c + i, :], core.ident[:])
                        last.then_inc(turned, 1)
                    pe.wait_ge(ht_copied, it * chunks + chunks)
                    for n, w in enumerate((wq, wk)):
                        for c in range(chunks):
                            pe.matmul(bank[:, 2 + 2 * n + c, :], w[:], h_t[:, c * BANK:(c + 1) * BANK],
                                      start=True, stop=True).then_inc(projected, 1)
                    pe.wait_ge(added, it * TILES)
                    for c in range(2):
                        for i in range(4):
                            t = 4 * c + i
                            last = pe.matmul(bank[:, 6 + c, i * P:(i + 1) * P], h_t[:, t * P:(t + 1) * P], wv[:],
                                             start=True, stop=True)
                        last.then_inc(projected, 1)
                    pe.wait_ge(qkv_copied, (it + 1) * 6)

                    def scores(qt):
                        s = 2 * (qt % 2)
                        if qt >= 2:
                            pe.wait_ge(probs, it * TILES + (qt - 1))
                        for lo in range(0, (qt + 1) * P, BANK):
                            n = min(BANK, (qt + 1) * P - lo)
                            last = pe.matmul(bank[:, s + lo // BANK, 0:n], q_t[:, qt * P:(qt + 1) * P],
                                             k_t[:, lo:lo + n], start=True, stop=True)
                        last.then_inc(scored, 1)

                    scores(0)
                    for qt in range(TILES):
                        if qt + 1 < TILES:
                            scores(qt + 1)
                        pe.wait_ge(probs, it * TILES + (qt + 1))
                        for n, (q, g) in enumerate(groups):
                            if q != qt:
                                continue
                            if n >= 2:
                                pe.wait_ge(pt_copied, it * NG + (n - 1))
                            for kt in range(4 * g, min(4 * g + 4, qt + 1)):
                                last = pe.transpose(bank[:, 4 + n % 2, (kt - 4 * g) * P:(kt - 4 * g + 1) * P],
                                                    p[:, qt % 2, kt * P:(kt + 1) * P], core.ident[:])
                            last.then_inc(p_turned, 1)
                        if qt >= 2:
                            pe.wait_ge(added, it * TILES + (qt - 1))
                        for kt in range(qt + 1):
                            if kt % 4 == 0:
                                n = groups.index((qt, kt // 4))
                                pe.wait_ge(pt_copied, it * NG + (n + 1))
                            last = pe.matmul(bank[:, 6 + qt % 2, 0:D], p_t[:, qt % 2, kt * P:(kt + 1) * P],
                                             v[:, kt, :], start=(kt == 0), stop=(kt == qt))
                        last.then_inc(mixed, 1)


class Heads:

    GROUP = 4

    def __init__(self, core, ctx, name, heads):
        nc = core.nc
        self.core, self.name, self.heads = core, name, heads
        self.width = D // heads
        self.groups = heads // self.GROUP
        self.total = B * self.groups
        self.pairs = [3, 3, 3] if 9 * self.width + 2 <= P else [3, 2, 1]
        self.rows = sum(self.pairs) * self.width
        self.gw = self.GROUP * self.width
        shape = [self.total, self.GROUP, 3, self.width, T]
        self.q_parts = nc.dram_tensor(f"{name}_q_parts", shape, BF16, kind="Internal").ap()
        self.k_parts = nc.dram_tensor(f"{name}_k_parts", shape, BF16, kind="Internal").ap()
        core.stage = name
        self.values = core.sbuf(ctx, "values", [P, self.total, TILES, self.GROUP * 32])
        self.mixed = core.sbuf(ctx, "mixed", [P, self.total, TILES, self.gw])


def experts(masked, lo, hi):
    if not masked:
        return [(lo, hi, D)]
    return [(2 * e, 2 * e + 2, D >> e) for e in range(lo // 2, hi // 2)]


def project_stage(core, hd, w, masked):
    nc, x, bank = core.nc, core.x, core.bank
    core.stage = hd.name + "_p"
    s_ = core.sem
    w_in, v_set = s_("w_in"), s_("v_set")
    normed, residual = s_("normed"), s_("residual")
    turned, ht_copied, projected, qk_copied, v_copied = (
        s_("turned"), s_("ht_copied"), s_("projected"), s_("qk_copied"), s_("v_copied"))
    cut, parts_out = s_("cut"), s_("parts_out")
    chunks = T // BANK
    NW = len(w) - 1
    with ExitStack() as ctx:
        sb = lambda name, shape, dtype=F32: core.sbuf(ctx, name, shape, dtype)
        ln = LayerNorm(core, ctx)
        wq, wk, wv = sb("wq", [P, D]), sb("wk", [P, D]), sb("wv", [P, D])
        out_bias = sb("out_bias", [P, D])
        if masked:
            q_bias, k_bias, norm_w, norm_b = (sb(n, [P, 1]) for n in ("q_bias", "k_bias", "norm_w", "norm_b"))
            v_bias = sb("v_bias", [P, D])
            second, both = sb("second", [P, TILES]), sb("both", [P, TILES])
            small = s_("small")
            first = sb("first", [P, TILES, D])
        h = sb("h", [P, TILES, D])
        h_t = sb("h_t", [P, T])
        q_t, k_t = sb("q_t", [P, T]), sb("k_t", [P, T])
        rest = sb("rest", [P, 2, T])
        parts = [sb("q_cut", [P, 3, T], BF16), sb("k_cut", [P, 3, T], BF16)]
        with nc.Block() as block:

            @block.sync
            def _(sp):
                for tile, source in ((wq, w["q"]), (wk, w["k"]), (wv, w["v"])):
                    sp.dma_start(tile[:], source).then_inc(w_in, 16)
                sp.dma_start(out_bias[:], w["out_bias"].partition_broadcast(P)).then_inc(w_in, 16)
                if masked:
                    sp.dma_start(v_bias[:], w["v_bias"].partition_broadcast(P)).then_inc(w_in, 16)
                    for tile, source in ((q_bias, "q_bias"), (k_bias, "k_bias"), (norm_w, "norm_w"),
                                         (norm_b, "norm_b")):
                        sp.dma_start(tile[:], w[source].rearrange("(d o) -> d o", o=1)).then_inc(w_in, 16)
                with sp.Fori(0, B) as it:
                    for n, dram in enumerate((hd.q_parts, hd.k_parts)):
                        sp.wait_ge(cut, it * 8 + 4 * (n + 1))
                        for part in range(3):
                            dst = dram[bass.ds(it * hd.groups, hd.groups), :, part].rearrange("g j e t -> (g j) e t")
                            sp.dma_start(dst, parts[n][:, part, :]).then_inc(parts_out, 16)
                sp.wait_ge(parts_out, 16 * 6 * B)

            @block.gpsimd
            def _(pool):
                values = hd.values[:].rearrange("p n i c -> p (n i) c")
                pool.memset(values, 0.0).then_inc(v_set, 1)
                pool.wait_ge(v_set, 1)
                ones = hd.values[:].rearrange("p n i (j r) -> p (n i j) r", r=32)[:, :, hd.width:hd.width + 1]
                pool.memset(ones, 1.0).then_inc(v_set, 1)
                pool.wait_ge(w_in, 16 * NW)
                with pool.Fori(0, B) as it:
                    ln.rstd_of(pool, it)
                    if masked:
                        base = it * 5
                        pool.wait_ge(ln.scaled, it + 1)
                        pool.tensor_tensor(second[:], ln.rstd[:], ln.rstd[:], ALU.mult).then_inc(small, 1)
                        pool.wait_ge(small, base + 1)
                        pool.tensor_tensor(second[:], second[:], ln.moments[:, :, 1], ALU.mult).then_inc(small, 1)
                        wait_apart(core, pool, small, base + 2)
                        pool.tensor_scalar(second[:], second[:], LN_EPS, None, ALU.add).then_inc(small, 1)
                        pool.wait_ge(small, base + 3)
                        pool.tensor_tensor(second[:], second[:], core.minus_half[:, 0:TILES], ALU.pow).then_inc(small, 1)
                        pool.wait_ge(small, base + 4)
                        pool.tensor_tensor(both[:], second[:], ln.rstd[:], ALU.mult).then_inc(small, 1)
                    pool.wait_ge(normed, (it + 1) * TILES * (2 if masked else 1))
                    for i in range(TILES):
                        row = tile_at(x, it * TILES + i)
                        if masked:
                            pool.tensor_tensor(row, row, first[:, i, :], ALU.add).then_inc(residual, 1)
                    if masked:
                        wait_apart(core, pool, residual, it * 2 * TILES + TILES)
                    for i in range(TILES):
                        m = experts(masked, 0, TILES)[i // 2][2] if masked else D
                        row = tile_at(x, it * TILES + i)[:, 0:m]
                        pool.tensor_tensor(row, row, out_bias[:, 0:m], ALU.add).then_inc(residual, 1)
                pool.wait_ge(residual, B * TILES * (2 if masked else 1))

            @block.vector
            def _(dve):
                with dve.Fori(0, B) as it:
                    ln.moments_of(dve, it)
                    if masked:
                        dve.wait_ge(small, (it + 1) * 5)
                        dve.wait_ge(residual, it * 2 * TILES)
                    else:
                        dve.wait_ge(ln.scaled, it + 1)
                    dve.wait_ge(turned, it * chunks)
                    rstd = both if masked else ln.rstd
                    for i in range(TILES):
                        dve.tensor_scalar(h[:, i, :], tile_at(x, it * TILES + i), ln.moments[:, i, 0:1],
                                          rstd[:, i:i + 1], ALU.subtract, ALU.mult).then_inc(normed, 1)
                    if masked:
                        for i in range(TILES):
                            dve.tensor_scalar(first[:, i, :], tile_at(x, it * TILES + i), ln.moments[:, i, 0:1],
                                              ln.rstd[:, i:i + 1], ALU.subtract, ALU.mult).then_inc(normed, 1)
                        dve.wait_ge(w_in, 16 * NW)
                    dve.wait_ge(v_set, 2)
                    for c in range(2):
                        dve.wait_ge(projected, it * 6 + (5 + c))
                        for g in range(hd.groups):
                            dst = hd.values[:, bass.ds(it * hd.groups + g, 1), 4 * c:4 * c + 4, :].rearrange(
                                "p o i (j r) -> p (o i) j r", r=32)[:, :, :, 0:hd.width]
                            src = bank[:, 6 + c, :].rearrange("p (i g j e) -> p g i j e", g=hd.groups, j=hd.GROUP,
                                                              e=hd.width)[:, g]
                            if masked:
                                vb = v_bias[:, g * hd.gw:(g + 1) * hd.gw].rearrange("p (j e) -> p j e", e=hd.width)
                                vb = vb.unsqueeze(1).broadcast_to([P, 4, hd.GROUP, hd.width])
                                dve.tensor_tensor(dst, src, vb, ALU.add).then_inc(v_copied, 1)
                            else:
                                dve.tensor_copy(dst, src).then_inc(v_copied, 1)
                    for n, whole in enumerate((q_t, k_t)):
                        dve.wait_ge(qk_copied, it * 4 + 2 * (n + 1))
                        dve.wait_ge(parts_out, it * 96 + 0)
                        dve.tensor_copy(parts[n][:, 0, :], whole[:]).then_inc(cut, 1)
                        dve.wait_ge(cut, it * 8 + 4 * n + 1)
                        dve.tensor_tensor(rest[:, n, :], whole[:], parts[n][:, 0, :], ALU.subtract).then_inc(cut, 1)
                        dve.wait_ge(cut, it * 8 + 4 * n + 2)
                        dve.tensor_copy(parts[n][:, 1, :], rest[:, n, :]).then_inc(cut, 1)
                        dve.wait_ge(cut, it * 8 + 4 * n + 3)
                        dve.tensor_tensor(parts[n][:, 2, :], rest[:, n, :], parts[n][:, 1, :],
                                          ALU.subtract).then_inc(cut, 1)

            @block.scalar
            def _(act):
                act.wait_ge(w_in, 16 * NW)
                with act.Fori(0, B) as it:
                    act.wait_ge(projected, it * 6)
                    for c in range(chunks):
                        act.wait_ge(turned, it * chunks + (c + 1))
                        dst = h_t[:, c * BANK:(c + 1) * BANK]
                        if masked:
                            act.activation(dst, bank[:, c, :], ACT.Identity, bias=norm_b[:],
                                           scale=norm_w[:]).then_inc(ht_copied, 1)
                        else:
                            act.activation(dst, bank[:, c, :], ACT.Copy).then_inc(ht_copied, 1)
                    act.wait_ge(cut, it * 8)
                    for n, whole in enumerate((q_t, k_t)):
                        for c in range(chunks):
                            act.wait_ge(projected, it * 6 + (2 * n + c + 1))
                            dst = whole[:, c * BANK:(c + 1) * BANK]
                            if masked:
                                act.activation(dst, bank[:, 2 + 2 * n + c, :], ACT.Identity,
                                               bias=(q_bias, k_bias)[n][:]).then_inc(qk_copied, 1)
                            else:
                                act.activation(dst, bank[:, 2 + 2 * n + c, :], ACT.Copy).then_inc(qk_copied, 1)

            @block.tensor
            def _(pe):
                pe.wait_ge(w_in, 16 * NW)
                with pe.Fori(0, B) as it:
                    for c in range(chunks):
                        if masked:
                            pe.wait_ge(normed, it * 2 * TILES + 4 * (c + 1))
                        else:
                            pe.wait_ge(normed, it * TILES + 4 * (c + 1))
                        for i in range(4):
                            last = pe.transpose(bank[:, c, i * P:(i + 1) * P], h[:, 4 * c + i, :], core.ident[:])
                        last.then_inc(turned, 1)
                    pe.wait_ge(ht_copied, it * chunks + chunks)
                    pe.wait_ge(qk_copied, it * 4)
                    for n, weight in enumerate((wq, wk)):
                        for c in range(chunks):
                            for lo, hi, m in experts(masked, 4 * c, 4 * c + 4):
                                last = pe.matmul(bank[:, 2 + 2 * n + c, (lo - 4 * c) * P:(hi - 4 * c) * P],
                                                 weight[0:m, :], h_t[0:m, lo * P:hi * P], start=True, stop=True)
                            last.then_inc(projected, 1)
                    pe.wait_ge(v_copied, it * 2 * hd.groups)
                    for c in range(2):
                        for lo, hi, m in experts(masked, 4 * c, 4 * c + 4):
                            for t in range(lo, hi):
                                last = pe.matmul(bank[:, 6 + c, (t - 4 * c) * P:(t - 4 * c + 1) * P],
                                                 h_t[0:m, t * P:(t + 1) * P], wv[0:m, :], start=True, stop=True)
                        last.then_inc(projected, 1)


def attend_stage(core, hd):
    nc, bank = core.nc, core.bank
    core.stage = hd.name + "_a"
    s_ = core.sem
    G, R, W, T2 = hd.GROUP, hd.rows, hd.width, T // 2
    scale = float(D) ** -0.5
    LOADS = 3 + sum(hd.pairs)
    qk_in = [s_("qk_in0"), s_("qk_in1")]
    v_in = [s_("v_in0"), s_("v_in1")]
    ones_set, scored, maxed, top_made, high_made, shifts_made = (
        s_("ones_set"), s_("scored"), s_("maxed"), s_("top_made"), s_("high_made"), s_("shifts_made"))
    shift_turned, shift_copied, shift_in = s_("shift_turned"), s_("shift_copied"), s_("shift_in")
    shifted, probs, mixed, mix_copied, mix_turned, inverted, written = (
        s_("shifted"), s_("probs"), s_("mixed"), s_("mix_copied"), s_("mix_turned"), s_("inverted"), s_("written"))
    RING, ITEMS = 3, 32
    ST, SC, MIX, MISC = 0, 3, 6, 7

    def wait_for_bank(engine, done, u, n):
        last = n - RING if n >= RING else max(range(n, ITEMS, RING)) - ITEMS
        wait_past(engine, done, u * ITEMS + (last + 1))

    with ExitStack() as ctx:
        sb = lambda name, shape, dtype=F32: core.sbuf(ctx, name, shape, dtype)
        q_stack, k_stack = sb("q_stack", [R + 2, 2, G, T], BF16), sb("k_stack", [R + 2, 2, G, T], BF16)
        v = sb("v", [P, 2, TILES, G * 32])
        p = sb("p", [P, 2, G, T2])
        halves = sb("halves", [P, 16, 2])
        top = sb("top", [P, 4, G])
        shift = sb("shift", [P, 4, 2, G], BF16)
        shift_rows = sb("shift_rows", [8, 2, T2], BF16)
        mix = sb("mix", [P, T2])
        inverse = sb("inverse", [P, 4, G])

        with nc.Block() as block:

            @block.sync
            def _(sp):
                def load(n, k):
                    at = 0
                    for a, count in enumerate(hd.pairs):
                        rows = slice(at, at + count * W)
                        src = hd.k_parts[bass.ds(n, 1), :, 0:count].rearrange("o j c e t -> (c e) (o j) t")
                        sp.dma_start(k_stack[rows, k], src).then_inc(qk_in[k], 16)
                        src = hd.q_parts[bass.ds(n, 1), :, a].rearrange("o j e t -> e (o j) t")
                        for c in range(count):
                            sp.dma_start(q_stack[at + c * W:at + (c + 1) * W, k], src).then_inc(qk_in[k], 16)
                        at += count * W
                    sp.dma_start(v[:, k], hd.values[:, bass.ds(n, 1)].rearrange("p o i c -> p (o i) c")).then_inc(
                        v_in[k], 16)

                def shift_load(u, ui):
                    k, qc = ui % 4 // 2, ui % 2
                    sp.wait_ge(shift_copied, u + 1)
                    for part in range(2):
                        sp.dma_start(q_stack[R + part:R + part + 1, k, :, qc * T2:(qc + 1) * T2],
                                     shift_rows[part * G:(part + 1) * G, qc, :]).then_inc(shift_in, 16)

                sp.wait_ge(ones_set, 1)
                load(0, 0)
                load(1, 1)
                shift_load(0, 0)

                def turn(it, first, last):
                    for ui in range(4):
                        u, k = it * 4 + ui, ui // 2
                        if ui % 2 == 0 and not (first and k == 0) and not (last and k == 1):
                            sp.wait_ge(mixed, u * TILES)
                            load(it * 2 + k + 1, (k + 1) % 2)
                        if not (last and ui == 3):
                            shift_load(u + 1, ui + 1)

                turns(sp, hd.total // 2, turn)

            @block.vector
            def _(dve):
                dve.memset(k_stack[R // 32 * 32:R + 2, :, :, :].rearrange("r k j t -> r (k j t)"), 1.0).then_inc(ones_set, 1)

                def maximum(u, n):
                    dve.wait_ge(scored, u * ITEMS + (n + 1))
                    dve.tensor_reduce(halves[:, n // 2, n % 2:n % 2 + 1], bank[:, SC + n % RING, :], AX,
                                      ALU.max).then_inc(maxed, 1)

                def shifts(u):
                    dve.wait_ge(maxed, (u + 1) * ITEMS)
                    dve.wait_ge(shift_turned, u)
                    dve.tensor_tensor(top[:].rearrange("p i j -> p j i"),
                                      halves[:, :, 0].rearrange("p (j i) -> p j i", j=G),
                                      halves[:, :, 1].rearrange("p (j i) -> p j i", j=G), ALU.max).then_inc(top_made, 1)
                    dve.wait_ge(top_made, u + 1)
                    dve.tensor_scalar(shift[:, :, 0, :], top[:], -1.0, None, ALU.mult).then_inc(high_made, 1)
                    dve.wait_ge(high_made, u + 1)
                    dve.scalar_tensor_tensor(shift[:, :, 1, :], top[:], -1.0, shift[:, :, 0, :], ALU.mult,
                                             ALU.subtract).then_inc(shifts_made, 1)

                def write_mixed(u, ui, it):
                    rows = bank[:, MISC, :].rearrange("p (i j r) -> p i j r", i=4, j=G)
                    dve.wait_ge(mix_turned, u + 1)
                    dve.reciprocal(inverse[:], rows[:, :, :, W]).then_inc(inverted, 1)
                    dve.wait_ge(inverted, u + 1)
                    dst = hd.mixed[:, bass.ds(it * 2 + ui // 2, 1), ui % 2 * 4:ui % 2 * 4 + 4, :].rearrange(
                        "p o i (j e) -> p (o i) j e", e=W)
                    dve.tensor_tensor(dst, rows[:, :, :, 0:W], inverse[:].unsqueeze(3).broadcast_to([P, 4, G, W]),
                                      ALU.mult).then_inc(written, 1)

                for n in range(ITEMS):
                    maximum(0, n)
                shifts(0)
                for n in range(ITEMS // 2):
                    maximum(1, n)

                def turn(it, first, last):
                    for ui in range(4):
                        u = it * 4 + ui
                        for kt in range(TILES):
                            for n in range(4 * kt, 4 * kt + 4):
                                if kt < 4 and not (last and ui == 3):
                                    maximum(u + 1, n + ITEMS // 2)
                                if kt >= 4 and not (last and ui >= 2):
                                    maximum(u + 2, n - ITEMS // 2)
                            if kt == 3 and not (last and ui == 3):
                                shifts(u + 1)
                            if kt == 2 and not (first and ui == 0):
                                write_mixed(u - 1, (ui - 1) % 4, it if ui else it - 1)

                turns(dve, hd.total // 2, turn)
                write_mixed(2 * hd.total - 1, 3, hd.total // 2 - 1)

            @block.scalar
            def _(act):
                def exponential(u, kt, j):
                    n = 4 * kt + j
                    act.wait_ge(shifted, u * ITEMS + (n + 1))
                    if j == 0:
                        wait_past(act, mixed, u * TILES + (kt - 1))
                    act.activation(p[:, kt % 2, j, :], bank[:, ST + n % RING, :], ACT.Exp,
                                   scale=scale).then_inc(probs, 1)

                def copy_shifts(u, ui):
                    act.wait_ge(shift_turned, u + 1)
                    if not (isinstance(u, int) and u < 2):
                        act.wait_ge(shift_in, (u - 1) * 32)
                    act.activation(shift_rows[:, ui % 2, :], bank[0:8, MISC, :], ACT.Copy).then_inc(shift_copied, 1)

                def copy_mix(u):
                    act.wait_ge(mixed, (u + 1) * TILES)
                    if not (isinstance(u, int) and u < 1):
                        act.wait_ge(mix_turned, u)
                    act.activation(mix[:], bank[:, MIX, :], ACT.Copy).then_inc(mix_copied, 1)

                copy_shifts(0, 0)

                def turn(it, first, last):
                    for ui in range(4):
                        u = it * 4 + ui
                        for kt in range(TILES):
                            for j in range(G):
                                exponential(u, kt, j)
                                if kt == 0 and j == 1 and not (first and ui == 0):
                                    copy_mix(u - 1)
                                if kt == 5 and j == 1 and not (last and ui == 3):
                                    copy_shifts(u + 1, ui + 1)

                turns(act, hd.total // 2, turn)
                copy_mix(2 * hd.total - 1)

            @block.tensor
            def _(pe):
                def scores(u, n, k, qc):
                    j, i, half = n // 8, n // 2 % 4, n % 2
                    at = qc * T2 + i * P
                    wait_for_bank(pe, maxed, u, n)
                    pe.matmul(bank[:, SC + n % RING, :], q_stack[0:R, k, j, at:at + P],
                              k_stack[0:R, k, j, half * BANK:(half + 1) * BANK],
                              start=True, stop=True).then_inc(scored, 1)

                def turn_shifts(u):
                    pe.wait_ge(shifts_made, u + 1)
                    if not (isinstance(u, int) and u < 2):
                        pe.wait_ge(written, u - 1)
                    for i in range(4):
                        last = pe.matmul(bank[0:8, MISC, i * P:(i + 1) * P], shift[:, i].rearrange("p s j -> p (s j)"),
                                         core.ident_bf[:], start=True, stop=True)
                    last.then_inc(shift_turned, 1)

                def shifted_scores(u, kt, k, qc, j):
                    n = 4 * kt + j
                    wait_for_bank(pe, probs, u, n)
                    pe.matmul(bank[:, ST + n % RING, :], k_stack[:, k, j, kt * P:(kt + 1) * P],
                              q_stack[:, k, j, qc * T2:(qc + 1) * T2], start=True, stop=True).then_inc(shifted, 1)

                def mix_values(s, kt, k):
                    pe.wait_ge(probs, s * G + G)
                    for j in range(G):
                        last = pe.matmul(bank[32 * j:32 * j + 32, MIX, :], v[:, k, kt, 32 * j:32 * j + 32],
                                         p[:, kt % 2, j, :], start=(kt == 0), stop=(kt == TILES - 1))
                    last.then_inc(mixed, 1)

                def turn_mix(u):
                    pe.wait_ge(mix_copied, u + 1)
                    pe.wait_ge(shift_copied, u + 2)
                    for i in range(4):
                        last = pe.transpose(bank[:, MISC, i * P:(i + 1) * P], mix[:, i * P:(i + 1) * P], core.ident[:])
                    last.then_inc(mix_turned, 1)

                pe.wait_ge(qk_in[0], 16 * LOADS)
                for n in range(ITEMS):
                    scores(0, n, 0, 0)
                turn_shifts(0)
                for n in range(ITEMS // 2):
                    scores(1, n, 0, 1)
                pe.wait_ge(shift_in, 32)
                for j in range(RING):
                    shifted_scores(0, 0, 0, 0, j)

                def turn(it, first, last):
                    for ui in range(4):
                        u, k, qc = it * 4 + ui, ui // 2, ui % 2
                        for kt in range(TILES):
                            s = u * TILES + kt
                            end = last and ui == 3
                            if kt == 4 and qc == 0 and not (last and k == 1):
                                pe.wait_ge(qk_in[(k + 1) % 2], (it + (1 + k)) * 16 * LOADS)
                            for j in range(G):
                                n = 4 * kt + j + RING
                                if n < ITEMS:
                                    shifted_scores(u, n // 4, k, qc, n % 4)
                                elif not end:
                                    if n == ITEMS:
                                        pe.wait_ge(shift_in, (u + 2) * 32)
                                    shifted_scores(u + 1, 0, (ui + 1) % 4 // 2, (ui + 1) % 2, n - ITEMS)
                                if kt < 4 and not end:
                                    scores(u + 1, 4 * kt + j + ITEMS // 2, (ui + 1) % 4 // 2, (ui + 1) % 2)
                                if kt >= 4 and not (last and ui >= 2):
                                    scores(u + 2, 4 * kt + j - ITEMS // 2, (ui + 2) % 4 // 2, (ui + 2) % 2)
                            if kt == 0:
                                if qc == 0:
                                    pe.wait_ge(v_in[k], (it + 1) * 16)
                                if not (first and ui == 0):
                                    pe.wait_ge(mix_copied, u)
                            mix_values(s, kt, k)
                            if kt == 1 and not (first and ui == 0):
                                turn_mix(u - 1)
                            if kt == 4 and not end:
                                turn_shifts(u + 1)

                turns(pe, hd.total // 2, turn)
                pe.wait_ge(mix_copied, 2 * hd.total)
                pe.wait_ge(written, 2 * hd.total - 1)
                for i in range(4):
                    last = pe.transpose(bank[:, MISC, i * P:(i + 1) * P], mix[:, i * P:(i + 1) * P], core.ident[:])
                last.then_inc(mix_turned, 1)


def turns(engine, count, turn):
    turn(0, True, False)
    with engine.Fori(1, count - 1) as it:
        turn(it, False, False)
    turn(count - 1, False, True)


def output_stage(core, hd, wo_t, masked):
    nc, x, bank = core.nc, core.x, core.bank
    core.stage = hd.name + "_o"
    s_ = core.sem
    w_in, staged, turned, copied, projected, added = (
        s_("w_in"), s_("staged"), s_("turned"), s_("copied"), s_("projected"), s_("added"))
    with ExitStack() as ctx:
        sb = lambda name, shape, dtype=F32: core.sbuf(ctx, name, shape, dtype)
        wo = sb("wo", [P, D])
        m_, m_t = sb("m", [P, TILES, D]), sb("m_t", [P, T])
        with nc.Block() as block:

            @block.sync
            def _(sp):
                sp.dma_start(wo[:], wo_t).then_inc(w_in, 16)

            @block.vector
            def _(dve):
                with dve.Fori(0, B) as it:
                    dve.wait_ge(turned, it * 2)
                    for g in range(hd.groups):
                        src = hd.mixed[:, bass.ds(it * hd.groups + g, 1)].rearrange("p o i c -> p (o i) c")
                        dve.tensor_copy(m_[:, :, g * hd.gw:(g + 1) * hd.gw], src).then_inc(staged, 1)
                    for c in range(2):
                        dve.wait_ge(projected, it * 2 + (c + 1))
                        for lo, hi, m in experts(masked, 4 * c, 4 * c + 4):
                            row = x[:, bass.ds(it * TILES + lo, hi - lo), 0:m]
                            src = bank[:, 4 + c, (lo - 4 * c) * P:(hi - 4 * c) * P].rearrange(
                                "p (i d) -> p i d", d=D)[:, :, 0:m]
                            dve.tensor_tensor(row, row, src, ALU.add).then_inc(added, 1)

            @block.scalar
            def _(act):
                with act.Fori(0, B) as it:
                    for c in range(2):
                        act.wait_ge(turned, it * 2 + (c + 1))
                        act.wait_ge(projected, it * 2)
                        act.activation(m_t[:, c * BANK:(c + 1) * BANK], bank[:, c, :], ACT.Copy).then_inc(copied, 1)

            @block.tensor
            def _(pe):
                pe.wait_ge(w_in, 16)
                with pe.Fori(0, B) as it:
                    pe.wait_ge(staged, (it + 1) * hd.groups)
                    pe.wait_ge(added, it * len(experts(masked, 0, TILES)) * (1 if masked else 2))
                    for c in range(2):
                        for i in range(4):
                            last = pe.transpose(bank[:, c, i * P:(i + 1) * P], m_[:, 4 * c + i, :], core.ident[:])
                        last.then_inc(turned, 1)
                    for c in range(2):
                        pe.wait_ge(copied, it * 2 + (c + 1))
                        for lo, hi, m in experts(masked, 4 * c, 4 * c + 4):
                            for t in range(lo, hi):
                                last = pe.matmul(bank[:, 4 + c, (t - 4 * c) * P:(t - 4 * c) * P + m],
                                                 m_t[0:m, t * P:(t + 1) * P], wo[0:m, 0:m], start=True, stop=True)
                        last.then_inc(projected, 1)


def heads_layer(core, name, heads, w, masked):
    with ExitStack() as ctx:
        hd = Heads(core, ctx, name, heads)
        project_stage(core, hd, w, masked)
        attend_stage(core, hd)
        output_stage(core, hd, w["o"], masked)



class Front:

    def __init__(self, core, ctx, second_eps=None, spare=0):
        self.core, self.second_eps = core, second_eps
        self.ln = LayerNorm(core, ctx)
        self.h = core.sbuf(ctx, "h", [P, TILES, D + spare])
        self.h_t = core.sbuf(ctx, "h_t", [P, T])
        self.normed, self.turned, self.copied = core.sem("normed"), core.sem("turned"), core.sem("ht_copied")
        if second_eps is not None:
            self.second, self.both = core.sbuf(ctx, "second", [P, TILES]), core.sbuf(ctx, "both", [P, TILES])
            self.small = core.sem("small")

    def on_vector(self, dve, it):
        ln = self.ln
        ln.moments_of(dve, it)
        if self.second_eps is None:
            dve.wait_ge(ln.scaled, it + 1)
            rstd = ln.rstd
        else:
            dve.wait_ge(self.small, (it + 1) * 5)
            rstd = self.both
        dve.wait_ge(self.turned, it * 2)
        for i in range(TILES):
            dve.tensor_scalar(self.h[:, i, 0:D], tile_at(self.core.x, it * TILES + i), ln.moments[:, i, 0:1],
                              rstd[:, i:i + 1], ALU.subtract, ALU.mult).then_inc(self.normed, 1)

    def on_gpsimd(self, pool, it):
        ln = self.ln
        ln.rstd_of(pool, it)
        if self.second_eps is None:
            return
        second, small, base = self.second, self.small, it * 5
        pool.wait_ge(ln.scaled, it + 1)
        pool.tensor_tensor(second[:], ln.rstd[:], ln.rstd[:], ALU.mult).then_inc(small, 1)
        pool.wait_ge(small, base + 1)
        pool.tensor_tensor(second[:], second[:], ln.moments[:, :, 1], ALU.mult).then_inc(small, 1)
        wait_apart(self.core, pool, small, base + 2)
        pool.tensor_scalar(second[:], second[:], self.second_eps, None, ALU.add).then_inc(small, 1)
        pool.wait_ge(small, base + 3)
        pool.tensor_tensor(second[:], second[:], self.core.minus_half[:, 0:TILES], ALU.pow).then_inc(small, 1)
        pool.wait_ge(small, base + 4)
        pool.wait_ge(self.normed, it * TILES)
        pool.tensor_tensor(self.both[:], second[:], ln.rstd[:], ALU.mult).then_inc(small, 1)

    def on_tensor(self, pe, it):
        for c in range(2):
            pe.wait_ge(self.normed, it * TILES + 4 * (c + 1))
            pe.wait_ge(self.copied, it * 2)
            for i in range(4):
                last = pe.transpose(self.core.bank[:, c, i * P:(i + 1) * P], self.h[:, 4 * c + i, 0:D],
                                    self.core.ident[:])
            last.then_inc(self.turned, 1)

    def on_scalar(self, act, it):
        for c in range(2):
            act.wait_ge(self.turned, it * 2 + (c + 1))
            act.activation(self.h_t[:, c * BANK:(c + 1) * BANK], self.core.bank[:, c, :],
                           ACT.Copy).then_inc(self.copied, 1)


def kernel_attention_stage(core, w):
    nc, x, bank = core.nc, core.x, core.bank
    core.stage = "lin"
    s_ = core.sem
    H, DH, F, HT = 16, 64, 32, 4
    w_in, filled, made = s_("w_in"), s_("filled"), s_("made")
    prepared, prep_copied = s_("prepared"), s_("prep_copied")
    featured, q_ready, biased, k_ready = s_("featured"), s_("q_ready"), s_("biased"), s_("k_ready")
    summed, sum_copied, blocks_made, headed, head_ready = (
        s_("summed"), s_("sum_copied"), s_("blocks_made"), s_("headed"), s_("head_ready"))
    divided, den_added, inverted, inv_turned, inv_copied, spread, q_scaled = (
        s_("divided"), s_("den_added"), s_("inverted"), s_("inv_turned"), s_("inv_copied"), s_("spread"), s_("q_scaled"))
    projected, added, residual = s_("projected"), s_("added"), s_("residual")
    with ExitStack() as ctx:
        sb = lambda name, shape, dtype=F32: core.sbuf(ctx, name, shape, dtype)
        front = Front(core, ctx, spare=1)
        wq, wk, wv, wo = (sb(n, [DH, H, D]) for n in ("wq", "wk", "wv", "wo"))
        fq, fk = sb("fq", [DH, F]), sb("fk", [DH, F])
        bq, bk, bv = sb("bq", [DH, H]), sb("bk", [DH, H]), sb("bv", [DH, H])
        out_bias = sb("out_bias", [P, D])
        wide_bias = sb("wide_bias", [DH, H, P])
        fold_q, fold_k, bias_k = sb("fold_q", [P, H * F]), sb("fold_k", [P, H * F]), sb("bias_k", [P, H * F])
        bias_q = sb("bias_q", [P, HT])
        fold_v, bias_v = sb("fold_v", [P, H, D]), sb("bias_v", [P, HT, D])
        ones = sb("ones", [P, 1])
        own = sb("own", [P, 4])
        spreads = sb("spreads", [P, P, F])
        q_f, k_f, k_raw = sb("q_f", [P, HT, T]), sb("k_f", [P, TILES, H * F]), sb("k_raw", [P, 2, H * F])
        sums, key_sums, blocks = sb("sums", [P, H * F]), sb("key_sums", [P, HT]), sb("blocks", [P, HT, 4])
        head = sb("head", [P, HT, D])
        den, inverse, inverse_t = sb("den", [P, P]), sb("inverse", [P, P]), sb("inverse_t", [P, P])
        with nc.Block() as block:

            @block.sync
            def _(sp):
                for tile, source in ((wq, "q"), (wk, "k"), (wv, "v"), (wo, "o")):
                    sp.dma_start(tile[:], w[source].rearrange("(h e) d -> e h d", e=DH)).then_inc(w_in, 16)
                for tile, source in ((fq, "fq"), (fk, "fk"), (bq, "bq"), (bk, "bk"), (bv, "bv")):
                    sp.dma_start(tile[:], w[source]).then_inc(w_in, 16)
                sp.dma_start(out_bias[:], w["out_bias"].partition_broadcast(P)).then_inc(w_in, 16)

            @block.gpsimd
            def _(pool):
                pool.memset(ones[:], 1.0).then_inc(filled, 1)
                pool.memset(front.h[:, :, D:D + 1], 1.0).then_inc(filled, 1)
                pool.memset(own[:], 1.0).then_inc(filled, 1)
                pool.wait_ge(filled, 3)
                pool.affine_select(out=own[:], in_=own[:], compare_op=ALU.is_ge, fill=0.0, base=0,
                                   pattern=[[-F, 4]], channel_multiplier=1).then_inc(filled, 1)
                pool.wait_ge(filled, 4)
                pool.affine_select(out=own[:], in_=own[:], compare_op=ALU.is_ge, fill=0.0, base=F - 1,
                                   pattern=[[F, 4]], channel_multiplier=-1).then_inc(filled, 1)
                pool.wait_ge(w_in, 160)
                with pool.Fori(0, B) as it:
                    front.on_gpsimd(pool, it)
                    pool.wait_ge(front.normed, (it + 1) * TILES)
                    for i in range(TILES):
                        row = tile_at(x, it * TILES + i)
                        pool.tensor_tensor(row, row, out_bias[:], ALU.add).then_inc(residual, 1)

            @block.vector
            def _(dve):
                dve.tensor_copy(spreads[:], core.ident[:].unsqueeze(2).broadcast_to([P, P, F])).then_inc(made, 1)
                dve.wait_ge(w_in, 160)
                dve.tensor_copy(wide_bias[:], bk[:].unsqueeze(2).broadcast_to([DH, H, P])).then_inc(made, 1)
                for n, (dst, b) in enumerate(((fold_q[:], 0), (fold_k[:], 1), (bias_k[:], 2), (bias_q[:], 3))):
                    dve.wait_ge(prepared, n + 1)
                    src = bank[:, b, 0:HT] if b == 3 else bank[:, b, :]
                    dve.tensor_copy(dst, src).then_inc(prep_copied, 1)
                dve.tensor_copy(wide_bias[:], bv[:].unsqueeze(2).broadcast_to([DH, H, P])).then_inc(made, 1)
                dve.wait_ge(prepared, 5)
                dve.tensor_copy(fold_v[:].rearrange("p h d -> p (h d)"),
                                bank[:, 4:8, :].rearrange("p b n -> p (b n)")).then_inc(prep_copied, 1)
                dve.wait_ge(prepared, 6)
                dve.tensor_copy(bias_v[:].rearrange("p h d -> p (h d)"), bank[:, 0, :]).then_inc(prep_copied, 1)
                with dve.Fori(0, B) as it:
                    dve.wait_ge(summed, it * 2)
                    front.on_vector(dve, it)
                    for i in range(TILES):
                        dve.wait_ge(featured, it * 16 + (8 + i + 1))
                        if i >= 2:
                            dve.wait_ge(k_ready, it * TILES + (i - 1))
                        dve.tensor_tensor(k_raw[:, i % 2, :], bank[:, 4 + i % 2, :], bias_k[:],
                                          ALU.add).then_inc(biased, 1)
                    dve.wait_ge(summed, it * 2 + 1)
                    dve.tensor_copy(sums[:], bank[:, 6, :]).then_inc(sum_copied, 1)
                    dve.wait_ge(summed, it * 2 + 2)
                    dve.tensor_copy(key_sums[:], bank[:, 7, 0:HT]).then_inc(sum_copied, 1)
                    dve.wait_ge(sum_copied, it * 2 + 2)
                    dve.tensor_tensor(blocks[:], key_sums[:].unsqueeze(2).broadcast_to([P, HT, 4]),
                                      own[:].unsqueeze(1).broadcast_to([P, HT, 4]), ALU.mult).then_inc(blocks_made, 1)
                    dve.wait_ge(headed, it + 1)
                    for t in range(HT):
                        dve.scalar_tensor_tensor(head[:, t, :], bias_v[:, t, :], key_sums[:, t:t + 1],
                                                 bank[:, 0, t * D:(t + 1) * D], ALU.mult,
                                                 ALU.add).then_inc(head_ready, 1)
                    dve.wait_ge(divided, it + 1)
                    dve.tensor_scalar(den[:], bank[:, 1, 0:P], 1e-6, None, ALU.add).then_inc(den_added, 1)
                    dve.wait_ge(den_added, it + 1)
                    dve.reciprocal(inverse[:], den[:]).then_inc(inverted, 1)
                    dve.wait_ge(inv_turned, it + 1)
                    dve.tensor_copy(inverse_t[:], bank[:, 1, P:2 * P]).then_inc(inv_copied, 1)
                    for t in range(HT):
                        for c in range(2):
                            n = 2 * t + c
                            dve.wait_ge(spread, it * 8 + (n + 1))
                            row = q_f[:, t, c * BANK:(c + 1) * BANK]
                            dve.tensor_tensor(row, row, bank[:, 2 + n % 4, :], ALU.mult).then_inc(q_scaled, 1)
                    dve.wait_ge(residual, (it + 1) * TILES)
                    for c in range(2):
                        dve.wait_ge(projected, it * 2 + (c + 1))
                        rows = x[:, bass.ds(it * TILES + 4 * c, 4), :].rearrange("p i d -> p (i d)")
                        dve.tensor_tensor(rows, rows, bank[:, 6 + c, :], ALU.add).then_inc(added, 1)

            @block.scalar
            def _(act):
                act.wait_ge(prep_copied, 6)
                with act.Fori(0, B) as it:
                    act.wait_ge(featured, it * 16)
                    front.on_scalar(act, it)
                    act.wait_ge(projected, it * 2)
                    for n in range(8):
                        t, c = n // 2, n % 2
                        act.wait_ge(featured, it * 16 + (n + 1))
                        act.activation(q_f[:, t, c * BANK:(c + 1) * BANK], bank[:, 2 + n % 2, :], ACT.Exp,
                                       bias=bias_q[:, t:t + 1]).then_inc(q_ready, 1)
                    for i in range(TILES):
                        act.wait_ge(biased, it * TILES + (i + 1))
                        act.activation(k_f[:, i, :], k_raw[:, i % 2, :], ACT.Exp).then_inc(k_ready, 1)

            @block.tensor
            def _(pe):
                pe.wait_ge(w_in, 160)
                for n, (weight, feat) in enumerate(((wq, fq), (wk, fk))):
                    for hd in range(H):
                        last = pe.matmul(bank[:, n, hd * F:(hd + 1) * F], weight[:, hd, :], feat[:], start=True, stop=True)
                    last.then_inc(prepared, 1)
                pe.wait_ge(made, 2)
                for hd in range(H):
                    last = pe.matmul(bank[:, 2, hd * F:(hd + 1) * F], wide_bias[:, hd, :], fk[:], start=True, stop=True)
                last.then_inc(prepared, 1)
                for j in range(4):
                    last = pe.matmul(bank[32 * j:32 * j + 32, 3, 0:HT], fq[:],
                                     bq[:].rearrange("e (t j) -> e j t", j=4)[:, j, :], start=True, stop=True)
                last.then_inc(prepared, 1)
                for hd in range(H):
                    last = pe.matmul(bank[:, 4 + hd // 4, hd % 4 * D:(hd % 4 + 1) * D], wv[:, hd, :], wo[:, hd, :],
                                     start=True, stop=True)
                last.then_inc(prepared, 1)
                pe.wait_ge(made, 3)
                pe.wait_ge(prep_copied, 1)
                for hd in range(H):
                    j, t = hd % 4, hd // 4
                    last = pe.matmul(bank[32 * j:32 * j + 32, 0, t * D:(t + 1) * D], wide_bias[:, hd, 0:32],
                                     wo[:, hd, :], start=True, stop=True)
                last.then_inc(prepared, 1)
                pe.wait_ge(prep_copied, 6)
                pe.wait_ge(filled, 5)
                with pe.Fori(0, B) as it:
                    pe.wait_ge(head_ready, it * HT)
                    pe.wait_ge(inv_copied, it)
                    pe.wait_ge(q_scaled, it * 8)
                    front.on_tensor(pe, it)
                    pe.wait_ge(front.copied, (it + 1) * 2)
                    for n in range(8):
                        t, c = n // 2, n % 2
                        if n >= 2:
                            pe.wait_ge(q_ready, it * 8 + (n - 1))
                        pe.matmul(bank[:, 2 + n % 2, :], fold_q[:, t * P:(t + 1) * P],
                                  front.h_t[:, c * BANK:(c + 1) * BANK], start=True, stop=True).then_inc(featured, 1)
                    for i in range(TILES):
                        if i >= 2:
                            pe.wait_ge(biased, it * TILES + (i - 1))
                        pe.matmul(bank[:, 4 + i % 2, :], front.h_t[:, i * P:(i + 1) * P], fold_k[:],
                                  start=True, stop=True).then_inc(featured, 1)
                    pe.wait_ge(added, it * 2)
                    for i in range(TILES):
                        pe.wait_ge(k_ready, it * TILES + (i + 1))
                        last = pe.matmul(bank[:, 6, :], front.h[:, i, 0:D], k_f[:, i, :], start=(i == 0),
                                         stop=(i == TILES - 1))
                    last.then_inc(summed, 1)
                    for t in range(HT):
                        for i in range(TILES):
                            last = pe.matmul(bank[:, 7, t:t + 1], k_f[:, i, t * P:(t + 1) * P],
                                             ones[:], start=(i == 0), stop=(i == TILES - 1))
                    last.then_inc(summed, 1)
                    pe.wait_ge(sum_copied, it * 2 + 1)
                    for hd in range(H):
                        j, t = hd % 4, hd // 4
                        last = pe.matmul(bank[32 * j:32 * j + 32, 0, t * D:(t + 1) * D], sums[:, hd * F:(hd + 1) * F],
                                         fold_v[:, hd, :], start=True, stop=True)
                    last.then_inc(headed, 1)
                    pe.wait_ge(blocks_made, it + 1)
                    pe.wait_ge(q_ready, (it + 1) * 8)
                    for i in range(TILES):
                        for t in range(HT):
                            last = pe.matmul(bank[:, 1, i * H + t * 4:i * H + t * 4 + 4], q_f[:, t, i * P:(i + 1) * P],
                                             blocks[:, t, :], start=True, stop=True)
                    last.then_inc(divided, 1)
                    pe.wait_ge(inverted, it + 1)
                    pe.transpose(bank[:, 1, P:2 * P], inverse[:], core.ident[:]).then_inc(inv_turned, 1)
                    pe.wait_ge(inv_copied, it + 1)
                    for t in range(HT):
                        for c in range(2):
                            n = 2 * t + c
                            if n >= 4:
                                pe.wait_ge(q_scaled, it * 8 + (n - 3))
                            for i in range(4):
                                col = (4 * c + i) * H + t * 4
                                last = pe.matmul(bank[:, 2 + n % 4, i * P:(i + 1) * P],
                                                 spreads[:, col:col + 4, :].rearrange("p j f -> p (j f)"),
                                                 inverse_t[:], start=True, stop=True)
                            last.then_inc(spread, 1)
                    pe.wait_ge(q_scaled, (it + 1) * 8)
                    pe.wait_ge(head_ready, (it + 1) * HT)
                    for c in range(2):
                        for i in range(4):
                            for t in range(HT):
                                last = pe.matmul(bank[:, 6 + c, i * D:(i + 1) * D],
                                                 q_f[:, t, (4 * c + i) * P:(4 * c + i + 1) * P], head[:, t, :],
                                                 start=(t == 0), stop=(t == HT - 1))
                        last.then_inc(projected, 1)



EXPERTS, HIDDEN, HC = 8, 512, 4
ROUTER_EPS = 1e-6


class Mixture:

    def __init__(self, core, ctx, name):
        nc = core.nc
        self.core, self.name = core, name
        core.stage = name
        sb = lambda n, shape, dtype=F32: core.sbuf(ctx, n, shape, dtype)
        self.w1 = [sb(f"w1_{part}", [P, EXPERTS, HIDDEN], F32R) for part in ("high", "low")]
        self.w2 = [sb(f"w2_{part}", [P, EXPERTS * HC, D], F32R) for part in ("high", "low")]
        self.b1 = sb("b1_folded", [P, EXPERTS * HC])
        self.b2 = sb("b2", [P, EXPERTS])
        self.x_parts = [sb(f"x_{part}", [P, B * T], F32R) for part in ("high", "low")]
        self.gates_t = nc.dram_tensor(f"{name}_gates_t", [EXPERTS, B * T], F32, kind="Internal").ap()


def mixture_weights_stage(core, mx, w):
    nc, bank = core.nc, core.bank
    core.stage = mx.name + "_w"
    s_ = core.sem
    w_in, scaled, cut, biased, b1_done = s_("w_in"), s_("scaled"), s_("cut"), s_("biased"), s_("b1_done")
    with ExitStack() as ctx:
        sb = lambda name, shape, dtype=F32: core.sbuf(ctx, name, shape, dtype)
        w1, w2 = sb("w1", [P, EXPERTS, HIDDEN]), sb("w2", [P, EXPERTS * HC, D])
        w1_scaled = sb("w1_scaled", [P, EXPERTS, HIDDEN])
        scale, shift, b1 = sb("scale", [P, EXPERTS]), sb("shift", [P, EXPERTS]), sb("b1", [P, EXPERTS * HC])
        with nc.Block() as block:

            @block.sync
            def _(sp):
                sp.dma_start(scale[:], w["scale"]).then_inc(w_in, 16)
                sp.dma_start(shift[:], w["shift"]).then_inc(w_in, 16)
                sp.dma_start(b1[:], w["b1"]).then_inc(w_in, 16)
                sp.dma_start(mx.b2[:], w["b2"]).then_inc(w_in, 16)
                sp.dma_start(w1[:], w["w1"].rearrange("e d n -> d e n")).then_inc(w_in, 16)
                sp.dma_start(w2[:], w["w2"].rearrange("e (c p) d -> p (e c) d", p=P)).then_inc(w_in, 16)

            @block.vector
            def _(dve):
                dve.wait_ge(w_in, 96)
                for e in range(EXPERTS):
                    dve.tensor_scalar(w1_scaled[:, e, :], w1[:, e, :], scale[:, e:e + 1], None,
                                      ALU.mult).then_inc(scaled, 1)
                dve.wait_ge(scaled, EXPERTS)
                dve.tensor_copy(mx.w1[0][:], w1_scaled[:]).then_inc(cut, 1)
                dve.tensor_copy(mx.w2[0][:], w2[:]).then_inc(cut, 1)
                dve.wait_ge(cut, 2)
                dve.tensor_tensor(mx.w1[1][:], w1_scaled[:], mx.w1[0][:].bitcast(F32), ALU.subtract).then_inc(cut, 1)
                dve.wait_ge(biased, 1)
                dve.tensor_tensor(mx.b1[:], bank[:, 0, 0:EXPERTS * HC], b1[:], ALU.add).then_inc(b1_done, 1)

            @block.gpsimd
            def _(pool):
                pool.wait_ge(cut, 2)
                pool.tensor_tensor(mx.w2[1][:], w2[:], mx.w2[0][:].bitcast(F32), ALU.subtract).then_inc(cut, 1)

            @block.tensor
            def _(pe):
                pe.wait_ge(w_in, 96)
                for e in range(EXPERTS):
                    for c in range(HC):
                        n = e * HC + c
                        last = pe.matmul(bank[:, 0, n:n + 1], w1[:, e, c * P:(c + 1) * P], shift[:, e:e + 1],
                                         start=True, stop=True)
                last.then_inc(biased, 1)


def route_stage(core, mx, w):
    nc, bank = core.nc, core.bank
    core.stage = mx.name + "_r"
    s_ = core.sem
    w_in, mask_made, prep, prep_mm, widened = s_("w_in"), s_("mask_made"), s_("prep"), s_("prep_mm"), s_("widened")
    routed, steps, exped, gates_turned, gates_copied, gates_out, kept = (
        s_("routed"), s_("steps"), s_("exped"), s_("gates_turned"), s_("gates_copied"), s_("gates_out"), s_("kept"))
    E = EXPERTS
    with ExitStack() as ctx:
        sb = lambda name, shape, dtype=F32: core.sbuf(ctx, name, shape, dtype)
        front = Front(core, ctx, second_eps=ROUTER_EPS)
        wr, wr_scaled, scale, shift = sb("wr", [P, E]), sb("wr_scaled", [P, E]), sb("scale", [P, 1]), sb("shift", [P, 1])
        shift_wide = sb("shift_wide", [P, P])
        router_b, bias = sb("router_b", [P, E]), sb("bias", [P, E])
        earlier = sb("earlier", [P, E, E])
        logit, e_ = sb("logit", [P, TILES, E]), sb("e", [P, TILES, E])
        row_max, row_sum, row_inv = sb("row_max", [P, TILES]), sb("row_sum", [P, TILES]), sb("row_inv", [P, TILES])
        above, equal = sb("above", [P, TILES, E, E]), sb("equal", [P, TILES, E, E])
        rank, chosen = sb("rank", [P, TILES, E]), sb("chosen", [P, TILES, E])
        gates, gates_rows = sb("gates", [P, E, TILES]), sb("gates_rows", [E * TILES, P])
        with nc.Block() as block:

            @block.sync
            def _(sp):
                for tile, source in ((wr, w["router_w"]), (scale, w["router_scale"]), (shift, w["router_shift"])):
                    sp.dma_start(tile[:], source).then_inc(w_in, 16)
                sp.dma_start(router_b[:], w["router_b"].partition_broadcast(P)).then_inc(w_in, 16)
                with sp.Fori(0, B) as it:
                    sp.wait_ge(gates_copied, it + 1)
                    dst = mx.gates_t[:, bass.ds(it * T, T)].rearrange("e (i p) -> e i p", p=P)
                    sp.dma_start(dst, gates_rows[:]).then_inc(gates_out, 16)
                sp.wait_ge(gates_out, 16 * B)

            @block.gpsimd
            def _(pool):
                pool.memset(earlier[:], 1.0).then_inc(mask_made, 1)
                pool.wait_ge(mask_made, 1)
                pool.affine_select(out=earlier[:], in_=earlier[:], compare_op=ALU.is_gt, fill=0.0, base=0,
                                   pattern=[[1, E], [-1, E]], channel_multiplier=0).then_inc(mask_made, 1)
                with pool.Fori(0, B) as it:
                    front.on_gpsimd(pool, it)

            @block.vector
            def _(dve):
                dve.wait_ge(w_in, 64)
                dve.wait_ge(mask_made, 2)
                dve.tensor_scalar(wr_scaled[:], wr[:], scale[:], None, ALU.mult).then_inc(widened, 1)
                dve.tensor_copy(shift_wide[:], shift[:].broadcast_to([P, P])).then_inc(widened, 1)
                dve.wait_ge(prep_mm, 1)
                dve.tensor_tensor(bias[:], bank[:, 3, 0:E], router_b[:], ALU.add).then_inc(prep, 1)
                dve.wait_ge(prep, 1)
                with dve.Fori(0, B) as it:
                    front.on_vector(dve, it)
                    base = it * 11

                    def step(n, instruction):
                        instruction.then_inc(steps, 1)
                        dve.wait_ge(steps, base + n)

                    dve.wait_ge(routed, it + 1)
                    logits = bank[:, 2, 0:TILES * E].rearrange("p (i e) -> p i e", e=E)
                    step(1, dve.tensor_tensor(logit[:], logits, bias[:].unsqueeze(1).broadcast_to([P, TILES, E]), ALU.add))
                    step(2, dve.tensor_reduce(row_max[:], logit[:], AX, ALU.max))
                    step(3, dve.tensor_tensor(logit[:], logit[:], row_max[:].unsqueeze(2).broadcast_to([P, TILES, E]),
                                              ALU.subtract))
                    dve.wait_ge(exped, it + 1)
                    mine = e_[:].unsqueeze(3).broadcast_to([P, TILES, E, E])
                    other = e_[:].unsqueeze(2).broadcast_to([P, TILES, E, E])
                    step(4, dve.tensor_tensor(above[:], other, mine, ALU.is_gt))
                    step(5, dve.tensor_tensor(equal[:], other, mine, ALU.is_equal))
                    tie = earlier[:].unsqueeze(1).broadcast_to([P, TILES, E, E])
                    step(6, dve.tensor_tensor(equal[:], equal[:], tie, ALU.mult))
                    step(7, dve.tensor_tensor(above[:], above[:], equal[:], ALU.add))
                    step(8, dve.tensor_reduce(rank[:], above[:], AX, ALU.add))
                    step(9, dve.scalar_tensor_tensor(chosen[:], rank[:], 1.5, e_[:], ALU.is_lt, ALU.mult))
                    step(10, dve.tensor_reduce(row_sum[:], chosen[:], AX, ALU.add))
                    step(11, dve.reciprocal(row_inv[:], row_sum[:]))
                    dve.wait_ge(gates_turned, it)
                    dve.tensor_tensor(gates[:].rearrange("p e i -> p i e"), chosen[:],
                                      row_inv[:].unsqueeze(2).broadcast_to([P, TILES, E]), ALU.mult).then_inc(kept, 1)
                    dve.wait_ge(front.copied, (it + 1) * 2)
                    high, low = (part[:, bass.ds(it * T, T)] for part in mx.x_parts)
                    dve.tensor_copy(high, front.h_t[:]).then_inc(kept, 1)
                    dve.wait_ge(kept, it * 3 + 2)
                    dve.tensor_tensor(low, front.h_t[:], high.bitcast(F32), ALU.subtract).then_inc(kept, 1)

            @block.scalar
            def _(act):
                with act.Fori(0, B) as it:
                    act.wait_ge(kept, it * 3)
                    front.on_scalar(act, it)
                    act.wait_ge(steps, it * 11 + 3)
                    act.activation(e_[:], logit[:], ACT.Exp).then_inc(exped, 1)
                    act.wait_ge(gates_turned, it + 1)
                    act.wait_ge(gates_out, it * 16)
                    act.activation(gates_rows[:], bank[0:E * TILES, 3, 0:P], ACT.Copy).then_inc(gates_copied, 1)

            @block.tensor
            def _(pe):
                pe.wait_ge(widened, 2)
                pe.matmul(bank[:, 3, 0:E], shift_wide[:], wr[:], start=True, stop=True).then_inc(prep_mm, 1)
                pe.wait_ge(prep, 1)
                with pe.Fori(0, B) as it:
                    front.on_tensor(pe, it)
                    pe.wait_ge(front.copied, (it + 1) * 2)
                    pe.wait_ge(steps, it * 11)
                    for i in range(TILES):
                        last = pe.matmul(bank[:, 2, i * E:(i + 1) * E], front.h_t[:, i * P:(i + 1) * P], wr_scaled[:],
                                         start=True, stop=True)
                    last.then_inc(routed, 1)
                    wait_apart(core, pe, gates_copied, it)
                    wait_apart(core, pe, kept, it * 3 + 1)
                    pe.transpose(bank[0:E * TILES, 3, 0:P], gates[:].rearrange("p e i -> p (e i)"),
                                 core.ident[:]).then_inc(gates_turned, 1)


def experts_stage(core, mx):
    nc, x, bank = core.nc, core.x, core.bank
    core.stage = mx.name + "_e"
    s_ = core.sem
    CHUNKS, STEPS, LAG, RING, GATES = B * T // BANK, EXPERTS * HC, 3, 8, 4
    TURN_AT = 6
    gate_in = [s_(f"gate_in{k}") for k in range(GATES)]
    hidden, active, high_cut, cut, met = s_("hidden"), s_("active"), s_("high_cut"), s_("cut"), s_("met")
    gated, summed, turned, added = s_("gated"), s_("summed"), s_("turned"), s_("added")
    HID, OUT, TURN = 0, 4, 6
    PRODUCTS = ((0, 0), (0, 1), (1, 0))
    with ExitStack() as ctx:
        sb = lambda name, shape, dtype=F32: core.sbuf(ctx, name, shape, dtype)
        gate = sb("gate", [P, GATES, BANK])
        h = sb("h", [P, RING, BANK])
        h_parts = [sb("h_high", [P, RING, BANK], F32R), sb("h_low", [P, RING, BANK], F32R)]
        part = sb("part", [P, 2, BANK])
        total = sb("total", [P, BANK])
        with nc.Block() as block:

            @block.sync
            def _(sp):
                def chunk(it):
                    for e in range(EXPERTS):
                        wait_past(sp, gated, it * EXPERTS + (e - GATES + 1))
                        src = mx.gates_t[e:e + 1, bass.ds(it * BANK, BANK)].broadcast_to([P, BANK])
                        sp.dma_start(gate[:, e % GATES, :], src).then_inc(gate_in[e % GATES], 16)

                chunk(0)
                with sp.Fori(1, CHUNKS) as it:
                    chunk(it)

            @block.vector
            def _(dve):
                def gated_part(it, e):
                    dve.wait_ge(met, it * STEPS + HC * (e + 1))
                    dve.wait_ge(gate_in[e % GATES], it * 32 + 16 * (e // GATES + 1))
                    wait_past(dve, summed, it * EXPERTS + (e - 1))
                    dve.scalar_tensor_tensor(part[:, e % 2, :], bank[:, OUT + e % 2, :],
                                             mx.b2[:, e % EXPERTS:e % EXPERTS + 1], gate[:, e % GATES, :],
                                             ALU.add, ALU.mult).then_inc(gated, 1)

                def add_chunk(it):
                    dve.wait_ge(turned, it + 1)
                    rows = x[:, bass.ds(it * 4, 4), :].rearrange("p i d -> p (i d)")
                    dve.tensor_tensor(rows, rows, bank[:, TURN, :], ALU.add).then_inc(added, 1)

                def chunk(it, first):
                    for s in range(STEPS):
                        n, slot = it * STEPS + s, s % RING
                        dve.wait_ge(active, n + 1)
                        wait_past(dve, met, it * STEPS + (s - RING + 1))
                        dve.tensor_copy(h_parts[0][:, slot, :], h[:, slot, :]).then_inc(high_cut, 1)
                        dve.wait_ge(high_cut, n + 1)
                        dve.tensor_tensor(h_parts[1][:, slot, :], h[:, slot, :], h_parts[0][:, slot, :].bitcast(F32),
                                          ALU.subtract).then_inc(cut, 1)
                        if s % HC == HC - 1 and not (first and s < HC):
                            gated_part(it, (s - LAG - HC) // HC)
                        if s == TURN_AT + 2 and not first:
                            add_chunk(it - 1)

                chunk(0, True)
                with dve.Fori(1, CHUNKS) as it:
                    chunk(it, False)
                gated_part(CHUNKS, -1)
                add_chunk(CHUNKS - 1)

            @block.gpsimd
            def _(pool):
                def chunk(it):
                    for e in range(EXPERTS):
                        if e == 0:
                            wait_apart(core, pool, turned, it)
                            wait_apart(core, pool, gated, it * EXPERTS + 1)
                            pool.tensor_copy(total[:], part[:, 0, :]).then_inc(summed, 1)
                        else:
                            pool.wait_ge(gated, it * EXPERTS + (e + 1))
                            pool.wait_ge(summed, it * EXPERTS + e)
                            pool.tensor_tensor(total[:], total[:], part[:, e % 2, :], ALU.add).then_inc(summed, 1)

                chunk(0)
                with pool.Fori(1, CHUNKS) as it:
                    chunk(it)

            @block.scalar
            def _(act):
                def chunk(it):
                    for s in range(STEPS):
                        act.wait_ge(hidden, it * STEPS + (s + 1))
                        wait_past(act, cut, it * STEPS + (s - RING + 1))
                        act.activation(h[:, s % RING, :], bank[:, HID + s % 4, :], ACT.Gelu,
                                       bias=mx.b1[:, s:s + 1]).then_inc(active, 1)

                chunk(0)
                with act.Fori(1, CHUNKS) as it:
                    chunk(it)

            @block.tensor
            def _(pe):
                def to_hidden(it, s):
                    wait_past(pe, active, it * STEPS + (s - 3))
                    e, c = s // HC, s % HC
                    for n, (a, b) in enumerate(PRODUCTS):
                        last = pe.matmul(bank[:, HID + s % 4, :], mx.w1[a][:, e, c * P:(c + 1) * P],
                                         mx.x_parts[b][:, bass.ds(it * BANK, BANK)], start=(n == 0), stop=(n == 2))
                    last.then_inc(hidden, 1)

                def to_output(it, s):
                    pe.wait_ge(cut, it * STEPS + (s + 1))
                    e, c = s // HC, s % HC
                    if c == 0:
                        wait_past(pe, gated, it * EXPERTS + (e - 1))
                    for n, (a, b) in enumerate(PRODUCTS):
                        last = pe.matmul(bank[:, OUT + e % 2, :], mx.w2[a][:, s % STEPS, :], h_parts[b][:, s % RING, :],
                                         start=(c == 0 and n == 0), stop=(c == HC - 1 and n == 2))
                    last.then_inc(met, 1)

                def turn_chunk(it):
                    pe.wait_ge(summed, (it + 1) * EXPERTS)
                    wait_past(pe, added, it)
                    for i in range(4):
                        last = pe.transpose(bank[:, TURN, i * P:(i + 1) * P], total[:, i * P:(i + 1) * P], core.ident[:])
                    last.then_inc(turned, 1)

                def chunk(it, first):
                    for s in range(STEPS):
                        to_hidden(it, s)
                        if not (first and s < LAG):
                            to_output(it, s - LAG)
                        if s == TURN_AT and not first:
                            turn_chunk(it - 1)

                chunk(0, True)
                with pe.Fori(1, CHUNKS) as it:
                    chunk(it, False)
                for s in range(-LAG, 0):
                    to_output(CHUNKS, s)
                turn_chunk(CHUNKS - 1)


def mixture_layer(core, name, w):
    with ExitStack() as ctx:
        mx = Mixture(core, ctx, name)
        mixture_weights_stage(core, mx, w)
        route_stage(core, mx, w)
        experts_stage(core, mx)



def recurrent_stage(core, w):
    nc, x, bank = core.nc, core.x, core.bank
    core.stage = "rec"
    s_ = core.sem
    H, DH, RANK, PAIRS, UNITS = 16, 8, 16, 8, 16
    NORM, GATE_SCALE, Q_SCALE = 1e-5, 1.0 / 16.0, float(DH) ** -0.5
    w_in, filled, made, folded, fold_copied = s_("w_in"), s_("filled"), s_("made"), s_("folded"), s_("fold_copied")
    projected, proj_copied, gate_steps, gate_min, cut, rest_cut = (
        s_("projected"), s_("proj_copied"), s_("gate_steps"), s_("gate_min"), s_("cut"), s_("rest_cut"))
    gates_out, silu_ready = s_("gates_out"), s_("silu_ready")
    decay_spread, v_spread, k_spread, q_spread = s_("decay_spread"), s_("v_spread"), s_("k_spread"), s_("q_spread")
    decay_copied, v_copied, outer, scanned, read = (
        s_("decay_copied"), s_("v_copied"), s_("outer"), s_("scanned"), s_("read"))
    gathered, got, turned, squared, meaned, root_steps, normed_out, silued = (
        s_("gathered"), s_("got"), s_("o_turned"), s_("squared"), s_("meaned"), s_("root_steps"), s_("normed_out"),
        s_("silued"))
    y_turned, y_copied, out_done, added = s_("y_turned"), s_("y_copied"), s_("out_done"), s_("added")
    with ExitStack() as ctx:
        sb = lambda name, shape, dtype=F32: core.sbuf(ctx, name, shape, dtype)
        front = Front(core, ctx)
        wq, wk, wv, wg, wo = (sb(n, [P, D]) for n in ("wq", "wk", "wv", "wg", "wo"))
        g1, g2, fold_g, wo_normed = sb("g1", [RANK, D]), sb("g2", [RANK, D]), sb("fold_g", [P, D]), sb("wo_normed", [P, D])
        g_bias, norm = sb("g_bias", [P, 1]), sb("norm", [P, 1])
        pick_d, pick_v = sb("pick_d", [P, PAIRS * P], F32R), sb("pick_v", [P, PAIRS * P], F32R)
        same = sb("same", [P, 2 * DH])
        gather = sb("gather", [P, PAIRS, P])
        minus_half = sb("minus_half", [P, 4 * H])
        base = [sb(n, [P, T]) for n in ("q_t", "k_t", "v_t", "z_t")]
        size, floor, decay = sb("size", [P, T]), sb("floor", [P, T]), sb("decay", [P, T])
        high = [sb(f"{n}_high", [P, T], F32R) for n in ("q", "k", "v", "decay")]
        low = [sb(f"{n}_low", [P, T], F32R) for n in ("q", "k", "v", "decay")]
        silu = sb("silu", [P, TILES, D])
        decay_p, v_p, kv = sb("decay_p", [P, 2, BANK]), sb("v_p", [P, 2, BANK]), sb("kv", [P, 2, BANK])
        state = sb("state", [P, 2, PAIRS, BANK])
        q_state = sb("q_state", [P, 2, BANK])
        o_t, square, y, y_t = sb("o_t", [P, BANK]), sb("square", [P, BANK]), sb("y", [P, BANK]), sb("y_t", [P, BANK])
        mean, root = sb("mean", [P, 4 * H]), sb("root", [P, 4 * H])
        with nc.Block() as block:

            @block.sync
            def _(sp):
                for tile, source in ((wq, "q"), (wk, "k"), (wv, "v"), (wg, "g"), (wo, "o"), (g1, "g1"), (g2, "g2"),
                                     (g_bias, "g_bias")):
                    sp.dma_start(tile[:], w[source]).then_inc(w_in, 16)
                sp.dma_start(norm[:], w["norm"].rearrange("(o v) -> o v", o=1).broadcast_to([H, DH])).then_inc(w_in, 16)

            @block.gpsimd
            def _(pool):
                pool.memset(minus_half[:], -0.5).then_inc(filled, 1)
                pool.memset(gather[:], 0.0).then_inc(filled, 1)
                with pool.Fori(0, B) as it:
                    front.on_gpsimd(pool, it)
                    for c in range(2):
                        n = it * 2 + c
                        pool.wait_ge(filled, 2)
                        wait_apart(core, pool, meaned, n + 1)
                        pool.tensor_scalar(root[:], mean[:], 1.0 / DH, NORM, ALU.mult, ALU.add).then_inc(root_steps, 1)
                        pool.wait_ge(root_steps, it * 4 + 2 * c + 1)
                        pool.tensor_tensor(root[:], root[:], minus_half[:], ALU.pow).then_inc(root_steps, 1)

            @block.vector
            def _(dve):
                ident = core.ident
                dve.wait_ge(w_in, 144)
                dve.wait_ge(filled, 2)
                dve.tensor_scalar(wo_normed[:], wo[:], norm[:], None, ALU.mult).then_inc(made, 1)
                dve.tensor_copy(pick_d[:].rearrange("p (m v) -> p m v", v=DH),
                                ident[:].unsqueeze(2).broadcast_to([P, P, DH])).then_inc(made, 1)
                dve.tensor_copy(pick_v[:].rearrange("p (h d v) -> p h d v", d=DH, v=DH),
                                ident[:].rearrange("p (h v) -> p h v", v=DH).unsqueeze(2).broadcast_to(
                                    [P, H, DH, DH])).then_inc(made, 1)
                dve.tensor_reduce(same[:].rearrange("p (j v) -> p j v", v=DH),
                                  ident[:].rearrange("p (j d v) -> p j v d", d=DH, v=DH), AX, ALU.add).then_inc(made, 1)
                dve.wait_ge(made, 4)
                for s in range(PAIRS):
                    dve.tensor_copy(gather[:, s, 2 * DH * s:2 * DH * (s + 1)], same[:]).then_inc(made, 1)
                dve.wait_ge(folded, 1)
                dve.tensor_copy(fold_g[:], bank[:, 7, 0:D]).then_inc(fold_copied, 1)

                def tail(it, c, part):
                    n = it * 2 + c
                    rows = bank[:, 7, :].rearrange("p (g v) -> p g v", v=DH)
                    if part == 0:
                        dve.wait_ge(squared, n + 1)
                        dve.tensor_reduce(mean[:], square[:].rearrange("p (g v) -> p g v", v=DH), AX,
                                          ALU.add).then_inc(meaned, 1)
                    if part == 1:
                        dve.wait_ge(root_steps, it * 4 + (2 * c + 2))
                        dve.tensor_tensor(y[:].rearrange("p (g v) -> p g v", v=DH), rows,
                                          root[:].unsqueeze(2).broadcast_to([P, 4 * H, DH]), ALU.mult).then_inc(normed_out, 1)
                        dve.wait_ge(normed_out, n + 1)
                        dve.wait_ge(silu_ready, it * 2 + 2)
                        dve.tensor_tensor(y[:], y[:], silu[:, 4 * c:4 * c + 4, :].rearrange("p i d -> p (i d)"),
                                          ALU.mult).then_inc(silued, 1)
                    if part == 2:
                        dve.wait_ge(out_done, n + 1)
                        row = x[:, bass.ds(it * TILES + 4 * c, 4), :].rearrange("p i d -> p (i d)")
                        dve.tensor_tensor(row, row, bank[:, 7, :], ALU.add).then_inc(added, 1)

                with dve.Fori(0, B) as it:
                    front.on_vector(dve, it)
                    for n, whole in enumerate((base[0], base[1], base[2])):
                        dve.wait_ge(proj_copied, it * 8 + 2 * (n + 1))
                        dve.wait_ge(q_spread, it * UNITS)
                        dve.tensor_copy(high[n][:], whole[:]).then_inc(cut, 1)
                        dve.wait_ge(cut, it * 4 + (n + 1))
                        dve.tensor_tensor(low[n][:], whole[:], high[n][:].bitcast(F32), ALU.subtract).then_inc(rest_cut, 1)
                    dve.wait_ge(proj_copied, it * 8 + 8)
                    dve.tensor_scalar(floor[:], base[3][:], 0.0, None, ALU.min).then_inc(gate_min, 1)
                    dve.wait_ge(gate_min, it * 2 + 1)
                    dve.wait_ge(gate_steps, it * 3 + 3)
                    dve.tensor_tensor(floor[:], floor[:], size[:], ALU.subtract).then_inc(gate_min, 1)
                    dve.wait_ge(gates_out, it + 1)
                    dve.tensor_copy(high[3][:], decay[:]).then_inc(cut, 1)
                    dve.wait_ge(cut, it * 4 + 4)
                    dve.tensor_tensor(low[3][:], decay[:], high[3][:].bitcast(F32), ALU.subtract).then_inc(rest_cut, 1)
                    for c in range(2):
                        for s in range(PAIRS):
                            u, slot = it * UNITS + (8 * c + s), s % 2
                            dve.wait_ge(k_spread, u + 1)
                            dve.wait_ge(v_copied, u + 1)
                            dve.tensor_tensor(kv[:, slot, :], bank[:, 4, :], v_p[:, slot, :], ALU.mult).then_inc(outer, 1)
                            dve.wait_ge(outer, u + 1)
                            dve.wait_ge(decay_copied, u + 1)
                            start = 0.0 if c == 0 else state[:, 0, s, BANK - 1:BANK]
                            dve.tensor_tensor_scan(state[:, c, s, :], decay_p[:, slot, :], kv[:, slot, :], start,
                                                   ALU.mult, ALU.add).then_inc(scanned, 1)
                            dve.wait_ge(scanned, u + 1)
                            dve.wait_ge(q_spread, u + 1)
                            if s >= 2:
                                dve.wait_ge(gathered, it * UNITS + (8 * c + s - 1))
                            else:
                                dve.wait_ge(gathered, it * UNITS + 8 * c)
                            dve.tensor_tensor(q_state[:, slot, :], state[:, c, s, :], bank[:, 5, :],
                                              ALU.mult).then_inc(read, 1)
                            if c == 1 and s in (2, 4, 6):
                                tail(it, 0, (s - 2) // 2)
                    for part in range(3):
                        tail(it, 1, part)

            @block.scalar
            def _(act):
                act.wait_ge(w_in, 144)

                def tail(it, c, part):
                    n = it * 2 + c
                    if part == 0:
                        act.wait_ge(gathered, it * UNITS + 8 * (c + 1))
                        act.activation(o_t[:], bank[:, 6, :], ACT.Copy).then_inc(got, 1)
                    if part == 1:
                        act.wait_ge(turned, n + 1)
                        act.activation(square[:], bank[:, 7, :], ACT.Square).then_inc(squared, 1)
                    if part == 2:
                        act.wait_ge(y_turned, n + 1)
                        act.activation(y_t[:], bank[:, 7, :], ACT.Copy).then_inc(y_copied, 1)

                with act.Fori(0, B) as it:
                    front.on_scalar(act, it)
                    act.wait_ge(rest_cut, it * 4)
                    for n in range(4):
                        for c in range(2):
                            act.wait_ge(projected, it * 10 + (2 * n + c + 1))
                            dst, src = base[n][:, c * BANK:(c + 1) * BANK], bank[:, 2 + (2 * n + c) % 4, :]
                            if n == 3:
                                act.activation(dst, src, ACT.Identity, bias=g_bias[:]).then_inc(proj_copied, 1)
                            else:
                                act.activation(dst, src, ACT.Copy, scale=Q_SCALE if n == 0 else 1.0).then_inc(proj_copied, 1)
                    act.wait_ge(proj_copied, it * 8 + 8)
                    act.activation(size[:], base[3][:], ACT.Abs).then_inc(gate_steps, 1)
                    act.wait_ge(gate_steps, it * 3 + 1)
                    act.activation(size[:], size[:], ACT.Exp, scale=-1.0).then_inc(gate_steps, 1)
                    act.wait_ge(gate_steps, it * 3 + 2)
                    act.activation(size[:], size[:], ACT.Ln, bias=1.0).then_inc(gate_steps, 1)
                    act.wait_ge(gate_min, it * 2 + 2)
                    act.activation(decay[:], floor[:], ACT.Exp, scale=GATE_SCALE).then_inc(gates_out, 1)
                    for c in range(2):
                        act.wait_ge(projected, it * 10 + (9 + c))
                        act.activation(silu[:, 4 * c:4 * c + 4, :].rearrange("p i d -> p (i d)"), bank[:, 6 + c, :],
                                       ACT.Silu).then_inc(silu_ready, 1)
                    for c in range(2):
                        for s in range(PAIRS):
                            u, slot = it * UNITS + (8 * c + s), s % 2
                            if s >= 2:
                                act.wait_ge(scanned, it * UNITS + (8 * c + s - 1))
                            else:
                                act.wait_ge(scanned, it * UNITS + 8 * c)
                            act.wait_ge(decay_spread, u + 1)
                            act.activation(decay_p[:, slot, :], bank[:, slot, :], ACT.Copy).then_inc(decay_copied, 1)
                            act.wait_ge(v_spread, u + 1)
                            act.activation(v_p[:, slot, :], bank[:, 2 + slot, :], ACT.Copy).then_inc(v_copied, 1)
                            if c == 1 and s in (0, 1, 4):
                                tail(it, 0, (0, 1, 4).index(s))
                    for part in range(3):
                        tail(it, 1, part)

            @block.tensor
            def _(pe):
                pe.wait_ge(w_in, 144)
                pe.matmul(bank[:, 7, 0:D], g1[:], g2[:], start=True, stop=True).then_inc(folded, 1)
                pe.wait_ge(fold_copied, 1)
                pe.wait_ge(made, 12)

                def spread_pair(it, c, s):
                    u, slot = it * UNITS + (8 * c + s), s % 2
                    cols, pick = slice(c * BANK, (c + 1) * BANK), slice(s * P, (s + 1) * P)
                    for n, picks, dst, ready, free, count in (
                            (3, pick_d, slot, decay_spread, decay_copied, 1), (2, pick_v, 2 + slot, v_spread, v_copied, 1),
                            (1, pick_d, 4, k_spread, outer, 0), (0, pick_d, 5, q_spread, read, 0)):
                        pe.wait_ge(free, it * UNITS + max(8 * c + s - count, 0))
                        pe.matmul(bank[:, dst, :], picks[:, pick], high[n][:, cols], start=True, stop=False)
                        pe.matmul(bank[:, dst, :], picks[:, pick], low[n][:, cols], start=False, stop=True).then_inc(ready, 1)

                def gather_pair(it, c, s):
                    u, slot = it * UNITS + (8 * c + s), s % 2
                    pe.wait_ge(read, u + 1)
                    if s == 0:
                        pe.wait_ge(got, it * 2 + c)
                    pe.matmul(bank[:, 6, :], gather[:, s, :], q_state[:, slot, :], start=(s == 0),
                              stop=(s == PAIRS - 1)).then_inc(gathered, 1)

                def tail(it, c, part):
                    n = it * 2 + c
                    if part == 0:
                        pe.wait_ge(got, n + 1)
                        pe.wait_ge(added, n)
                        for i in range(4):
                            last = pe.transpose(bank[:, 7, i * P:(i + 1) * P], o_t[:, i * P:(i + 1) * P], core.ident[:])
                        last.then_inc(turned, 1)
                    if part == 1:
                        pe.wait_ge(silued, n + 1)
                        for i in range(4):
                            last = pe.transpose(bank[:, 7, i * P:(i + 1) * P], y[:, i * P:(i + 1) * P], core.ident[:])
                        last.then_inc(y_turned, 1)
                        pe.wait_ge(y_copied, n + 1)
                        for i in range(4):
                            last = pe.matmul(bank[:, 7, i * P:(i + 1) * P], y_t[:, i * P:(i + 1) * P], wo_normed[:],
                                             start=True, stop=True)
                        last.then_inc(out_done, 1)

                with pe.Fori(0, B) as it:
                    pe.wait_ge(decay_copied, it * UNITS)
                    front.on_tensor(pe, it)
                    pe.wait_ge(front.copied, (it + 1) * 2)
                    pe.wait_ge(v_copied, it * UNITS)
                    pe.wait_ge(read, it * UNITS)
                    for n, weight in enumerate((wq, wk, wv, fold_g)):
                        for c in range(2):
                            if n >= 2:
                                pe.wait_ge(proj_copied, it * 8 + (2 * n + c - 3))
                            pe.matmul(bank[:, 2 + (2 * n + c) % 4, :], weight[:], front.h_t[:, c * BANK:(c + 1) * BANK],
                                      start=True, stop=True).then_inc(projected, 1)
                    pe.wait_ge(got, it * 2)
                    pe.wait_ge(added, it * 2)
                    for c in range(2):
                        for i in range(4):
                            t = 4 * c + i
                            last = pe.matmul(bank[:, 6 + c, i * P:(i + 1) * P], front.h_t[:, t * P:(t + 1) * P], wg[:],
                                             start=True, stop=True)
                        last.then_inc(projected, 1)
                    pe.wait_ge(proj_copied, it * 8 + 8)
                    pe.wait_ge(silu_ready, it * 2 + 2)
                    pe.wait_ge(rest_cut, it * 4 + 4)
                    for c in range(2):
                        for s in range(PAIRS):
                            spread_pair(it, c, s)
                            if s:
                                gather_pair(it, c, s - 1)
                            if c == 1 and s == 1:
                                tail(it, 0, 0)
                            if c == 1 and s == 5:
                                tail(it, 0, 1)
                        gather_pair(it, c, PAIRS - 1)
                    tail(it, 1, 0)
                    tail(it, 1, 1)


def program(nc, a, out, stages=None):
    with ExitStack() as ctx:
        core = Core(nc, ctx)
        nested = {"q": a["L0_ffn_q_w_t"], "k": a["L0_ffn_k_w_t"], "v": a["L0_ffn_v_w_t"], "o": a["L0_ffn_o_w_t"],
                  "out_bias": a["L0_ffn_o_b"], "q_bias": a["L0_ffn_q_b"], "k_bias": a["L0_ffn_k_b"],
                  "v_bias": a["L0_ffn_v_b"], "norm_w": a["L0_ffn_norm_w"], "norm_b": a["L0_ffn_norm_b"]}
        wide = {"q": a["L0_attn_b_Wq_t"], "k": a["L0_attn_b_Wk_t"], "v": a["L0_attn_b_Wv_t"],
                "o": a["L0_attn_b_Wff_t"], "out_bias": a["L0_attn_b_bff"]}
        linear = {"q": a["L1_attn_a_Wq_t"], "k": a["L1_attn_a_Wk_t"], "v": a["L1_attn_a_Wv_t"],
                  "o": a["L1_attn_a_Wproj"], "fq": a["L1_attn_a_wq_feat"], "fk": a["L1_attn_a_wk_feat"],
                  "bq": a["L1_attn_a_bq"], "bk": a["L1_attn_a_bk"], "bv": a["L1_attn_a_bv"],
                  "out_bias": a["L1_attn_a_bproj"]}
        mixture = {"router_w": a["L1_ffn_router_w_t"], "router_scale": a["L1_ffn_router_ln_scale"],
                   "router_shift": a["L1_ffn_router_ln_bias"], "router_b": a["L1_ffn_router_b"],
                   "scale": a["L1_ffn_expert_ln_scale_t"], "shift": a["L1_ffn_expert_ln_bias_t"],
                   "w1": a["L1_ffn_w1_t"], "b1": a["L1_ffn_b1_t"], "w2": a["L1_ffn_w2_t"], "b2": a["L1_ffn_b2_t"]}
        recurrent = {"q": a["L1_attn_b_Wq"], "k": a["L1_attn_b_Wk"], "v": a["L1_attn_b_Wv"], "g": a["L1_attn_b_Wg"],
                     "o": a["L1_attn_b_Wo"], "g1": a["L1_attn_b_Wg1_t"], "g2": a["L1_attn_b_Wg2"],
                     "g_bias": a["L1_attn_b_bg2"], "norm": a["L1_attn_b_g_norm_w"]}
        plan = [
            lambda: causal_stage(core, a["L0_attn_a_Wq_t"], a["L0_attn_a_Wk_t"], a["L0_attn_a_Wv_t"]),
            lambda: heads_layer(core, "nested1", 8, nested, True),
            lambda: heads_layer(core, "wide", 16, wide, False),
            lambda: heads_layer(core, "nested2", 8, nested, True),
            lambda: kernel_attention_stage(core, linear),
            lambda: mixture_layer(core, "mix1", mixture),
            lambda: recurrent_stage(core, recurrent),
            lambda: mixture_layer(core, "mix2", mixture),
        ]
        load_stage(core, a["L0_attn_a_x"])
        for n, stage in enumerate(plan):
            if stages is None or n in stages:
                with nc.cleanup_on_exit():
                    stage()
        store_stage(core, out)


_LAYOUT = [
    ("L0_attn_a_x", "L0_attn_a_x", False),
    ("L0_attn_a_Wq_t", "L0_attn_a_Wq", True),
    ("L0_attn_a_Wk_t", "L0_attn_a_Wk", True),
    ("L0_attn_a_Wv_t", "L0_attn_a_Wv", True),
    ("L0_attn_b_Wq_t", "L0_attn_b_Wq", True),
    ("L0_attn_b_Wk_t", "L0_attn_b_Wk", True),
    ("L0_attn_b_Wv_t", "L0_attn_b_Wv", True),
    ("L0_attn_b_Wff_t", "L0_attn_b_Wff", True),
    ("L0_attn_b_bff", "L0_attn_b_bff", False),
    ("L0_ffn_norm_w", "L0_ffn_norm_w", False),
    ("L0_ffn_norm_b", "L0_ffn_norm_b", False),
    ("L0_ffn_q_w_t", "L0_ffn_q_w", True),
    ("L0_ffn_q_b", "L0_ffn_q_b", False),
    ("L0_ffn_k_w_t", "L0_ffn_k_w", True),
    ("L0_ffn_k_b", "L0_ffn_k_b", False),
    ("L0_ffn_v_w_t", "L0_ffn_v_w", True),
    ("L0_ffn_v_b", "L0_ffn_v_b", False),
    ("L0_ffn_o_w_t", "L0_ffn_o_w", True),
    ("L0_ffn_o_b", "L0_ffn_o_b", False),
    ("L1_attn_a_Wq_t", "L1_attn_a_Wq", True),
    ("L1_attn_a_Wk_t", "L1_attn_a_Wk", True),
    ("L1_attn_a_Wv_t", "L1_attn_a_Wv", True),
    ("L1_attn_a_Wproj", "L1_attn_a_Wproj", False),
    ("L1_attn_a_wq_feat", "L1_attn_a_wq_feat", False),
    ("L1_attn_a_wk_feat", "L1_attn_a_wk_feat", False),
    ("L1_attn_a_bq", "L1_attn_a_bq", (16, 64)),
    ("L1_attn_a_bk", "L1_attn_a_bk", (16, 64)),
    ("L1_attn_a_bv", "L1_attn_a_bv", (16, 64)),
    ("L1_attn_a_bproj", "L1_attn_a_bproj", False),
    ("L1_attn_b_Wq", "L1_attn_b_Wq", False),
    ("L1_attn_b_Wk", "L1_attn_b_Wk", False),
    ("L1_attn_b_Wv", "L1_attn_b_Wv", False),
    ("L1_attn_b_Wg1_t", "L1_attn_b_Wg1", True),
    ("L1_attn_b_Wg2", "L1_attn_b_Wg2", False),
    ("L1_attn_b_bg2", "L1_attn_b_bg2", (1, D)),
    ("L1_attn_b_Wg", "L1_attn_b_Wg", False),
    ("L1_attn_b_g_norm_w", "L1_attn_b_g_norm_w", False),
    ("L1_attn_b_Wo", "L1_attn_b_Wo", False),
    ("L1_ffn_router_ln_scale", "L1_ffn_router_ln_scale", (1, D)),
    ("L1_ffn_router_ln_bias", "L1_ffn_router_ln_bias", (1, D)),
    ("L1_ffn_router_w_t", "L1_ffn_router_w", True),
    ("L1_ffn_router_b", "L1_ffn_router_b", False),
    ("L1_ffn_expert_ln_scale_t", "L1_ffn_expert_ln_scale", True),
    ("L1_ffn_expert_ln_bias_t", "L1_ffn_expert_ln_bias", True),
    ("L1_ffn_w1_t", "L1_ffn_w1", True),
    ("L1_ffn_b1_t", "L1_ffn_b1", (EXPERTS * HC, P)),
    ("L1_ffn_w2_t", "L1_ffn_w2", True),
    ("L1_ffn_b2_t", "L1_ffn_b2", True),
]


def laid_out(inputs):
    import numpy as np

    arrays = {}
    for name, source, swapped in _LAYOUT:
        v = np.asarray(inputs[source])
        if isinstance(swapped, tuple):
            v = v.reshape(swapped)
        arrays[name] = np.ascontiguousarray(np.swapaxes(v, -1, -2) if swapped else v)
    return arrays


def kernel(**inputs):
    import concourse.bacc as bacc
    from concourse.bass_utils import run_bass_kernel_spmd

    nc = bacc.Bacc("TRN2", target_bir_lowering=False, num_devices=1)
    arrays = laid_out(inputs)
    a = {n: nc.dram_tensor(n, v.shape, mybir.dt.from_np(v.dtype), kind="ExternalInput").ap()
         for n, v in arrays.items()}
    out = nc.dram_tensor("out", (B, T, D), F32, kind="ExternalOutput").ap()
    program(nc, a, out)
    return run_bass_kernel_spmd(nc, [arrays], core_ids=[0]).results[0]["out"]
```

```python
from contextlib import ExitStack

import concourse.bass as bass
from concourse import mybir

F32 = mybir.dt.float32
F32R = mybir.dt.float32r
BF16 = mybir.dt.bfloat16
ALU = mybir.AluOpType
ACT = mybir.ActivationFunctionType
AX = mybir.AxisListType.X

P = 128
D = 128
B = 4
T = 1024
TILES = T // P
NT = B * TILES
BANK = 512
MASKED = -1.0e30
LN_EPS = 1e-5


class Core:

    def __init__(self, nc, ctx):
        self.nc, self.ctx = nc, ctx
        self.x = ctx.enter_context(nc.sbuf_tensor("x_resident", [P, NT, D], F32))
        self.ident = ctx.enter_context(nc.sbuf_tensor("ident", [P, P], F32))
        self.ident_bf = ctx.enter_context(nc.sbuf_tensor("ident_bf", [P, P], BF16))
        self.minus_half = ctx.enter_context(nc.sbuf_tensor("minus_half", [P, 2 * TILES], F32))
        self.bank = ctx.enter_context(nc.psum_tensor("banks", [P, 8, BANK], F32))
        self.passed = nc.alloc_semaphore(name="passed")
        self.stage = ""

    def sem(self, name):
        return self.nc.alloc_semaphore(name=f"{self.stage}_{name}")

    def sbuf(self, stage_ctx, name, shape, dtype=F32):
        return stage_ctx.enter_context(self.nc.sbuf_tensor(f"{self.stage}_{name}", shape, dtype))


def wait_past(engine, semaphore, value):
    if not (isinstance(value, int) and value <= 0):
        engine.wait_ge(semaphore, value)


def wait_apart(core, engine, semaphore, value):
    engine.wait_ge(semaphore, value)
    engine.sem_inc(core.passed, 1)


def tile_at(x, tile):
    return x[:, bass.ds(tile, 1), :].rearrange("p o d -> p (o d)")


def load_stage(core, x_dram):
    nc = core.nc
    core.stage = "load"
    x_in, filled, shaped = core.sem("x_in"), core.sem("filled"), core.sem("shaped")
    with nc.Block() as block:

        @block.sync
        def _(sp):
            for b in range(B):
                sp.dma_start(core.x[:, b * TILES:(b + 1) * TILES, :],
                             x_dram[b].rearrange("(i p) d -> p i d", p=P)).then_inc(x_in, 16)
            sp.wait_ge(x_in, 16 * B)

        @block.gpsimd
        def _(pool):
            pool.memset(core.ident[:], 0.0).then_inc(filled, 1)
            pool.wait_ge(filled, 1)
            pool.affine_select(out=core.ident[:], in_=core.ident[:], compare_op=ALU.not_equal, fill=1.0,
                               base=0, pattern=[[-1, P]], channel_multiplier=1).then_inc(shaped, 1)
            pool.memset(core.minus_half[:], -0.5).then_inc(filled, 1)
            pool.wait_ge(filled, 2)
            pool.wait_ge(shaped, 1)
            pool.tensor_copy(core.ident_bf[:], core.ident[:]).then_inc(shaped, 1)
            pool.wait_ge(shaped, 2)


def store_stage(core, out_dram):
    nc = core.nc
    core.stage = "store"
    stored = core.sem("stored")
    with nc.Block() as block:

        @block.sync
        def _(sp):
            for b in range(B):
                sp.dma_start(out_dram[b].rearrange("(i p) d -> p i d", p=P),
                             core.x[:, b * TILES:(b + 1) * TILES, :]).then_inc(stored, 16)
            sp.wait_ge(stored, 16 * B)


class LayerNorm:

    STEPS = 2 * TILES

    def __init__(self, core, ctx, name="ln"):
        self.core = core
        self.stats = core.sbuf(ctx, f"{name}_stats", [P, TILES, 6])
        self.moments = core.sbuf(ctx, f"{name}_moments", [P, TILES, 2])
        self.rstd = core.sbuf(ctx, f"{name}_rstd", [P, TILES])
        self.padded = core.sbuf(ctx, f"{name}_padded", [P, TILES])
        self.steps = core.sem(f"{name}_steps")
        self.padded_ready = core.sem(f"{name}_padded_ready")
        self.scaled = core.sem(f"{name}_scaled")

    def moments_of(self, dve, it):
        before = it * self.STEPS
        for i in range(TILES):
            dve.bn_stats(self.stats[:, i, :], tile_at(self.core.x, it * TILES + i)).then_inc(self.steps, 1)
        wait_apart(self.core, dve, self.steps, before + TILES)
        for i in range(TILES):
            dve.bn_aggr(self.moments[:, i, :], self.stats[:, i, :]).then_inc(self.steps, 1)

    def rstd_of(self, pool, it):
        wait_apart(self.core, pool, self.steps, (it + 1) * self.STEPS)
        pool.tensor_scalar(self.padded[:], self.moments[:, :, 1], LN_EPS, None, ALU.add).then_inc(self.padded_ready, 1)
        pool.wait_ge(self.padded_ready, it + 1)
        pool.tensor_tensor(self.rstd[:], self.padded[:], self.core.minus_half[:, 0:TILES], ALU.pow).then_inc(self.scaled, 1)


def causal_stage(core, wq_t, wk_t, wv_t):
    nc, x, bank = core.nc, core.x, core.bank
    core.stage = "causal"
    scale = float(D) ** -0.5
    s_ = core.sem
    w_in, mask_made = s_("w_in"), s_("mask_made")
    normed, turned, ht_copied, projected, qkv_copied = (
        s_("normed"), s_("turned"), s_("ht_copied"), s_("projected"), s_("qkv_copied"))
    scored, masked, maxed, shifted, probs = s_("scored"), s_("masked"), s_("maxed"), s_("shifted"), s_("probs")
    p_turned, pt_copied, mixed, inverted, added = (
        s_("p_turned"), s_("pt_copied"), s_("mixed"), s_("inverted"), s_("added"))
    chunks = T // BANK
    groups = [(qt, g) for qt in range(TILES) for g in range(qt // 4 + 1)]
    NG = len(groups)
    with ExitStack() as ctx:
        sb = lambda name, shape, dtype=F32: core.sbuf(ctx, name, shape, dtype)
        ln = LayerNorm(core, ctx)
        wq, wk, wv = sb("wq", [P, D]), sb("wk", [P, D]), sb("wv", [P, D])
        above = sb("above", [P, P])
        h = sb("h", [P, TILES, D])
        h_t = sb("h_t", [P, T])
        q_t, k_t, v = sb("q_t", [P, T]), sb("k_t", [P, T]), sb("v", [P, TILES, D])
        top, shift, total, inverse = (sb("top", [P, TILES]), sb("shift", [P, TILES]), sb("total", [P, TILES]),
                                      sb("inverse", [P, TILES]))
        p, p_t = sb("p", [P, 2, T]), sb("p_t", [P, 2, T])
        with nc.Block() as block:

            @block.sync
            def _(sp):
                sp.dma_start(wq[:], wq_t).then_inc(w_in, 16)
                sp.dma_start(wk[:], wk_t).then_inc(w_in, 16)
                sp.dma_start(wv[:], wv_t).then_inc(w_in, 16)

            @block.gpsimd
            def _(pool):
                pool.memset(above[:], 0.0).then_inc(mask_made, 1)
                pool.wait_ge(mask_made, 1)
                pool.affine_select(out=above[:], in_=above[:], compare_op=ALU.is_ge, fill=MASKED, base=0,
                                   pattern=[[-1, P]], channel_multiplier=1).then_inc(mask_made, 1)
                with pool.Fori(0, B) as it:
                    ln.rstd_of(pool, it)

            @block.vector
            def _(dve):
                dve.wait_ge(mask_made, 2)

                def normalise(it):
                    dve.wait_ge(ln.scaled, it + 1)
                    wait_past(dve, turned, it * chunks)
                    for i in range(TILES):
                        dve.tensor_scalar(h[:, i, :], tile_at(x, it * TILES + i), ln.moments[:, i, 0:1],
                                          ln.rstd[:, i:i + 1], ALU.subtract, ALU.mult).then_inc(normed, 1)

                ln.moments_of(dve, 0)
                normalise(0)

                def turn(it, first, last_turn):
                    for c in range(chunks):
                        dve.wait_ge(projected, it * 6 + (3 + c))
                        dve.tensor_copy(k_t[:, c * BANK:(c + 1) * BANK], bank[:, 4 + c, :]).then_inc(qkv_copied, 1)
                    dve.wait_ge(projected, it * 6 + 6)
                    dve.tensor_copy(v[:, 4:8, :].rearrange("p i d -> p (i d)"), bank[:, 7, :]).then_inc(qkv_copied, 1)

                    def row_max(qt):
                        s = 2 * (qt % 2)
                        dve.wait_ge(scored, it * TILES + (qt + 1))
                        diag = bank[:, s + qt // 4, (qt % 4) * P:(qt % 4 + 1) * P]
                        dve.tensor_tensor(diag, diag, above[:], ALU.add).then_inc(masked, 1)
                        dve.wait_ge(masked, it * TILES + (qt + 1))
                        row = bank[:, s:s + 2, :].rearrange("p b n -> p (b n)")[:, 0:(qt + 1) * P]
                        dve.tensor_reduce(top[:, qt:qt + 1], row, AX, ALU.max).then_inc(maxed, 1)
                        dve.wait_ge(maxed, it * TILES + (qt + 1))
                        dve.tensor_scalar(shift[:, qt:qt + 1], top[:, qt:qt + 1], -scale, None,
                                          ALU.mult).then_inc(shifted, 1)

                    def copy_blocks(qt):
                        for n, (q, g) in enumerate(groups):
                            if q == qt:
                                w = min(4, qt + 1 - 4 * g)
                                dve.wait_ge(p_turned, it * NG + (n + 1))
                                dve.tensor_copy(p_t[:, qt % 2, g * BANK:g * BANK + w * P],
                                                bank[:, 4 + n % 2, 0:w * P]).then_inc(pt_copied, 1)

                    def finish(qt):
                        dve.wait_ge(probs, it * TILES + (qt + 1))
                        dve.reciprocal(inverse[:, qt:qt + 1], total[:, qt:qt + 1]).then_inc(inverted, 1)
                        dve.wait_ge(inverted, it * TILES + (qt + 1))
                        dve.wait_ge(mixed, it * TILES + (qt + 1))
                        row = tile_at(x, it * TILES + qt)
                        dve.scalar_tensor_tensor(row, bank[:, 6 + qt % 2, 0:D], inverse[:, qt:qt + 1], row,
                                                 ALU.mult, ALU.add).then_inc(added, 1)

                    row_max(0)
                    for qt in range(TILES):
                        if qt + 1 < TILES:
                            row_max(qt + 1)
                        if qt == 1 and not last_turn:
                            dve.wait_ge(normed, (it + 1) * TILES)
                            ln.moments_of(dve, it + 1)
                        if qt == 4 and not last_turn:
                            normalise(it + 1)
                        copy_blocks(qt)
                        if qt:
                            finish(qt - 1)
                    finish(TILES - 1)

                turns(dve, B, turn)

            @block.scalar
            def _(act):
                with act.Fori(0, B) as it:
                    for c in range(chunks):
                        act.wait_ge(turned, it * chunks + (c + 1))
                        act.activation(h_t[:, c * BANK:(c + 1) * BANK], bank[:, c, :], ACT.Copy).then_inc(ht_copied, 1)
                    for c in range(chunks):
                        act.wait_ge(projected, it * 6 + (1 + c))
                        act.activation(q_t[:, c * BANK:(c + 1) * BANK], bank[:, 2 + c, :],
                                       ACT.Copy).then_inc(qkv_copied, 1)
                    act.wait_ge(projected, it * 6 + 5)
                    act.activation(v[:, 0:4, :].rearrange("p i d -> p (i d)"), bank[:, 6, :],
                                   ACT.Copy).then_inc(qkv_copied, 1)
                    for qt in range(TILES):
                        s = 2 * (qt % 2)
                        act.wait_ge(shifted, it * TILES + (qt + 1))
                        if qt >= 2:
                            act.wait_ge(p_turned, it * NG + (1 + max(n for n, (q, _) in enumerate(groups)
                                                                     if q == qt - 2)))
                        row = bank[:, s:s + 2, :].rearrange("p b n -> p (b n)")[:, 0:(qt + 1) * P]
                        act.activation(p[:, qt % 2, 0:(qt + 1) * P], row, ACT.Exp, bias=shift[:, qt:qt + 1],
                                       scale=scale, accum_out=total[:, qt:qt + 1]).then_inc(probs, 1)

            @block.tensor
            def _(pe):
                pe.wait_ge(w_in, 48)
                with pe.Fori(0, B) as it:
                    for c in range(chunks):
                        pe.wait_ge(normed, it * TILES + 4 * (c + 1))
                        for i in range(4):
                            last = pe.transpose(bank[:, c, i * P:(i + 1) * P], h[:, 4 * c + i, :], core.ident[:])
                        last.then_inc(turned, 1)
                    pe.wait_ge(ht_copied, it * chunks + chunks)
                    for n, w in enumerate((wq, wk)):
                        for c in range(chunks):
                            pe.matmul(bank[:, 2 + 2 * n + c, :], w[:], h_t[:, c * BANK:(c + 1) * BANK],
                                      start=True, stop=True).then_inc(projected, 1)
                    pe.wait_ge(added, it * TILES)
                    for c in range(2):
                        for i in range(4):
                            t = 4 * c + i
                            last = pe.matmul(bank[:, 6 + c, i * P:(i + 1) * P], h_t[:, t * P:(t + 1) * P], wv[:],
                                             start=True, stop=True)
                        last.then_inc(projected, 1)
                    pe.wait_ge(qkv_copied, (it + 1) * 6)

                    def scores(qt):
                        s = 2 * (qt % 2)
                        if qt >= 2:
                            pe.wait_ge(probs, it * TILES + (qt - 1))
                        for lo in range(0, (qt + 1) * P, BANK):
                            n = min(BANK, (qt + 1) * P - lo)
                            last = pe.matmul(bank[:, s + lo // BANK, 0:n], q_t[:, qt * P:(qt + 1) * P],
                                             k_t[:, lo:lo + n], start=True, stop=True)
                        last.then_inc(scored, 1)

                    def turn_probs(qt):
                        pe.wait_ge(probs, it * TILES + (qt + 1))
                        for n, (q, g) in enumerate(groups):
                            if q != qt:
                                continue
                            if n >= 2:
                                pe.wait_ge(pt_copied, it * NG + (n - 1))
                            for kt in range(4 * g, min(4 * g + 4, qt + 1)):
                                last = pe.transpose(bank[:, 4 + n % 2, (kt - 4 * g) * P:(kt - 4 * g + 1) * P],
                                                    p[:, qt % 2, kt * P:(kt + 1) * P], core.ident[:])
                            last.then_inc(p_turned, 1)

                    def mix_values(qt):
                        if qt >= 2:
                            pe.wait_ge(added, it * TILES + (qt - 1))
                        for kt in range(qt + 1):
                            if kt % 4 == 0:
                                n = groups.index((qt, kt // 4))
                                pe.wait_ge(pt_copied, it * NG + (n + 1))
                            last = pe.matmul(bank[:, 6 + qt % 2, 0:D], p_t[:, qt % 2, kt * P:(kt + 1) * P],
                                             v[:, kt, :], start=(kt == 0), stop=(kt == qt))
                        last.then_inc(mixed, 1)

                    scores(0)
                    for qt in range(TILES):
                        if qt + 1 < TILES:
                            scores(qt + 1)
                        if qt:
                            mix_values(qt - 1)
                        turn_probs(qt)
                    mix_values(TILES - 1)


class Heads:

    GROUP = 4

    def __init__(self, core, ctx, name, heads):
        nc = core.nc
        self.core, self.name, self.heads = core, name, heads
        self.width = D // heads
        self.groups = heads // self.GROUP
        self.total = B * self.groups
        self.pairs = [3, 3, 3] if 9 * self.width + 2 <= P else [3, 2, 1]
        self.rows = sum(self.pairs) * self.width
        self.gw = self.GROUP * self.width
        shape = [self.total, self.GROUP, 3, self.width, T]
        self.q_parts = nc.dram_tensor(f"{name}_q_parts", shape, BF16, kind="Internal").ap()
        self.k_parts = nc.dram_tensor(f"{name}_k_parts", shape, BF16, kind="Internal").ap()
        core.stage = name
        self.values = core.sbuf(ctx, "values", [P, self.total, TILES, self.GROUP * 32])
        self.mixed = core.sbuf(ctx, "mixed", [P, self.total, TILES, self.gw])
        self.q_stack = core.sbuf(ctx, "q_stack", [self.rows + 2, 2, self.GROUP, T], BF16)
        self.k_stack = core.sbuf(ctx, "k_stack", [self.rows + 2, 2, self.GROUP, T], BF16)
        self.v = core.sbuf(ctx, "v", [P, 2, TILES, self.GROUP * 32])
        self.wo, self.wo_in = core.sbuf(ctx, "wo", [P, D]), core.sem("wo_in")
        self.qk_in = [core.sem("qk_in0"), core.sem("qk_in1")]
        self.parts_out = core.sem("parts_out")
        self.v_in = [core.sem("v_in0"), core.sem("v_in1")]
        self.LOADS = 3 + sum(self.pairs)

    def load(self, sp, n, k):
        at = 0
        for a, count in enumerate(self.pairs):
            end = at + count * self.width
            src = self.k_parts[bass.ds(n, 1), :, 0:count].rearrange("o j c e t -> (c e) (o j) t")
            sp.dma_start(self.k_stack[at:end, k], src).then_inc(self.qk_in[k], 16)
            src = self.q_parts[bass.ds(n, 1), :, a].rearrange("o j e t -> e (o j) t")
            for c in range(count):
                rows = slice(at + c * self.width, at + (c + 1) * self.width)
                sp.dma_start(self.q_stack[rows, k], src).then_inc(self.qk_in[k], 16)
            at = end
        sp.dma_start(self.v[:, k], self.values[:, bass.ds(n, 1)].rearrange("p o i c -> p (o i) c")).then_inc(
            self.v_in[k], 16)


def experts(masked, lo, hi):
    if not masked:
        return [(lo, hi, D)]
    return [(2 * e, 2 * e + 2, D >> e) for e in range(lo // 2, hi // 2)]


def project_stage(core, hd, w, masked):
    nc, x, bank = core.nc, core.x, core.bank
    core.stage = hd.name + "_p"
    s_ = core.sem
    w_in, v_set = s_("w_in"), s_("v_set")
    normed, residual = s_("normed"), s_("residual")
    turned, ht_copied, projected, qk_copied, v_copied = (
        s_("turned"), s_("ht_copied"), s_("projected"), s_("qk_copied"), s_("v_copied"))
    cut, ones_set, parts_out = s_("cut"), s_("ones_set"), hd.parts_out
    chunks = T // BANK
    NW = len(w) - 1
    with ExitStack() as ctx:
        sb = lambda name, shape, dtype=F32: core.sbuf(ctx, name, shape, dtype)
        ln = LayerNorm(core, ctx)
        wq, wk, wv = sb("wq", [P, D]), sb("wk", [P, D]), sb("wv", [P, D])
        out_bias = sb("out_bias", [P, D])
        if masked:
            q_bias, k_bias, norm_w, norm_b = (sb(n, [P, 1]) for n in ("q_bias", "k_bias", "norm_w", "norm_b"))
            v_bias = sb("v_bias", [P, D])
            second, both = sb("second", [P, TILES]), sb("both", [P, TILES])
            small = s_("small")
            first = sb("first", [P, TILES, D])
        h = sb("h", [P, TILES, D])
        h_t = sb("h_t", [P, T])
        q_t, k_t = sb("q_t", [P, T]), sb("k_t", [P, T])
        rest = sb("rest", [P, 2, T])
        parts = [sb("q_cut", [P, 3, T], BF16), sb("k_cut", [P, 3, T], BF16)]
        with nc.Block() as block:

            @block.sync
            def _(sp):
                for tile, source in ((wq, w["q"]), (wk, w["k"]), (wv, w["v"])):
                    sp.dma_start(tile[:], source).then_inc(w_in, 16)
                sp.dma_start(out_bias[:], w["out_bias"].partition_broadcast(P)).then_inc(w_in, 16)
                if masked:
                    sp.dma_start(v_bias[:], w["v_bias"].partition_broadcast(P)).then_inc(w_in, 16)
                    for tile, source in ((q_bias, "q_bias"), (k_bias, "k_bias"), (norm_w, "norm_w"),
                                         (norm_b, "norm_b")):
                        sp.dma_start(tile[:], w[source].rearrange("(d o) -> d o", o=1)).then_inc(w_in, 16)
                sp.dma_start(hd.wo[:], w["o"]).then_inc(hd.wo_in, 16)

                def store(it):
                    for n, dram in enumerate((hd.q_parts, hd.k_parts)):
                        sp.wait_ge(cut, it * 8 + 4 * (n + 1))
                        for part in range(3):
                            dst = dram[bass.ds(it * hd.groups, hd.groups), :, part].rearrange("g j e t -> (g j) e t")
                            sp.dma_start(dst, parts[n][:, part, :]).then_inc(parts_out, 16)

                store(0)
                sp.wait_ge(ones_set, 1)
                sp.wait_ge(parts_out, 16 * 6)
                sp.wait_ge(v_copied, 2 * hd.groups)
                for k in range(2):
                    hd.load(sp, k, k)
                with sp.Fori(1, B) as it:
                    store(it)

            @block.gpsimd
            def _(pool):
                def factors(it):
                    ln.rstd_of(pool, it)
                    if masked:
                        base = it * 5
                        pool.wait_ge(ln.scaled, it + 1)
                        pool.tensor_tensor(second[:], ln.rstd[:], ln.rstd[:], ALU.mult).then_inc(small, 1)
                        pool.wait_ge(small, base + 1)
                        pool.tensor_tensor(second[:], second[:], ln.moments[:, :, 1], ALU.mult).then_inc(small, 1)
                        wait_apart(core, pool, small, base + 2)
                        pool.tensor_scalar(second[:], second[:], LN_EPS, None, ALU.add).then_inc(small, 1)
                        pool.wait_ge(small, base + 3)
                        pool.tensor_tensor(second[:], second[:], core.minus_half[:, 0:TILES], ALU.pow).then_inc(small, 1)
                        pool.wait_ge(small, base + 4)
                        pool.tensor_tensor(both[:], second[:], ln.rstd[:], ALU.mult).then_inc(small, 1)

                def residuals(it):
                    pool.wait_ge(normed, (it + 1) * TILES * (2 if masked else 1))
                    for i in range(TILES):
                        row = tile_at(x, it * TILES + i)
                        if masked:
                            pool.tensor_tensor(row, row, first[:, i, :], ALU.add).then_inc(residual, 1)
                    if masked:
                        wait_apart(core, pool, residual, it * 2 * TILES + TILES)
                    for i in range(TILES):
                        m = experts(masked, 0, TILES)[i // 2][2] if masked else D
                        row = tile_at(x, it * TILES + i)[:, 0:m]
                        pool.tensor_tensor(row, row, out_bias[:, 0:m], ALU.add).then_inc(residual, 1)

                per_sequence = TILES * (2 if masked else 1)
                factors(0)
                wait_apart(core, pool, normed, per_sequence)
                factors(1)
                pool.wait_ge(w_in, 16 * NW)
                residuals(0)
                values = hd.values[:].rearrange("p n i c -> p (n i) c")
                pool.memset(values, 0.0).then_inc(v_set, 1)
                pool.wait_ge(v_set, 1)
                ones = hd.values[:].rearrange("p n i (j r) -> p (n i j) r", r=32)[:, :, hd.width:hd.width + 1]
                pool.memset(ones, 1.0).then_inc(v_set, 1)
                pool.wait_ge(v_set, 2)
                ones_rows = hd.k_stack[hd.rows // 32 * 32:hd.rows + 2, :, :, :]
                pool.memset(ones_rows.rearrange("r k j t -> r (k j t)"), 1.0).then_inc(ones_set, 1)
                pool.wait_ge(ones_set, 1)
                with pool.Fori(1, B - 1) as it:
                    residuals(it)
                    factors(it + 1)
                residuals(B - 1)
                pool.wait_ge(residual, B * TILES * (2 if masked else 1))

            @block.vector
            def _(dve):
                def normalise(it):
                    if masked:
                        dve.wait_ge(small, (it + 1) * 5)
                        wait_past(dve, residual, it * 2 * TILES)
                    else:
                        dve.wait_ge(ln.scaled, it + 1)
                    wait_past(dve, turned, it * chunks)
                    rstd = both if masked else ln.rstd
                    for i in range(TILES):
                        dve.tensor_scalar(h[:, i, :], tile_at(x, it * TILES + i), ln.moments[:, i, 0:1],
                                          rstd[:, i:i + 1], ALU.subtract, ALU.mult).then_inc(normed, 1)
                    if masked:
                        for i in range(TILES):
                            dve.tensor_scalar(first[:, i, :], tile_at(x, it * TILES + i), ln.moments[:, i, 0:1],
                                              ln.rstd[:, i:i + 1], ALU.subtract, ALU.mult).then_inc(normed, 1)

                def cut_parts(it, n, whole):
                    dve.wait_ge(qk_copied, it * 4 + 2 * (n + 1))
                    wait_past(dve, parts_out, it * 96)
                    dve.tensor_copy(parts[n][:, 0, :], whole[:]).then_inc(cut, 1)
                    dve.wait_ge(cut, it * 8 + 4 * n + 1)
                    dve.tensor_tensor(rest[:, n, :], whole[:], parts[n][:, 0, :], ALU.subtract).then_inc(cut, 1)
                    dve.wait_ge(cut, it * 8 + 4 * n + 2)
                    dve.tensor_copy(parts[n][:, 1, :], rest[:, n, :]).then_inc(cut, 1)
                    dve.wait_ge(cut, it * 8 + 4 * n + 3)
                    dve.tensor_tensor(parts[n][:, 2, :], rest[:, n, :], parts[n][:, 1, :],
                                      ALU.subtract).then_inc(cut, 1)

                def store_values(it):
                    for c in range(2):
                        dve.wait_ge(projected, it * 6 + (5 + c))
                        for g in range(hd.groups):
                            dst = hd.values[:, bass.ds(it * hd.groups + g, 1), 4 * c:4 * c + 4, :].rearrange(
                                "p o i (j r) -> p (o i) j r", r=32)[:, :, :, 0:hd.width]
                            src = bank[:, 6 + c, :].rearrange("p (i g j e) -> p g i j e", g=hd.groups, j=hd.GROUP,
                                                              e=hd.width)[:, g]
                            if masked:
                                vb = v_bias[:, g * hd.gw:(g + 1) * hd.gw].rearrange("p (j e) -> p j e", e=hd.width)
                                vb = vb.unsqueeze(1).broadcast_to([P, 4, hd.GROUP, hd.width])
                                dve.tensor_tensor(dst, src, vb, ALU.add).then_inc(v_copied, 1)
                            else:
                                dve.tensor_copy(dst, src).then_inc(v_copied, 1)

                def turn(it, first_turn, last_turn):
                    if first_turn:
                        ln.moments_of(dve, 0)
                        normalise(0)
                    if not last_turn:
                        dve.wait_ge(normed, (it + 1) * TILES * (2 if masked else 1))
                        ln.moments_of(dve, it + 1)
                    cut_parts(it, 0, q_t)
                    if not last_turn:
                        normalise(it + 1)
                    cut_parts(it, 1, k_t)
                    if first_turn:
                        dve.wait_ge(w_in, 16 * NW)
                        dve.wait_ge(v_set, 2)
                    store_values(it)

                turns(dve, B, turn)

            @block.scalar
            def _(act):
                act.wait_ge(w_in, 16 * NW)
                with act.Fori(0, B) as it:
                    act.wait_ge(projected, it * 6)
                    for c in range(chunks):
                        act.wait_ge(turned, it * chunks + (c + 1))
                        dst = h_t[:, c * BANK:(c + 1) * BANK]
                        if masked:
                            act.activation(dst, bank[:, c, :], ACT.Identity, bias=norm_b[:],
                                           scale=norm_w[:]).then_inc(ht_copied, 1)
                        else:
                            act.activation(dst, bank[:, c, :], ACT.Copy).then_inc(ht_copied, 1)
                    act.wait_ge(cut, it * 8)
                    for n, whole in enumerate((q_t, k_t)):
                        for c in range(chunks):
                            act.wait_ge(projected, it * 6 + (2 * n + c + 1))
                            dst = whole[:, c * BANK:(c + 1) * BANK]
                            if masked:
                                act.activation(dst, bank[:, 2 + 2 * n + c, :], ACT.Identity,
                                               bias=(q_bias, k_bias)[n][:]).then_inc(qk_copied, 1)
                            else:
                                act.activation(dst, bank[:, 2 + 2 * n + c, :], ACT.Copy).then_inc(qk_copied, 1)

            @block.tensor
            def _(pe):
                pe.wait_ge(w_in, 16 * NW)
                with pe.Fori(0, B) as it:
                    for c in range(chunks):
                        if masked:
                            pe.wait_ge(normed, it * 2 * TILES + 4 * (c + 1))
                        else:
                            pe.wait_ge(normed, it * TILES + 4 * (c + 1))
                        for i in range(4):
                            last = pe.transpose(bank[:, c, i * P:(i + 1) * P], h[:, 4 * c + i, :], core.ident[:])
                        last.then_inc(turned, 1)
                    pe.wait_ge(ht_copied, it * chunks + chunks)
                    pe.wait_ge(qk_copied, it * 4)
                    for n, weight in enumerate((wq, wk)):
                        for c in range(chunks):
                            for lo, hi, m in experts(masked, 4 * c, 4 * c + 4):
                                last = pe.matmul(bank[:, 2 + 2 * n + c, (lo - 4 * c) * P:(hi - 4 * c) * P],
                                                 weight[0:m, :], h_t[0:m, lo * P:hi * P], start=True, stop=True)
                            last.then_inc(projected, 1)
                    pe.wait_ge(v_copied, it * 2 * hd.groups)
                    for c in range(2):
                        for lo, hi, m in experts(masked, 4 * c, 4 * c + 4):
                            for t in range(lo, hi):
                                last = pe.matmul(bank[:, 6 + c, (t - 4 * c) * P:(t - 4 * c + 1) * P],
                                                 h_t[0:m, t * P:(t + 1) * P], wv[0:m, :], start=True, stop=True)
                        last.then_inc(projected, 1)


def attend_stage(core, hd):
    nc, bank = core.nc, core.bank
    core.stage = hd.name + "_a"
    s_ = core.sem
    G, R, W, T2 = hd.GROUP, hd.rows, hd.width, T // 2
    scale = float(D) ** -0.5
    LOADS, qk_in, v_in = hd.LOADS, hd.qk_in, hd.v_in
    q_stack, k_stack, v = hd.q_stack, hd.k_stack, hd.v
    scored, maxed, top_made, high_made, shifts_made = (
        s_("scored"), s_("maxed"), s_("top_made"), s_("high_made"), s_("shifts_made"))
    shift_turned, shift_copied, shift_in = s_("shift_turned"), s_("shift_copied"), s_("shift_in")
    shifted, probs, mixed, mix_copied, mix_turned, inverted, written = (
        s_("shifted"), s_("probs"), s_("mixed"), s_("mix_copied"), s_("mix_turned"), s_("inverted"), s_("written"))
    RING, ITEMS = 3, 32
    ST, SC, MIX, MISC = 0, 3, 6, 7

    def wait_for_bank(engine, done, u, n):
        last = n - RING if n >= RING else max(range(n, ITEMS, RING)) - ITEMS
        wait_past(engine, done, u * ITEMS + (last + 1))

    with ExitStack() as ctx:
        sb = lambda name, shape, dtype=F32: core.sbuf(ctx, name, shape, dtype)
        p = sb("p", [P, 2, G, T2])
        halves = sb("halves", [P, 16, 2])
        top = sb("top", [P, 4, G])
        shift = sb("shift", [P, 4, 2, G], BF16)
        shift_rows = sb("shift_rows", [8, 2, T2], BF16)
        mix = sb("mix", [P, T2])
        inverse = sb("inverse", [P, 4, G])

        with nc.Block() as block:

            @block.sync
            def _(sp):
                def shift_load(u, ui):
                    k, qc = ui % 4 // 2, ui % 2
                    sp.wait_ge(shift_copied, u + 1)
                    for part in range(2):
                        sp.dma_start(q_stack[R + part:R + part + 1, k, :, qc * T2:(qc + 1) * T2],
                                     shift_rows[part * G:(part + 1) * G, qc, :]).then_inc(shift_in, 16)

                shift_load(0, 0)
                sp.wait_ge(hd.parts_out, 16 * 6 * B)

                def turn(it, first, last):
                    for ui in range(4):
                        u, k = it * 4 + ui, ui // 2
                        if ui % 2 == 0 and not (first and k == 0) and not (last and k == 1):
                            sp.wait_ge(mixed, u * TILES)
                            hd.load(sp, it * 2 + k + 1, (k + 1) % 2)
                        if not (last and ui == 3):
                            shift_load(u + 1, ui + 1)

                turns(sp, hd.total // 2, turn)

            @block.vector
            def _(dve):
                def maximum(u, n):
                    dve.wait_ge(scored, u * ITEMS + (n + 1))
                    dve.tensor_reduce(halves[:, n // 2, n % 2:n % 2 + 1], bank[:, SC + n % RING, :], AX,
                                      ALU.max).then_inc(maxed, 1)

                def shifts(u):
                    dve.wait_ge(maxed, (u + 1) * ITEMS)
                    dve.wait_ge(shift_turned, u)
                    dve.tensor_tensor(top[:].rearrange("p i j -> p j i"),
                                      halves[:, :, 0].rearrange("p (j i) -> p j i", j=G),
                                      halves[:, :, 1].rearrange("p (j i) -> p j i", j=G), ALU.max).then_inc(top_made, 1)
                    dve.wait_ge(top_made, u + 1)
                    dve.tensor_scalar(shift[:, :, 0, :], top[:], -1.0, None, ALU.mult).then_inc(high_made, 1)
                    dve.wait_ge(high_made, u + 1)
                    dve.scalar_tensor_tensor(shift[:, :, 1, :], top[:], -1.0, shift[:, :, 0, :], ALU.mult,
                                             ALU.subtract).then_inc(shifts_made, 1)

                def write_mixed(u, ui, it):
                    rows = bank[:, MISC, :].rearrange("p (i j r) -> p i j r", i=4, j=G)
                    dve.wait_ge(mix_turned, u + 1)
                    dve.reciprocal(inverse[:], rows[:, :, :, W]).then_inc(inverted, 1)
                    dve.wait_ge(inverted, u + 1)
                    dst = hd.mixed[:, bass.ds(it * 2 + ui // 2, 1), ui % 2 * 4:ui % 2 * 4 + 4, :].rearrange(
                        "p o i (j e) -> p (o i) j e", e=W)
                    dve.tensor_tensor(dst, rows[:, :, :, 0:W], inverse[:].unsqueeze(3).broadcast_to([P, 4, G, W]),
                                      ALU.mult).then_inc(written, 1)

                for n in range(ITEMS):
                    maximum(0, n)
                shifts(0)
                for n in range(ITEMS // 2):
                    maximum(1, n)

                def turn(it, first, last):
                    for ui in range(4):
                        u = it * 4 + ui
                        for kt in range(TILES):
                            for n in range(4 * kt, 4 * kt + 4):
                                if kt < 4 and not (last and ui == 3):
                                    maximum(u + 1, n + ITEMS // 2)
                                if kt >= 4 and not (last and ui >= 2):
                                    maximum(u + 2, n - ITEMS // 2)
                            if kt == 3 and not (last and ui == 3):
                                shifts(u + 1)
                            if kt == 2 and not (first and ui == 0):
                                write_mixed(u - 1, (ui - 1) % 4, it if ui else it - 1)

                turns(dve, hd.total // 2, turn)
                write_mixed(2 * hd.total - 1, 3, hd.total // 2 - 1)

            @block.scalar
            def _(act):
                def exponential(u, kt, j):
                    n = 4 * kt + j
                    act.wait_ge(shifted, u * ITEMS + (n + 1))
                    if j == 0:
                        wait_past(act, mixed, u * TILES + (kt - 1))
                    act.activation(p[:, kt % 2, j, :], bank[:, ST + n % RING, :], ACT.Exp,
                                   scale=scale).then_inc(probs, 1)

                def copy_shifts(u, ui):
                    act.wait_ge(shift_turned, u + 1)
                    if not (isinstance(u, int) and u < 2):
                        act.wait_ge(shift_in, (u - 1) * 32)
                    act.activation(shift_rows[:, ui % 2, :], bank[0:8, MISC, :], ACT.Copy).then_inc(shift_copied, 1)

                def copy_mix(u):
                    act.wait_ge(mixed, (u + 1) * TILES)
                    if not (isinstance(u, int) and u < 1):
                        act.wait_ge(mix_turned, u)
                    act.activation(mix[:], bank[:, MIX, :], ACT.Copy).then_inc(mix_copied, 1)

                copy_shifts(0, 0)

                def turn(it, first, last):
                    for ui in range(4):
                        u = it * 4 + ui
                        for kt in range(TILES):
                            for j in range(G):
                                exponential(u, kt, j)
                                if kt == 0 and j == 3 and not (first and ui == 0):
                                    copy_mix(u - 1)
                                if kt == 5 and j == 3 and not (last and ui == 3):
                                    copy_shifts(u + 1, ui + 1)

                turns(act, hd.total // 2, turn)
                copy_mix(2 * hd.total - 1)

            @block.tensor
            def _(pe):
                def scores(u, n, k, qc):
                    j, i, half = n // 8, n // 2 % 4, n % 2
                    at = qc * T2 + i * P
                    wait_for_bank(pe, maxed, u, n)
                    pe.matmul(bank[:, SC + n % RING, :], q_stack[0:R, k, j, at:at + P],
                              k_stack[0:R, k, j, half * BANK:(half + 1) * BANK],
                              start=True, stop=True).then_inc(scored, 1)

                def turn_shifts(u):
                    pe.wait_ge(shifts_made, u + 1)
                    if not (isinstance(u, int) and u < 2):
                        pe.wait_ge(written, u - 1)
                    for i in range(4):
                        last = pe.matmul(bank[0:8, MISC, i * P:(i + 1) * P], shift[:, i].rearrange("p s j -> p (s j)"),
                                         core.ident_bf[:], start=True, stop=True)
                    last.then_inc(shift_turned, 1)

                def shifted_scores(u, kt, k, qc, j):
                    n = 4 * kt + j
                    wait_for_bank(pe, probs, u, n)
                    pe.matmul(bank[:, ST + n % RING, :], k_stack[:, k, j, kt * P:(kt + 1) * P],
                              q_stack[:, k, j, qc * T2:(qc + 1) * T2], start=True, stop=True).then_inc(shifted, 1)

                def mix_values(s, kt, k):
                    pe.wait_ge(probs, s * G + G)
                    for j in range(G):
                        last = pe.matmul(bank[32 * j:32 * j + 32, MIX, :], v[:, k, kt, 32 * j:32 * j + 32],
                                         p[:, kt % 2, j, :], start=(kt == 0), stop=(kt == TILES - 1))
                    last.then_inc(mixed, 1)

                def turn_mix(u):
                    pe.wait_ge(mix_copied, u + 1)
                    pe.wait_ge(shift_copied, u + 2)
                    for i in range(4):
                        last = pe.transpose(bank[:, MISC, i * P:(i + 1) * P], mix[:, i * P:(i + 1) * P], core.ident[:])
                    last.then_inc(mix_turned, 1)

                pe.wait_ge(qk_in[0], 16 * LOADS)
                for n in range(ITEMS):
                    scores(0, n, 0, 0)
                turn_shifts(0)
                for n in range(ITEMS // 2):
                    scores(1, n, 0, 1)
                pe.wait_ge(shift_in, 32)
                for j in range(RING):
                    shifted_scores(0, 0, 0, 0, j)

                def turn(it, first, last):
                    for ui in range(4):
                        u, k, qc = it * 4 + ui, ui // 2, ui % 2
                        for kt in range(TILES):
                            s = u * TILES + kt
                            end = last and ui == 3
                            if kt == 4 and qc == 0 and not (last and k == 1):
                                pe.wait_ge(qk_in[(k + 1) % 2], (it + (1 + k)) * 16 * LOADS)
                            for j in range(G):
                                n = 4 * kt + j + RING
                                if n < ITEMS:
                                    shifted_scores(u, n // 4, k, qc, n % 4)
                                elif not end:
                                    if n == ITEMS:
                                        pe.wait_ge(shift_in, (u + 2) * 32)
                                    shifted_scores(u + 1, 0, (ui + 1) % 4 // 2, (ui + 1) % 2, n - ITEMS)
                                if kt < 4 and not end:
                                    scores(u + 1, 4 * kt + j + ITEMS // 2, (ui + 1) % 4 // 2, (ui + 1) % 2)
                                if kt >= 4 and not (last and ui >= 2):
                                    scores(u + 2, 4 * kt + j - ITEMS // 2, (ui + 2) % 4 // 2, (ui + 2) % 2)
                            if kt == 0:
                                if qc == 0:
                                    pe.wait_ge(v_in[k], (it + 1) * 16)
                                if not (first and ui == 0):
                                    pe.wait_ge(mix_copied, u)
                            mix_values(s, kt, k)
                            if kt == 1 and not (first and ui == 0):
                                turn_mix(u - 1)
                            if kt == 4 and not end:
                                turn_shifts(u + 1)

                turns(pe, hd.total // 2, turn)
                pe.wait_ge(mix_copied, 2 * hd.total)
                pe.wait_ge(written, 2 * hd.total - 1)
                for i in range(4):
                    last = pe.transpose(bank[:, MISC, i * P:(i + 1) * P], mix[:, i * P:(i + 1) * P], core.ident[:])
                last.then_inc(mix_turned, 1)


def turns(engine, count, turn):
    turn(0, True, False)
    with engine.Fori(1, count - 1) as it:
        turn(it, False, False)
    turn(count - 1, False, True)


def output_stage(core, hd, masked):
    nc, x, bank = core.nc, core.x, core.bank
    core.stage = hd.name + "_o"
    s_ = core.sem
    wo = hd.wo
    staged, turned, copied, projected, added = (
        s_("staged"), s_("turned"), s_("copied"), s_("projected"), s_("added"))
    with ExitStack() as ctx:
        sb = lambda name, shape, dtype=F32: core.sbuf(ctx, name, shape, dtype)
        m_, m_t = sb("m", [P, TILES, D]), sb("m_t", [P, T])
        with nc.Block() as block:

            @block.vector
            def _(dve):
                with dve.Fori(0, B) as it:
                    dve.wait_ge(turned, it * 2)
                    for g in range(hd.groups):
                        src = hd.mixed[:, bass.ds(it * hd.groups + g, 1)].rearrange("p o i c -> p (o i) c")
                        dve.tensor_copy(m_[:, :, g * hd.gw:(g + 1) * hd.gw], src).then_inc(staged, 1)
                    for c in range(2):
                        dve.wait_ge(projected, it * 2 + (c + 1))
                        for lo, hi, m in experts(masked, 4 * c, 4 * c + 4):
                            row = x[:, bass.ds(it * TILES + lo, hi - lo), 0:m]
                            src = bank[:, 4 + c, (lo - 4 * c) * P:(hi - 4 * c) * P].rearrange(
                                "p (i d) -> p i d", d=D)[:, :, 0:m]
                            dve.tensor_tensor(row, row, src, ALU.add).then_inc(added, 1)

            @block.scalar
            def _(act):
                with act.Fori(0, B) as it:
                    for c in range(2):
                        act.wait_ge(turned, it * 2 + (c + 1))
                        act.wait_ge(projected, it * 2)
                        act.activation(m_t[:, c * BANK:(c + 1) * BANK], bank[:, c, :], ACT.Copy).then_inc(copied, 1)

            @block.tensor
            def _(pe):
                pe.wait_ge(hd.wo_in, 16)
                with pe.Fori(0, B) as it:
                    pe.wait_ge(staged, (it + 1) * hd.groups)
                    for c in range(2):
                        for i in range(4):
                            last = pe.transpose(bank[:, c, i * P:(i + 1) * P], m_[:, 4 * c + i, :], core.ident[:])
                        last.then_inc(turned, 1)
                    pe.wait_ge(added, it * len(experts(masked, 0, TILES)) * (1 if masked else 2))
                    for c in range(2):
                        pe.wait_ge(copied, it * 2 + (c + 1))
                        for lo, hi, m in experts(masked, 4 * c, 4 * c + 4):
                            for t in range(lo, hi):
                                last = pe.matmul(bank[:, 4 + c, (t - 4 * c) * P:(t - 4 * c) * P + m],
                                                 m_t[0:m, t * P:(t + 1) * P], wo[0:m, 0:m], start=True, stop=True)
                        last.then_inc(projected, 1)


def heads_layer(core, name, heads, w, masked):
    with ExitStack() as ctx:
        hd = Heads(core, ctx, name, heads)
        project_stage(core, hd, w, masked)
        attend_stage(core, hd)
        output_stage(core, hd, masked)



class Front:

    def __init__(self, core, ctx, second_eps=None, spare=0):
        self.core, self.second_eps = core, second_eps
        self.ln = LayerNorm(core, ctx)
        self.h = core.sbuf(ctx, "h", [P, TILES, D + spare])
        self.h_t = core.sbuf(ctx, "h_t", [P, T])
        self.normed, self.turned, self.copied = core.sem("normed"), core.sem("turned"), core.sem("ht_copied")
        if second_eps is not None:
            self.second, self.both = core.sbuf(ctx, "second", [P, TILES]), core.sbuf(ctx, "both", [P, TILES])
            self.small = core.sem("small")

    def on_vector(self, dve, it):
        self.ln.moments_of(dve, it)
        self.normalise(dve, it)

    def normalise(self, dve, it):
        ln = self.ln
        if self.second_eps is None:
            dve.wait_ge(ln.scaled, it + 1)
            rstd = ln.rstd
        else:
            dve.wait_ge(self.small, (it + 1) * 5)
            rstd = self.both
        dve.wait_ge(self.turned, it * 2)
        for i in range(TILES):
            dve.tensor_scalar(self.h[:, i, 0:D], tile_at(self.core.x, it * TILES + i), ln.moments[:, i, 0:1],
                              rstd[:, i:i + 1], ALU.subtract, ALU.mult).then_inc(self.normed, 1)

    def on_gpsimd(self, pool, it):
        ln = self.ln
        ln.rstd_of(pool, it)
        if self.second_eps is None:
            return
        second, small, base = self.second, self.small, it * 5
        pool.wait_ge(ln.scaled, it + 1)
        pool.tensor_tensor(second[:], ln.rstd[:], ln.rstd[:], ALU.mult).then_inc(small, 1)
        pool.wait_ge(small, base + 1)
        pool.tensor_tensor(second[:], second[:], ln.moments[:, :, 1], ALU.mult).then_inc(small, 1)
        wait_apart(self.core, pool, small, base + 2)
        pool.tensor_scalar(second[:], second[:], self.second_eps, None, ALU.add).then_inc(small, 1)
        pool.wait_ge(small, base + 3)
        pool.tensor_tensor(second[:], second[:], self.core.minus_half[:, 0:TILES], ALU.pow).then_inc(small, 1)
        pool.wait_ge(small, base + 4)
        pool.wait_ge(self.normed, it * TILES)
        pool.tensor_tensor(self.both[:], second[:], ln.rstd[:], ALU.mult).then_inc(small, 1)

    def on_tensor(self, pe, it):
        for c in range(2):
            pe.wait_ge(self.normed, it * TILES + 4 * (c + 1))
            pe.wait_ge(self.copied, it * 2)
            for i in range(4):
                last = pe.transpose(self.core.bank[:, c, i * P:(i + 1) * P], self.h[:, 4 * c + i, 0:D],
                                    self.core.ident[:])
            last.then_inc(self.turned, 1)

    def on_scalar(self, act, it):
        for c in range(2):
            act.wait_ge(self.turned, it * 2 + (c + 1))
            act.activation(self.h_t[:, c * BANK:(c + 1) * BANK], self.core.bank[:, c, :],
                           ACT.Copy).then_inc(self.copied, 1)


def kernel_attention_stage(core, w):
    nc, x, bank = core.nc, core.x, core.bank
    core.stage = "lin"
    s_ = core.sem
    H, DH, F, HT = 16, 64, 32, 4
    w_in, filled, made = s_("w_in"), s_("filled"), s_("made")
    prepared, prep_copied = s_("prepared"), s_("prep_copied")
    featured, q_ready, biased, k_ready = s_("featured"), s_("q_ready"), s_("biased"), s_("k_ready")
    summed, sum_copied, blocks_made, headed, head_ready = (
        s_("summed"), s_("sum_copied"), s_("blocks_made"), s_("headed"), s_("head_ready"))
    divided, den_added, inverted, inv_turned, inv_copied, spread, q_scaled = (
        s_("divided"), s_("den_added"), s_("inverted"), s_("inv_turned"), s_("inv_copied"), s_("spread"), s_("q_scaled"))
    projected, added, residual, tiles_added = s_("projected"), s_("added"), s_("residual"), s_("tiles_added")
    with ExitStack() as ctx:
        sb = lambda name, shape, dtype=F32: core.sbuf(ctx, name, shape, dtype)
        front = Front(core, ctx, spare=1)
        wq, wk, wv, wo = (sb(n, [DH, H, D]) for n in ("wq", "wk", "wv", "wo"))
        fq, fk = sb("fq", [DH, F]), sb("fk", [DH, F])
        bq, bk, bv = sb("bq", [DH, H]), sb("bk", [DH, H]), sb("bv", [DH, H])
        out_bias = sb("out_bias", [P, D])
        wide_bias = sb("wide_bias", [DH, H, P])
        fold_q, fold_k, bias_k = sb("fold_q", [P, H * F]), sb("fold_k", [P, H * F]), sb("bias_k", [P, H * F])
        bias_q = sb("bias_q", [P, HT])
        fold_v, bias_v = sb("fold_v", [P, H, D]), sb("bias_v", [P, HT, D])
        ones = sb("ones", [P, 1])
        own = sb("own", [P, 4])
        spreads = sb("spreads", [P, P, F])
        q_f, k_f, k_raw = sb("q_f", [P, HT, T]), sb("k_f", [P, TILES, H * F]), sb("k_raw", [P, 2, H * F])
        sums, key_sums, blocks = sb("sums", [P, H * F]), sb("key_sums", [P, HT]), sb("blocks", [P, HT, 4])
        k_total = sb("k_total", [P, H * F])
        head = sb("head", [P, HT, D])
        den, inverse, inverse_t = sb("den", [P, P]), sb("inverse", [P, P]), sb("inverse_t", [P, P])
        with nc.Block() as block:

            @block.sync
            def _(sp):
                for tile, source in ((wq, "q"), (wk, "k"), (wv, "v"), (wo, "o")):
                    sp.dma_start(tile[:], w[source].rearrange("(h e) d -> e h d", e=DH)).then_inc(w_in, 16)
                for tile, source in ((fq, "fq"), (fk, "fk"), (bq, "bq"), (bk, "bk"), (bv, "bv")):
                    sp.dma_start(tile[:], w[source]).then_inc(w_in, 16)
                sp.dma_start(out_bias[:], w["out_bias"].partition_broadcast(P)).then_inc(w_in, 16)

            @block.gpsimd
            def _(pool):
                pool.memset(ones[:], 1.0).then_inc(filled, 1)
                pool.memset(front.h[:, :, D:D + 1], 1.0).then_inc(filled, 1)
                pool.memset(own[:], 1.0).then_inc(filled, 1)
                pool.wait_ge(filled, 3)
                pool.affine_select(out=own[:], in_=own[:], compare_op=ALU.is_ge, fill=0.0, base=0,
                                   pattern=[[-F, 4]], channel_multiplier=1).then_inc(filled, 1)
                pool.wait_ge(filled, 4)
                pool.affine_select(out=own[:], in_=own[:], compare_op=ALU.is_ge, fill=0.0, base=F - 1,
                                   pattern=[[F, 4]], channel_multiplier=-1).then_inc(filled, 1)
                front.on_gpsimd(pool, 0)
                pool.wait_ge(w_in, 160)

                def turn(it, first, last):
                    if not last:
                        front.on_gpsimd(pool, it + 1)
                    pool.wait_ge(front.normed, (it + 1) * TILES)
                    for i in range(TILES):
                        row = tile_at(x, it * TILES + i)
                        pool.tensor_tensor(row, row, out_bias[:], ALU.add).then_inc(residual, 1)

                turns(pool, B, turn)

            @block.vector
            def _(dve):
                dve.tensor_copy(spreads[:], core.ident[:].unsqueeze(2).broadcast_to([P, P, F])).then_inc(made, 1)
                front.on_vector(dve, 0)
                dve.wait_ge(w_in, 160)
                dve.tensor_copy(wide_bias[:], bk[:].unsqueeze(2).broadcast_to([DH, H, P])).then_inc(made, 1)
                for n, (dst, b) in enumerate(((fold_q[:], 0), (fold_k[:], 1), (bias_k[:], 2), (bias_q[:], 3))):
                    dve.wait_ge(prepared, n + 1)
                    src = bank[:, b, 0:HT] if b == 3 else bank[:, b, :]
                    dve.tensor_copy(dst, src).then_inc(prep_copied, 1)
                dve.tensor_copy(wide_bias[:], bv[:].unsqueeze(2).broadcast_to([DH, H, P])).then_inc(made, 1)
                dve.wait_ge(prepared, 5)
                dve.tensor_copy(fold_v[:].rearrange("p h d -> p (h d)"),
                                bank[:, 4:8, :].rearrange("p b n -> p (b n)")).then_inc(prep_copied, 1)
                dve.wait_ge(prepared, 6)
                dve.tensor_copy(bias_v[:].rearrange("p h d -> p (h d)"), bank[:, 0, :]).then_inc(prep_copied, 1)
                def add_tile(it, i):
                    n = it * (TILES - 1) + (i - 1)
                    dve.wait_ge(k_ready, it * TILES + (i + 1))
                    if i == 1:
                        wait_past(dve, summed, it * 2)
                    else:
                        dve.wait_ge(tiles_added, n)
                    dve.tensor_tensor(k_total[:], k_f[:, 0, :] if i == 1 else k_total[:], k_f[:, i, :],
                                      ALU.add).then_inc(tiles_added, 1)

                def turn(it, first, last):
                    for i in range(TILES):
                        dve.wait_ge(featured, it * 16 + (8 + i + 1))
                        if i >= 2:
                            dve.wait_ge(k_ready, it * TILES + (i - 1))
                        dve.tensor_tensor(k_raw[:, i % 2, :], bank[:, 4 + i % 2, :], bias_k[:],
                                          ALU.add).then_inc(biased, 1)
                        if i >= 3:
                            add_tile(it, i - 2)
                    add_tile(it, TILES - 2)
                    add_tile(it, TILES - 1)
                    dve.wait_ge(summed, it * 2 + 1)
                    dve.tensor_copy(sums[:], bank[:, 6, :]).then_inc(sum_copied, 1)
                    dve.wait_ge(summed, it * 2 + 2)
                    dve.tensor_copy(key_sums[:], bank[:, 7, 0:HT]).then_inc(sum_copied, 1)
                    dve.wait_ge(sum_copied, it * 2 + 2)
                    dve.tensor_tensor(blocks[:], key_sums[:].unsqueeze(2).broadcast_to([P, HT, 4]),
                                      own[:].unsqueeze(1).broadcast_to([P, HT, 4]), ALU.mult).then_inc(blocks_made, 1)
                    dve.wait_ge(headed, it + 1)
                    for t in range(HT):
                        dve.scalar_tensor_tensor(head[:, t, :], bias_v[:, t, :], key_sums[:, t:t + 1],
                                                 bank[:, 0, t * D:(t + 1) * D], ALU.mult,
                                                 ALU.add).then_inc(head_ready, 1)
                    if not last:
                        front.on_vector(dve, it + 1)
                    dve.wait_ge(divided, it + 1)
                    dve.tensor_scalar(den[:], bank[:, 1, 0:P], 1e-6, None, ALU.add).then_inc(den_added, 1)
                    dve.wait_ge(den_added, it + 1)
                    dve.reciprocal(inverse[:], den[:]).then_inc(inverted, 1)
                    dve.wait_ge(inv_turned, it + 1)
                    dve.tensor_copy(inverse_t[:], bank[:, 1, P:2 * P]).then_inc(inv_copied, 1)
                    for t in range(HT):
                        for c in range(2):
                            n = 2 * t + c
                            dve.wait_ge(spread, it * 8 + (n + 1))
                            row = q_f[:, t, c * BANK:(c + 1) * BANK]
                            dve.tensor_tensor(row, row, bank[:, 2 + n % 4, :], ALU.mult).then_inc(q_scaled, 1)
                    dve.wait_ge(residual, (it + 1) * TILES)
                    for c in range(2):
                        dve.wait_ge(projected, it * 2 + (c + 1))
                        rows = x[:, bass.ds(it * TILES + 4 * c, 4), :].rearrange("p i d -> p (i d)")
                        dve.tensor_tensor(rows, rows, bank[:, 6 + c, :], ALU.add).then_inc(added, 1)

                turns(dve, B, turn)

            @block.scalar
            def _(act):
                act.wait_ge(prep_copied, 6)
                front.on_scalar(act, 0)

                def turn(it, first, last):
                    wait_past(act, projected, it * 2)
                    for n in range(8):
                        t, c = n // 2, n % 2
                        act.wait_ge(featured, it * 16 + (n + 1))
                        act.activation(q_f[:, t, c * BANK:(c + 1) * BANK], bank[:, 2 + n % 2, :], ACT.Exp,
                                       bias=bias_q[:, t:t + 1]).then_inc(q_ready, 1)
                    for i in range(TILES):
                        act.wait_ge(biased, it * TILES + (i + 1))
                        act.activation(k_f[:, i, :], k_raw[:, i % 2, :], ACT.Exp).then_inc(k_ready, 1)
                    if not last:
                        front.on_scalar(act, it + 1)

                turns(act, B, turn)

            @block.tensor
            def _(pe):
                pe.wait_ge(w_in, 160)
                for n, (weight, feat) in enumerate(((wq, fq), (wk, fk))):
                    for hd in range(H):
                        last = pe.matmul(bank[:, n, hd * F:(hd + 1) * F], weight[:, hd, :], feat[:], start=True, stop=True)
                    last.then_inc(prepared, 1)
                pe.wait_ge(made, 2)
                for hd in range(H):
                    last = pe.matmul(bank[:, 2, hd * F:(hd + 1) * F], wide_bias[:, hd, :], fk[:], start=True, stop=True)
                last.then_inc(prepared, 1)
                for j in range(4):
                    last = pe.matmul(bank[32 * j:32 * j + 32, 3, 0:HT], fq[:],
                                     bq[:].rearrange("e (t j) -> e j t", j=4)[:, j, :], start=True, stop=True)
                last.then_inc(prepared, 1)
                for hd in range(H):
                    last = pe.matmul(bank[:, 4 + hd // 4, hd % 4 * D:(hd % 4 + 1) * D], wv[:, hd, :], wo[:, hd, :],
                                     start=True, stop=True)
                last.then_inc(prepared, 1)
                pe.wait_ge(made, 3)
                pe.wait_ge(prep_copied, 1)
                for hd in range(H):
                    j, t = hd % 4, hd // 4
                    last = pe.matmul(bank[32 * j:32 * j + 32, 0, t * D:(t + 1) * D], wide_bias[:, hd, 0:32],
                                     wo[:, hd, :], start=True, stop=True)
                last.then_inc(prepared, 1)
                pe.wait_ge(prep_copied, 6)
                pe.wait_ge(filled, 5)
                front.on_tensor(pe, 0)

                def turn(it, first, last):
                    pe.wait_ge(front.copied, (it + 1) * 2)
                    for n in range(8):
                        t, c = n // 2, n % 2
                        if n >= 2:
                            pe.wait_ge(q_ready, it * 8 + (n - 1))
                        pe.matmul(bank[:, 2 + n % 2, :], fold_q[:, t * P:(t + 1) * P],
                                  front.h_t[:, c * BANK:(c + 1) * BANK], start=True, stop=True).then_inc(featured, 1)
                    for i in range(TILES):
                        if i >= 2:
                            pe.wait_ge(biased, it * TILES + (i - 1))
                        pe.matmul(bank[:, 4 + i % 2, :], front.h_t[:, i * P:(i + 1) * P], fold_k[:],
                                  start=True, stop=True).then_inc(featured, 1)
                    wait_past(pe, added, it * 2)
                    for i in range(TILES):
                        pe.wait_ge(k_ready, it * TILES + (i + 1))
                        mm = pe.matmul(bank[:, 6, :], front.h[:, i, 0:D], k_f[:, i, :], start=(i == 0),
                                         stop=(i == TILES - 1))
                    mm.then_inc(summed, 1)
                    pe.wait_ge(sum_copied, it * 2 + 1)
                    for hd in range(H):
                        j, t = hd % 4, hd // 4
                        mm = pe.matmul(bank[32 * j:32 * j + 32, 0, t * D:(t + 1) * D], sums[:, hd * F:(hd + 1) * F],
                                         fold_v[:, hd, :], start=True, stop=True)
                    mm.then_inc(headed, 1)
                    pe.wait_ge(tiles_added, (it + 1) * (TILES - 1))
                    for t in range(HT):
                        mm = pe.matmul(bank[:, 7, t:t + 1], k_total[:, t * P:(t + 1) * P], ones[:], start=True, stop=True)
                    mm.then_inc(summed, 1)
                    pe.wait_ge(blocks_made, it + 1)
                    pe.wait_ge(q_ready, (it + 1) * 8)
                    for i in range(TILES):
                        for t in range(HT):
                            mm = pe.matmul(bank[:, 1, i * H + t * 4:i * H + t * 4 + 4], q_f[:, t, i * P:(i + 1) * P],
                                             blocks[:, t, :], start=True, stop=True)
                    mm.then_inc(divided, 1)
                    pe.wait_ge(inverted, it + 1)
                    pe.transpose(bank[:, 1, P:2 * P], inverse[:], core.ident[:]).then_inc(inv_turned, 1)
                    pe.wait_ge(inv_copied, it + 1)
                    for t in range(HT):
                        for c in range(2):
                            n = 2 * t + c
                            if n >= 4:
                                pe.wait_ge(q_scaled, it * 8 + (n - 3))
                            for i in range(4):
                                col = (4 * c + i) * H + t * 4
                                mm = pe.matmul(bank[:, 2 + n % 4, i * P:(i + 1) * P],
                                                 spreads[:, col:col + 4, :].rearrange("p j f -> p (j f)"),
                                                 inverse_t[:], start=True, stop=True)
                            mm.then_inc(spread, 1)
                    if not last:
                        front.on_tensor(pe, it + 1)
                    pe.wait_ge(q_scaled, (it + 1) * 8)
                    pe.wait_ge(head_ready, (it + 1) * HT)
                    for c in range(2):
                        for i in range(4):
                            for t in range(HT):
                                mm = pe.matmul(bank[:, 6 + c, i * D:(i + 1) * D],
                                                 q_f[:, t, (4 * c + i) * P:(4 * c + i + 1) * P], head[:, t, :],
                                                 start=(t == 0), stop=(t == HT - 1))
                        mm.then_inc(projected, 1)

                turns(pe, B, turn)


EXPERTS, HIDDEN, HC = 8, 512, 4
ROUTER_EPS = 1e-6
BIAS_BANK = 4


class Mixture:

    def __init__(self, core, ctx, name):
        nc = core.nc
        self.core, self.name = core, name
        core.stage = name
        sb = lambda n, shape, dtype=F32: core.sbuf(ctx, n, shape, dtype)
        self.w1 = [sb(f"w1_{part}", [P, EXPERTS, HIDDEN], F32R) for part in ("high", "low")]
        self.w2 = [sb(f"w2_{part}", [P, EXPERTS * HC, D], F32R) for part in ("high", "low")]
        self.b1 = sb("b1_folded", [P, EXPERTS * HC])
        self.b2 = sb("b2", [P, EXPERTS])
        self.x_parts = [sb(f"x_{part}", [P, B * T], F32R) for part in ("high", "low")]
        self.gates_t = nc.dram_tensor(f"{name}_gates_t", [EXPERTS, B * T], F32, kind="Internal").ap()


class RawWeights:

    def __init__(self, core, ctx, mx):
        core.stage = mx.name + "_w"
        sb = lambda name, shape: core.sbuf(ctx, name, shape)
        self.b2 = mx.b2
        self.w1, self.w2 = sb("w1", [P, EXPERTS, HIDDEN]), sb("w2", [P, EXPERTS * HC, D])
        self.scale, self.shift, self.b1 = sb("scale", [P, EXPERTS]), sb("shift", [P, EXPERTS]), sb("b1", [P, EXPERTS * HC])
        self.core, self.loaded, self.folded = core, core.sem("loaded"), core.sem("folded")

    def load(self, sp, w):
        for tile, source in ((self.scale, w["scale"]), (self.shift, w["shift"]), (self.b1, w["b1"]), (self.b2, w["b2"]),
                             (self.w1, w["w1"].rearrange("e d n -> d e n")),
                             (self.w2, w["w2"].rearrange("e (c p) d -> p (e c) d", p=P))):
            sp.dma_start(tile[:], source).then_inc(self.loaded, 16)

    def fold_shift(self, pe, experts):
        for e in experts:
            for c in range(HC):
                n = e * HC + c
                last = pe.matmul(self.core.bank[:, BIAS_BANK, n:n + 1], self.w1[:, e, c * P:(c + 1) * P],
                                 self.shift[:, e:e + 1], start=True, stop=True)
        last.then_inc(self.folded, 1)


def mixture_weights_stage(core, mx, raw):
    nc, bank = core.nc, core.bank
    core.stage = mx.name + "_w"
    s_ = core.sem
    scaled, rest_scaled, cut, b1_done = s_("scaled"), s_("rest_scaled"), s_("cut"), s_("b1_done")
    w1 = raw.w1
    with nc.Block() as block:

        @block.vector
        def _(dve):
            dve.tensor_tensor(mx.b1[:], bank[:, BIAS_BANK, 0:EXPERTS * HC], raw.b1[:], ALU.add).then_inc(b1_done, 1)
            for e in range(EXPERTS // 2):
                dve.tensor_scalar(w1[:, e, :], w1[:, e, :], raw.scale[:, e:e + 1], None, ALU.mult).then_inc(scaled, 1)
            dve.wait_ge(scaled, EXPERTS // 2)
            dve.wait_ge(rest_scaled, EXPERTS // 2)
            dve.tensor_copy(mx.w1[0][:], w1[:]).then_inc(cut, 1)
            dve.wait_ge(cut, 1)
            dve.tensor_tensor(mx.w1[1][:], w1[:], mx.w1[0][:].bitcast(F32), ALU.subtract).then_inc(cut, 1)

        @block.scalar
        def _(act):
            for e in range(EXPERTS // 2, EXPERTS):
                act.activation(w1[:, e, :], w1[:, e, :], ACT.Copy, scale=raw.scale[:, e:e + 1]).then_inc(rest_scaled, 1)


def route_stage(core, mx, w, raw):
    nc, bank = core.nc, core.bank
    core.stage = mx.name + "_r"
    s_ = core.sem
    w_in, mask_made, prep, prep_mm, widened = s_("w_in"), s_("mask_made"), s_("prep"), s_("prep_mm"), s_("widened")
    routed, steps, exped, gates_turned, gates_copied, gates_out, kept = (
        s_("routed"), s_("steps"), s_("exped"), s_("gates_turned"), s_("gates_copied"), s_("gates_out"), s_("kept"))
    w2_cut, w2_rest_cut = s_("w2_cut"), s_("w2_rest_cut")
    E = EXPERTS
    with ExitStack() as ctx:
        sb = lambda name, shape, dtype=F32: core.sbuf(ctx, name, shape, dtype)
        front = Front(core, ctx, second_eps=ROUTER_EPS)
        wr, wr_scaled, scale, shift = sb("wr", [P, E]), sb("wr_scaled", [P, E]), sb("scale", [P, 1]), sb("shift", [P, 1])
        shift_wide = sb("shift_wide", [P, P])
        router_b, bias = sb("router_b", [P, E]), sb("bias", [P, E])
        earlier = sb("earlier", [P, E, E])
        logit, e_ = sb("logit", [P, TILES, E]), sb("e", [P, TILES, E])
        row_max, row_sum, row_inv = sb("row_max", [P, TILES]), sb("row_sum", [P, TILES]), sb("row_inv", [P, TILES])
        above, equal = sb("above", [P, TILES, E, E]), sb("equal", [P, TILES, E, E])
        rank, chosen = sb("rank", [P, TILES, E]), sb("chosen", [P, TILES, E])
        gates, gates_rows = sb("gates", [P, E, TILES]), sb("gates_rows", [E * TILES, P])
        with nc.Block() as block:

            @block.sync
            def _(sp):
                for tile, source in ((wr, w["router_w"]), (scale, w["router_scale"]), (shift, w["router_shift"])):
                    sp.dma_start(tile[:], source).then_inc(w_in, 16)
                sp.dma_start(router_b[:], w["router_b"].partition_broadcast(P)).then_inc(w_in, 16)
                raw.load(sp, w)
                with sp.Fori(0, B) as it:
                    sp.wait_ge(gates_copied, it + 1)
                    dst = mx.gates_t[:, bass.ds(it * T, T)].rearrange("e (i p) -> e i p", p=P)
                    sp.dma_start(dst, gates_rows[:]).then_inc(gates_out, 16)
                sp.wait_ge(gates_out, 16 * B)

            @block.gpsimd
            def _(pool):
                front.on_gpsimd(pool, 0)
                pool.memset(earlier[:], 1.0).then_inc(mask_made, 1)
                pool.wait_ge(mask_made, 1)
                pool.affine_select(out=earlier[:], in_=earlier[:], compare_op=ALU.is_gt, fill=0.0, base=0,
                                   pattern=[[1, E], [-1, E]], channel_multiplier=0).then_inc(mask_made, 1)
                with pool.Fori(1, B) as it:
                    front.on_gpsimd(pool, it)
                pool.wait_ge(w2_cut, 1)
                pool.tensor_tensor(mx.w2[1][:], raw.w2[:], mx.w2[0][:].bitcast(F32), ALU.subtract).then_inc(w2_rest_cut, 1)

            @block.vector
            def _(dve):
                front.on_vector(dve, 0)
                dve.wait_ge(w_in, 64)
                dve.wait_ge(mask_made, 2)
                dve.tensor_scalar(wr_scaled[:], wr[:], scale[:], None, ALU.mult).then_inc(widened, 1)
                dve.tensor_copy(shift_wide[:], shift[:].broadcast_to([P, P])).then_inc(widened, 1)
                dve.wait_ge(prep_mm, 1)
                dve.tensor_tensor(bias[:], bank[:, 3, 0:E], router_b[:], ALU.add).then_inc(prep, 1)
                dve.wait_ge(prep, 1)

                def turn(it, first, last):
                    base = it * 11
                    if not last:
                        dve.wait_ge(front.normed, (it + 1) * TILES)
                        front.ln.moments_of(dve, it + 1)
                    dve.wait_ge(front.copied, (it + 1) * 2)
                    high, low = (part[:, bass.ds(it * T, T)] for part in mx.x_parts)
                    dve.tensor_copy(high, front.h_t[:]).then_inc(kept, 1)
                    dve.wait_ge(kept, it * 3 + 1)
                    dve.tensor_tensor(low, front.h_t[:], high.bitcast(F32), ALU.subtract).then_inc(kept, 1)

                    def step(n, instruction):
                        instruction.then_inc(steps, 1)
                        dve.wait_ge(steps, base + n)

                    dve.wait_ge(routed, it + 1)
                    logits = bank[:, 2, 0:TILES * E].rearrange("p (i e) -> p i e", e=E)
                    step(1, dve.tensor_tensor(logit[:], logits, bias[:].unsqueeze(1).broadcast_to([P, TILES, E]), ALU.add))
                    step(2, dve.tensor_reduce(row_max[:], logit[:], AX, ALU.max))
                    step(3, dve.tensor_tensor(logit[:], logit[:], row_max[:].unsqueeze(2).broadcast_to([P, TILES, E]),
                                              ALU.subtract))
                    dve.wait_ge(exped, it + 1)
                    mine = e_[:].unsqueeze(3).broadcast_to([P, TILES, E, E])
                    other = e_[:].unsqueeze(2).broadcast_to([P, TILES, E, E])
                    step(4, dve.tensor_tensor(above[:], other, mine, ALU.is_gt))
                    step(5, dve.tensor_tensor(equal[:], other, mine, ALU.is_equal))
                    tie = earlier[:].unsqueeze(1).broadcast_to([P, TILES, E, E])
                    step(6, dve.tensor_tensor(equal[:], equal[:], tie, ALU.mult))
                    step(7, dve.tensor_tensor(above[:], above[:], equal[:], ALU.add))
                    if not last:
                        front.normalise(dve, it + 1)
                    step(8, dve.tensor_reduce(rank[:], above[:], AX, ALU.add))
                    step(9, dve.scalar_tensor_tensor(chosen[:], rank[:], 1.5, e_[:], ALU.is_lt, ALU.mult))
                    step(10, dve.tensor_reduce(row_sum[:], chosen[:], AX, ALU.add))
                    step(11, dve.reciprocal(row_inv[:], row_sum[:]))
                    wait_past(dve, gates_turned, it)
                    dve.tensor_tensor(gates[:].rearrange("p e i -> p i e"), chosen[:],
                                      row_inv[:].unsqueeze(2).broadcast_to([P, TILES, E]), ALU.mult).then_inc(kept, 1)

                turns(dve, B, turn)

            @block.scalar
            def _(act):
                front.on_scalar(act, 0)

                def turn(it, first, last):
                    act.wait_ge(steps, it * 11 + 3)
                    act.activation(e_[:], logit[:], ACT.Exp).then_inc(exped, 1)
                    if not last:
                        act.wait_ge(kept, it * 3 + 2)
                        front.on_scalar(act, it + 1)
                    act.wait_ge(gates_turned, it + 1)
                    wait_past(act, gates_out, it * 16)
                    act.activation(gates_rows[:], bank[0:E * TILES, 3, 0:P], ACT.Copy).then_inc(gates_copied, 1)
                    if first:
                        act.wait_ge(raw.loaded, 96)
                        act.activation(mx.w2[0][:], raw.w2[:], ACT.Copy).then_inc(w2_cut, 1)

                turns(act, B, turn)

            @block.tensor
            def _(pe):
                pe.wait_ge(widened, 2)
                pe.matmul(bank[:, 3, 0:E], shift_wide[:], wr[:], start=True, stop=True).then_inc(prep_mm, 1)
                pe.wait_ge(prep, 1)

                def route(it, logits_read):
                    front.on_tensor(pe, it)
                    pe.wait_ge(front.copied, (it + 1) * 2)
                    if logits_read is not None:
                        pe.wait_ge(steps, logits_read)
                    for i in range(TILES):
                        mm = pe.matmul(bank[:, 2, i * E:(i + 1) * E], front.h_t[:, i * P:(i + 1) * P], wr_scaled[:],
                                       start=True, stop=True)
                    mm.then_inc(routed, 1)

                route(0, None)

                def turn(it, first, last):
                    if not last:
                        route(it + 1, it * 11 + 1)
                    else:
                        raw.fold_shift(pe, range(EXPERTS // 2, EXPERTS))
                    if not first:
                        wait_apart(core, pe, gates_copied, it)
                    wait_apart(core, pe, kept, it * 3 + 3)
                    pe.transpose(bank[0:E * TILES, 3, 0:P], gates[:].rearrange("p e i -> p (e i)"),
                                 core.ident[:]).then_inc(gates_turned, 1)
                    if first:
                        pe.wait_ge(raw.loaded, 96)
                        raw.fold_shift(pe, range(EXPERTS // 2))

                turns(pe, B, turn)


def experts_stage(core, mx):
    nc, x, bank = core.nc, core.x, core.bank
    core.stage = mx.name + "_e"
    s_ = core.sem
    CHUNKS, STEPS, LAG, RING, GATES = B * T // BANK, EXPERTS * HC, 3, 8, 4
    TURN_AT = 6
    gate_in = [s_(f"gate_in{k}") for k in range(GATES)]
    hidden, active, high_cut, cut, met = s_("hidden"), s_("active"), s_("high_cut"), s_("cut"), s_("met")
    gated, summed, turned, added = s_("gated"), s_("summed"), s_("turned"), s_("added")
    HID, OUT, TURN = 0, 4, 6
    PRODUCTS = ((0, 0), (0, 1), (1, 0))
    with ExitStack() as ctx:
        sb = lambda name, shape, dtype=F32: core.sbuf(ctx, name, shape, dtype)
        gate = sb("gate", [P, GATES, BANK])
        h = sb("h", [P, RING, BANK])
        h_parts = [sb("h_high", [P, RING, BANK], F32R), sb("h_low", [P, RING, BANK], F32R)]
        part = sb("part", [P, 2, BANK])
        total = sb("total", [P, BANK])
        with nc.Block() as block:

            @block.sync
            def _(sp):
                def chunk(it):
                    for e in range(EXPERTS):
                        wait_past(sp, gated, it * EXPERTS + (e - GATES + 1))
                        src = mx.gates_t[e:e + 1, bass.ds(it * BANK, BANK)].broadcast_to([P, BANK])
                        sp.dma_start(gate[:, e % GATES, :], src).then_inc(gate_in[e % GATES], 16)

                chunk(0)
                with sp.Fori(1, CHUNKS) as it:
                    chunk(it)

            @block.vector
            def _(dve):
                def gated_part(it, e):
                    dve.wait_ge(met, it * STEPS + HC * (e + 1))
                    dve.wait_ge(gate_in[e % GATES], it * 32 + 16 * (e // GATES + 1))
                    wait_past(dve, summed, it * EXPERTS + (e - 1))
                    dve.scalar_tensor_tensor(part[:, e % 2, :], bank[:, OUT + e % 2, :],
                                             mx.b2[:, e % EXPERTS:e % EXPERTS + 1], gate[:, e % GATES, :],
                                             ALU.add, ALU.mult).then_inc(gated, 1)

                def add_chunk(it):
                    dve.wait_ge(turned, it + 1)
                    rows = x[:, bass.ds(it * 4, 4), :].rearrange("p i d -> p (i d)")
                    dve.tensor_tensor(rows, rows, bank[:, TURN, :], ALU.add).then_inc(added, 1)

                def chunk(it, first):
                    for s in range(STEPS):
                        n, slot = it * STEPS + s, s % RING
                        dve.wait_ge(active, n + 1)
                        wait_past(dve, met, it * STEPS + (s - RING + 1))
                        dve.tensor_copy(h_parts[0][:, slot, :], h[:, slot, :]).then_inc(high_cut, 1)
                        dve.wait_ge(high_cut, n + 1)
                        dve.tensor_tensor(h_parts[1][:, slot, :], h[:, slot, :], h_parts[0][:, slot, :].bitcast(F32),
                                          ALU.subtract).then_inc(cut, 1)
                        if s % HC == HC - 1 and not (first and s < HC):
                            gated_part(it, (s - LAG - HC) // HC)
                        if s == TURN_AT + 2 and not first:
                            add_chunk(it - 1)

                chunk(0, True)
                with dve.Fori(1, CHUNKS) as it:
                    chunk(it, False)
                gated_part(CHUNKS, -1)
                add_chunk(CHUNKS - 1)

            @block.gpsimd
            def _(pool):
                def chunk(it):
                    for e in range(EXPERTS):
                        if e == 0:
                            wait_apart(core, pool, turned, it)
                            wait_apart(core, pool, gated, it * EXPERTS + 1)
                            pool.tensor_copy(total[:], part[:, 0, :]).then_inc(summed, 1)
                        else:
                            pool.wait_ge(gated, it * EXPERTS + (e + 1))
                            pool.wait_ge(summed, it * EXPERTS + e)
                            pool.tensor_tensor(total[:], total[:], part[:, e % 2, :], ALU.add).then_inc(summed, 1)

                chunk(0)
                with pool.Fori(1, CHUNKS) as it:
                    chunk(it)

            @block.scalar
            def _(act):
                def chunk(it):
                    for s in range(STEPS):
                        act.wait_ge(hidden, it * STEPS + (s + 1))
                        wait_past(act, cut, it * STEPS + (s - RING + 1))
                        act.activation(h[:, s % RING, :], bank[:, HID + s % 4, :], ACT.Gelu,
                                       bias=mx.b1[:, s:s + 1]).then_inc(active, 1)

                chunk(0)
                with act.Fori(1, CHUNKS) as it:
                    chunk(it)

            @block.tensor
            def _(pe):
                def to_hidden(it, s):
                    wait_past(pe, active, it * STEPS + (s - 3))
                    e, c = s // HC, s % HC
                    for n, (a, b) in enumerate(PRODUCTS):
                        last = pe.matmul(bank[:, HID + s % 4, :], mx.w1[a][:, e, c * P:(c + 1) * P],
                                         mx.x_parts[b][:, bass.ds(it * BANK, BANK)], start=(n == 0), stop=(n == 2))
                    last.then_inc(hidden, 1)

                def to_output(it, s):
                    pe.wait_ge(cut, it * STEPS + (s + 1))
                    e, c = s // HC, s % HC
                    if c == 0:
                        wait_past(pe, gated, it * EXPERTS + (e - 1))
                    for n, (a, b) in enumerate(PRODUCTS):
                        last = pe.matmul(bank[:, OUT + e % 2, :], mx.w2[a][:, s % STEPS, :], h_parts[b][:, s % RING, :],
                                         start=(c == 0 and n == 0), stop=(c == HC - 1 and n == 2))
                    last.then_inc(met, 1)

                def turn_chunk(it):
                    pe.wait_ge(summed, (it + 1) * EXPERTS)
                    wait_past(pe, added, it)
                    for i in range(4):
                        last = pe.transpose(bank[:, TURN, i * P:(i + 1) * P], total[:, i * P:(i + 1) * P], core.ident[:])
                    last.then_inc(turned, 1)

                def chunk(it, first):
                    for s in range(STEPS):
                        to_hidden(it, s)
                        if not (first and s < LAG):
                            to_output(it, s - LAG)
                        if s == TURN_AT and not first:
                            turn_chunk(it - 1)

                chunk(0, True)
                with pe.Fori(1, CHUNKS) as it:
                    chunk(it, False)
                for s in range(-LAG, 0):
                    to_output(CHUNKS, s)
                turn_chunk(CHUNKS - 1)


def mixture_layer(core, name, w):
    with ExitStack() as ctx:
        mx = Mixture(core, ctx, name)
        with ExitStack() as raw_ctx:
            raw = RawWeights(core, raw_ctx, mx)
            route_stage(core, mx, w, raw)
            mixture_weights_stage(core, mx, raw)
        experts_stage(core, mx)



def recurrent_stage(core, w):
    nc, x, bank = core.nc, core.x, core.bank
    core.stage = "rec"
    s_ = core.sem
    H, DH, RANK, PAIRS, UNITS = 16, 8, 16, 8, 16
    NORM, GATE_SCALE, Q_SCALE = 1e-5, 1.0 / 16.0, float(DH) ** -0.5
    w_in, filled, made, folded, fold_copied = s_("w_in"), s_("filled"), s_("made"), s_("folded"), s_("fold_copied")
    projected, proj_copied, gate_steps, gate_min, cut, rest_cut = (
        s_("projected"), s_("proj_copied"), s_("gate_steps"), s_("gate_min"), s_("cut"), s_("rest_cut"))
    gates_out, silu_ready = s_("gates_out"), s_("silu_ready")
    decay_spread, v_spread, k_spread, q_spread = s_("decay_spread"), s_("v_spread"), s_("k_spread"), s_("q_spread")
    decay_copied, v_copied, outer, scanned, read = (
        s_("decay_copied"), s_("v_copied"), s_("outer"), s_("scanned"), s_("read"))
    gathered, got, turned, squared, meaned, root_taken, root_steps, normed_out, silued = (
        s_("gathered"), s_("got"), s_("o_turned"), s_("squared"), s_("meaned"), s_("root_taken"), s_("root_steps"),
        s_("normed_out"), s_("silued"))
    DECAY, VALUE, KEY, QUERY, GATHERED, TAIL = 0, 1, 2, 4, 6, 7
    ORDER = (3, 0, 1, 2)
    y_turned, y_copied, out_done, added = s_("y_turned"), s_("y_copied"), s_("out_done"), s_("added")
    with ExitStack() as ctx:
        sb = lambda name, shape, dtype=F32: core.sbuf(ctx, name, shape, dtype)
        front = Front(core, ctx)
        wq, wk, wv, wg, wo = (sb(n, [P, D]) for n in ("wq", "wk", "wv", "wg", "wo"))
        g1, g2, fold_g, wo_normed = sb("g1", [RANK, D]), sb("g2", [RANK, D]), sb("fold_g", [P, D]), sb("wo_normed", [P, D])
        g_bias, norm = sb("g_bias", [P, 1]), sb("norm", [P, 1])
        pick_d, pick_v = sb("pick_d", [P, PAIRS * P], F32R), sb("pick_v", [P, PAIRS * P], F32R)
        same = sb("same", [P, 2 * DH])
        gather = sb("gather", [P, PAIRS, P])
        base = [sb(n, [P, T]) for n in ("q_t", "k_t", "v_t", "z_t")]
        size, floor, decay = sb("size", [P, T]), sb("floor", [P, T]), sb("decay", [P, T])
        high = [sb(f"{n}_high", [P, T], F32R) for n in ("q", "k", "v", "decay")]
        low = [sb(f"{n}_low", [P, T], F32R) for n in ("q", "k", "v", "decay")]
        silu = sb("silu", [P, TILES, D])
        decay_p, v_p, kv = sb("decay_p", [P, 2, BANK]), sb("v_p", [P, 2, BANK]), sb("kv", [P, 2, BANK])
        state = sb("state", [P, 2, PAIRS, BANK])
        q_state = sb("q_state", [P, 2, BANK])
        o_t, square, y, y_t = sb("o_t", [P, BANK]), sb("square", [P, BANK]), sb("y", [P, BANK]), sb("y_t", [P, BANK])
        mean, root, step = sb("mean", [P, 4 * H]), sb("root", [P, 4 * H]), sb("step", [P, 4 * H])
        with nc.Block() as block:

            @block.sync
            def _(sp):
                for tile, source in ((wq, "q"), (wk, "k"), (wv, "v"), (wg, "g"), (wo, "o"), (g1, "g1"), (g2, "g2"),
                                     (g_bias, "g_bias")):
                    sp.dma_start(tile[:], w[source]).then_inc(w_in, 16)
                sp.dma_start(norm[:], w["norm"].rearrange("(o v) -> o v", o=1).broadcast_to([H, DH])).then_inc(w_in, 16)

            @block.gpsimd
            def _(pool):
                pool.memset(gather[:], 0.0).then_inc(filled, 1)
                with pool.Fori(0, B) as it:
                    front.on_gpsimd(pool, it)

            @block.vector
            def _(dve):
                ident = core.ident
                front.on_vector(dve, 0)
                dve.wait_ge(w_in, 144)
                dve.wait_ge(filled, 1)
                dve.tensor_scalar(wo_normed[:], wo[:], norm[:], None, ALU.mult).then_inc(made, 1)
                dve.tensor_copy(pick_d[:].rearrange("p (m v) -> p m v", v=DH),
                                ident[:].unsqueeze(2).broadcast_to([P, P, DH])).then_inc(made, 1)
                dve.tensor_copy(pick_v[:].rearrange("p (h d v) -> p h d v", d=DH, v=DH),
                                ident[:].rearrange("p (h v) -> p h v", v=DH).unsqueeze(2).broadcast_to(
                                    [P, H, DH, DH])).then_inc(made, 1)
                dve.tensor_reduce(same[:].rearrange("p (j v) -> p j v", v=DH),
                                  ident[:].rearrange("p (j d v) -> p j v d", d=DH, v=DH), AX, ALU.add).then_inc(made, 1)
                dve.wait_ge(made, 4)
                for s in range(PAIRS):
                    dve.tensor_copy(gather[:, s, 2 * DH * s:2 * DH * (s + 1)], same[:]).then_inc(made, 1)
                dve.wait_ge(folded, 1)
                dve.tensor_copy(fold_g[:], bank[:, TAIL, 0:D]).then_inc(fold_copied, 1)

                def tail(it, c, part):
                    n = it * 2 + c
                    rows = bank[:, TAIL, :].rearrange("p (g v) -> p g v", v=DH)
                    if part == 0:
                        dve.wait_ge(squared, n + 1)
                        dve.tensor_reduce(mean[:], square[:].rearrange("p (g v) -> p g v", v=DH), AX,
                                          ALU.add).then_inc(meaned, 1)
                        dve.wait_ge(meaned, n * 2 + 1)
                        dve.tensor_scalar(mean[:], mean[:], 1.0 / DH, NORM, ALU.mult, ALU.add).then_inc(meaned, 1)
                    if part == 1:
                        dve.wait_ge(root_taken, n + 1)
                        dve.reciprocal(root[:], root[:]).then_inc(root_steps, 1)
                        dve.wait_ge(root_steps, n * 5 + 1)
                        dve.tensor_tensor(step[:], root[:], root[:], ALU.mult).then_inc(root_steps, 1)
                        dve.wait_ge(root_steps, n * 5 + 2)
                        dve.tensor_tensor(step[:], step[:], mean[:], ALU.mult).then_inc(root_steps, 1)
                        dve.wait_ge(root_steps, n * 5 + 3)
                        dve.tensor_scalar(step[:], step[:], -0.5, 1.5, ALU.mult, ALU.add).then_inc(root_steps, 1)
                        dve.wait_ge(root_steps, n * 5 + 4)
                        dve.tensor_tensor(root[:], root[:], step[:], ALU.mult).then_inc(root_steps, 1)
                        dve.wait_ge(root_steps, n * 5 + 5)
                        dve.tensor_tensor(y[:].rearrange("p (g v) -> p g v", v=DH), rows,
                                          root[:].unsqueeze(2).broadcast_to([P, 4 * H, DH]), ALU.mult).then_inc(normed_out, 1)
                        dve.wait_ge(normed_out, n + 1)
                        dve.wait_ge(silu_ready, it * 2 + 2)
                        dve.tensor_tensor(y[:], y[:], silu[:, 4 * c:4 * c + 4, :].rearrange("p i d -> p (i d)"),
                                          ALU.mult).then_inc(silued, 1)
                    if part == 2:
                        dve.wait_ge(out_done, n + 1)
                        row = x[:, bass.ds(it * TILES + 4 * c, 4), :].rearrange("p i d -> p (i d)")
                        dve.tensor_tensor(row, row, bank[:, TAIL, :], ALU.add).then_inc(added, 1)

                def outer_product(it, c, s):
                    u, slot = it * UNITS + (8 * c + s), s % 2
                    dve.wait_ge(k_spread, u + 1)
                    dve.wait_ge(v_copied, u + 1)
                    dve.tensor_tensor(kv[:, slot, :], bank[:, KEY + slot, :], v_p[:, slot, :], ALU.mult).then_inc(outer, 1)

                def turn(it, first, last):
                    if not first:
                        front.on_vector(dve, it)
                        tail(it - 1, 1, 0)
                    dve.wait_ge(proj_copied, it * 8 + 2)
                    dve.tensor_scalar(floor[:], base[3][:], 0.0, None, ALU.min).then_inc(gate_min, 1)
                    for n in range(3):
                        dve.wait_ge(proj_copied, it * 8 + 2 * (n + 2))
                        dve.tensor_copy(high[n][:], base[n][:]).then_inc(cut, 1)
                        if n == 1:
                            dve.wait_ge(gate_min, it * 2 + 1)
                            dve.wait_ge(gate_steps, it * 3 + 3)
                            dve.tensor_tensor(floor[:], floor[:], size[:], ALU.subtract).then_inc(gate_min, 1)
                        dve.wait_ge(cut, it * 4 + (n + 1))
                        dve.tensor_tensor(low[n][:], base[n][:], high[n][:].bitcast(F32), ALU.subtract).then_inc(rest_cut, 1)
                        if n == 0 and not first:
                            tail(it - 1, 1, 1)
                    dve.wait_ge(gates_out, it + 1)
                    dve.tensor_copy(high[3][:], decay[:]).then_inc(cut, 1)
                    dve.wait_ge(cut, it * 4 + 4)
                    dve.tensor_tensor(low[3][:], decay[:], high[3][:].bitcast(F32), ALU.subtract).then_inc(rest_cut, 1)
                    if not first:
                        tail(it - 1, 1, 2)
                    outer_product(it, 0, 0)
                    for c in range(2):
                        for s in range(PAIRS):
                            u, slot = it * UNITS + (8 * c + s), s % 2
                            dve.wait_ge(outer, u + 1)
                            dve.wait_ge(decay_copied, u + 1)
                            start = 0.0 if c == 0 else state[:, 0, s, BANK - 1:BANK]
                            dve.tensor_tensor_scan(state[:, c, s, :], decay_p[:, slot, :], kv[:, slot, :], start,
                                                   ALU.mult, ALU.add).then_inc(scanned, 1)
                            if 8 * c + s < UNITS - 1:
                                outer_product(it, (8 * c + s + 1) // 8, (s + 1) % 8)
                            dve.wait_ge(scanned, u + 1)
                            dve.wait_ge(q_spread, u + 1)
                            wait_past(dve, gathered, u - 1)
                            dve.tensor_tensor(q_state[:, slot, :], state[:, c, s, :], bank[:, QUERY + slot, :],
                                              ALU.mult).then_inc(read, 1)
                            if c == 1 and s in (3, 5, 7):
                                tail(it, 0, (s - 3) // 2)
                    if last:
                        for part in range(3):
                            tail(it, 1, part)

                turns(dve, B, turn)

            @block.scalar
            def _(act):
                act.wait_ge(w_in, 144)

                def tail(it, c, part):
                    n = it * 2 + c
                    if part == 0:
                        act.wait_ge(gathered, it * UNITS + 8 * (c + 1))
                        act.activation(o_t[:], bank[:, GATHERED, :], ACT.Copy).then_inc(got, 1)
                    if part == 1:
                        act.wait_ge(turned, n + 1)
                        act.activation(square[:], bank[:, TAIL, :], ACT.Square).then_inc(squared, 1)
                    if part == 2:
                        act.wait_ge(meaned, n * 2 + 2)
                        act.activation(root[:], mean[:], ACT.Sqrt).then_inc(root_taken, 1)
                    if part == 3:
                        act.wait_ge(y_turned, n + 1)
                        act.activation(y_t[:], bank[:, TAIL, :], ACT.Copy).then_inc(y_copied, 1)

                def turn(it, first, last):
                    if not first:
                        tail(it - 1, 1, 0)
                        tail(it - 1, 1, 1)
                    front.on_scalar(act, it)
                    if not first:
                        tail(it - 1, 1, 2)
                    act.wait_ge(rest_cut, it * 4)
                    for at, n in enumerate(ORDER):
                        for c in range(2):
                            act.wait_ge(projected, it * 10 + (2 * at + c + 1))
                            dst, src = base[n][:, c * BANK:(c + 1) * BANK], bank[:, 2 + (2 * at + c) % 4, :]
                            if n == 3:
                                act.activation(dst, src, ACT.Identity, bias=g_bias[:]).then_inc(proj_copied, 1)
                            else:
                                act.activation(dst, src, ACT.Copy, scale=Q_SCALE if n == 0 else 1.0).then_inc(proj_copied, 1)
                        if at == 0:
                            act.wait_ge(proj_copied, it * 8 + 2)
                            act.activation(size[:], base[3][:], ACT.Abs).then_inc(gate_steps, 1)
                            act.wait_ge(gate_steps, it * 3 + 1)
                            act.activation(size[:], size[:], ACT.Exp, scale=-1.0).then_inc(gate_steps, 1)
                            act.wait_ge(gate_steps, it * 3 + 2)
                            act.activation(size[:], size[:], ACT.Ln, bias=1.0).then_inc(gate_steps, 1)
                        if at == 2 and not first:
                            tail(it - 1, 1, 3)
                    act.wait_ge(gate_min, it * 2 + 2)
                    act.activation(decay[:], floor[:], ACT.Exp, scale=GATE_SCALE).then_inc(gates_out, 1)
                    for c in range(2):
                        act.wait_ge(projected, it * 10 + (9 + c))
                        act.activation(silu[:, 4 * c:4 * c + 4, :].rearrange("p i d -> p (i d)"), bank[:, 6 + c, :],
                                       ACT.Silu).then_inc(silu_ready, 1)
                    for c in range(2):
                        for s in range(PAIRS):
                            u, slot = it * UNITS + (8 * c + s), s % 2
                            act.wait_ge(v_spread, u + 1)
                            wait_past(act, outer, u - 1)
                            act.activation(v_p[:, slot, :], bank[:, VALUE, :], ACT.Copy).then_inc(v_copied, 1)
                            act.wait_ge(decay_spread, u + 1)
                            wait_past(act, scanned, u - 1)
                            act.activation(decay_p[:, slot, :], bank[:, DECAY, :], ACT.Copy).then_inc(decay_copied, 1)
                            if c == 1 and s in (1, 3, 4, 7):
                                tail(it, 0, (1, 3, 4, 7).index(s))
                    if last:
                        for part in range(4):
                            tail(it, 1, part)

                turns(act, B, turn)

            @block.tensor
            def _(pe):
                pe.wait_ge(w_in, 144)
                pe.matmul(bank[:, TAIL, 0:D], g1[:], g2[:], start=True, stop=True).then_inc(folded, 1)
                pe.wait_ge(fold_copied, 1)
                pe.wait_ge(made, 12)

                def spread_pair(it, c, s):
                    u, slot = it * UNITS + (8 * c + s), s % 2
                    cols, pick = slice(c * BANK, (c + 1) * BANK), slice(s * P, (s + 1) * P)
                    for n, picks, dst, ready, free, back in (
                            (2, pick_v, VALUE, v_spread, v_copied, 1), (1, pick_d, KEY + slot, k_spread, outer, 2),
                            (3, pick_d, DECAY, decay_spread, decay_copied, 1), (0, pick_d, QUERY + slot, q_spread, read, 2)):
                        wait_past(pe, free, u + (1 - back))
                        pe.matmul(bank[:, dst, :], picks[:, pick], high[n][:, cols], start=True, stop=False)
                        pe.matmul(bank[:, dst, :], picks[:, pick], low[n][:, cols], start=False, stop=True).then_inc(ready, 1)

                def gather_pair(it, c, s):
                    u, slot = it * UNITS + (8 * c + s), s % 2
                    pe.wait_ge(read, u + 1)
                    if s == 0:
                        pe.wait_ge(got, it * 2 + c)
                    pe.matmul(bank[:, GATHERED, :], gather[:, s, :], q_state[:, slot, :], start=(s == 0),
                              stop=(s == PAIRS - 1)).then_inc(gathered, 1)

                def tail(it, c, part):
                    n = it * 2 + c
                    if part == 0:
                        pe.wait_ge(got, n + 1)
                        pe.wait_ge(added, n)
                        for i in range(4):
                            last = pe.transpose(bank[:, TAIL, i * P:(i + 1) * P], o_t[:, i * P:(i + 1) * P], core.ident[:])
                        last.then_inc(turned, 1)
                    if part == 1:
                        pe.wait_ge(silued, n + 1)
                        for i in range(4):
                            last = pe.transpose(bank[:, TAIL, i * P:(i + 1) * P], y[:, i * P:(i + 1) * P], core.ident[:])
                        last.then_inc(y_turned, 1)
                        pe.wait_ge(y_copied, n + 1)
                        for i in range(4):
                            last = pe.matmul(bank[:, TAIL, i * P:(i + 1) * P], y_t[:, i * P:(i + 1) * P], wo_normed[:],
                                             start=True, stop=True)
                        last.then_inc(out_done, 1)

                def turn(it, first, last):
                    if not first:
                        tail(it - 1, 1, 0)
                    front.on_tensor(pe, it)
                    pe.wait_ge(front.copied, (it + 1) * 2)
                    for at, n in enumerate(ORDER):
                        for c in range(2):
                            if at >= 2:
                                pe.wait_ge(proj_copied, it * 8 + (2 * at + c - 3))
                            pe.matmul(bank[:, 2 + (2 * at + c) % 4, :], (wq, wk, wv, fold_g)[n][:], front.h_t[:, c * BANK:(c + 1) * BANK],
                                      start=True, stop=True).then_inc(projected, 1)
                    if not first:
                        tail(it - 1, 1, 1)
                        pe.wait_ge(added, it * 2)
                    for c in range(2):
                        for i in range(4):
                            t = 4 * c + i
                            mm = pe.matmul(bank[:, 6 + c, i * P:(i + 1) * P], front.h_t[:, t * P:(t + 1) * P], wg[:],
                                           start=True, stop=True)
                        mm.then_inc(projected, 1)
                    pe.wait_ge(proj_copied, it * 8 + 8)
                    pe.wait_ge(silu_ready, it * 2 + 2)
                    pe.wait_ge(rest_cut, it * 4 + 4)
                    spread_pair(it, 0, 0)
                    for c in range(2):
                        for s in range(PAIRS):
                            if 8 * c + s < UNITS - 1:
                                spread_pair(it, (8 * c + s + 1) // 8, (s + 1) % 8)
                            if 8 * c + s > 0:
                                gather_pair(it, (8 * c + s - 1) // 8, (s - 1) % 8)
                            if c == 1 and s == 1:
                                tail(it, 0, 0)
                            if c == 1 and s == 6:
                                tail(it, 0, 1)
                    gather_pair(it, 1, PAIRS - 1)
                    if last:
                        tail(it, 1, 0)
                        tail(it, 1, 1)

                turns(pe, B, turn)


def program(nc, a, out):
    with ExitStack() as ctx:
        core = Core(nc, ctx)
        nested = {"q": a["L0_ffn_q_w_t"], "k": a["L0_ffn_k_w_t"], "v": a["L0_ffn_v_w_t"], "o": a["L0_ffn_o_w_t"],
                  "out_bias": a["L0_ffn_o_b"], "q_bias": a["L0_ffn_q_b"], "k_bias": a["L0_ffn_k_b"],
                  "v_bias": a["L0_ffn_v_b"], "norm_w": a["L0_ffn_norm_w"], "norm_b": a["L0_ffn_norm_b"]}
        wide = {"q": a["L0_attn_b_Wq_t"], "k": a["L0_attn_b_Wk_t"], "v": a["L0_attn_b_Wv_t"],
                "o": a["L0_attn_b_Wff_t"], "out_bias": a["L0_attn_b_bff"]}
        linear = {"q": a["L1_attn_a_Wq_t"], "k": a["L1_attn_a_Wk_t"], "v": a["L1_attn_a_Wv_t"],
                  "o": a["L1_attn_a_Wproj"], "fq": a["L1_attn_a_wq_feat"], "fk": a["L1_attn_a_wk_feat"],
                  "bq": a["L1_attn_a_bq"], "bk": a["L1_attn_a_bk"], "bv": a["L1_attn_a_bv"],
                  "out_bias": a["L1_attn_a_bproj"]}
        mixture = {"router_w": a["L1_ffn_router_w_t"], "router_scale": a["L1_ffn_router_ln_scale"],
                   "router_shift": a["L1_ffn_router_ln_bias"], "router_b": a["L1_ffn_router_b"],
                   "scale": a["L1_ffn_expert_ln_scale_t"], "shift": a["L1_ffn_expert_ln_bias_t"],
                   "w1": a["L1_ffn_w1_t"], "b1": a["L1_ffn_b1_t"], "w2": a["L1_ffn_w2_t"], "b2": a["L1_ffn_b2_t"]}
        recurrent = {"q": a["L1_attn_b_Wq"], "k": a["L1_attn_b_Wk"], "v": a["L1_attn_b_Wv"], "g": a["L1_attn_b_Wg"],
                     "o": a["L1_attn_b_Wo"], "g1": a["L1_attn_b_Wg1_t"], "g2": a["L1_attn_b_Wg2"],
                     "g_bias": a["L1_attn_b_bg2"], "norm": a["L1_attn_b_g_norm_w"]}
        plan = [
            lambda: causal_stage(core, a["L0_attn_a_Wq_t"], a["L0_attn_a_Wk_t"], a["L0_attn_a_Wv_t"]),
            lambda: heads_layer(core, "nested1", 8, nested, True),
            lambda: heads_layer(core, "wide", 16, wide, False),
            lambda: heads_layer(core, "nested2", 8, nested, True),
            lambda: kernel_attention_stage(core, linear),
            lambda: mixture_layer(core, "mix1", mixture),
            lambda: recurrent_stage(core, recurrent),
            lambda: mixture_layer(core, "mix2", mixture),
        ]
        load_stage(core, a["L0_attn_a_x"])
        for layer in plan:
            with nc.cleanup_on_exit():
                layer()
        store_stage(core, out)


_LAYOUT = [
    ("L0_attn_a_x", "L0_attn_a_x", False),
    ("L0_attn_a_Wq_t", "L0_attn_a_Wq", True),
    ("L0_attn_a_Wk_t", "L0_attn_a_Wk", True),
    ("L0_attn_a_Wv_t", "L0_attn_a_Wv", True),
    ("L0_attn_b_Wq_t", "L0_attn_b_Wq", True),
    ("L0_attn_b_Wk_t", "L0_attn_b_Wk", True),
    ("L0_attn_b_Wv_t", "L0_attn_b_Wv", True),
    ("L0_attn_b_Wff_t", "L0_attn_b_Wff", True),
    ("L0_attn_b_bff", "L0_attn_b_bff", False),
    ("L0_ffn_norm_w", "L0_ffn_norm_w", False),
    ("L0_ffn_norm_b", "L0_ffn_norm_b", False),
    ("L0_ffn_q_w_t", "L0_ffn_q_w", True),
    ("L0_ffn_q_b", "L0_ffn_q_b", False),
    ("L0_ffn_k_w_t", "L0_ffn_k_w", True),
    ("L0_ffn_k_b", "L0_ffn_k_b", False),
    ("L0_ffn_v_w_t", "L0_ffn_v_w", True),
    ("L0_ffn_v_b", "L0_ffn_v_b", False),
    ("L0_ffn_o_w_t", "L0_ffn_o_w", True),
    ("L0_ffn_o_b", "L0_ffn_o_b", False),
    ("L1_attn_a_Wq_t", "L1_attn_a_Wq", True),
    ("L1_attn_a_Wk_t", "L1_attn_a_Wk", True),
    ("L1_attn_a_Wv_t", "L1_attn_a_Wv", True),
    ("L1_attn_a_Wproj", "L1_attn_a_Wproj", False),
    ("L1_attn_a_wq_feat", "L1_attn_a_wq_feat", False),
    ("L1_attn_a_wk_feat", "L1_attn_a_wk_feat", False),
    ("L1_attn_a_bq", "L1_attn_a_bq", (16, 64)),
    ("L1_attn_a_bk", "L1_attn_a_bk", (16, 64)),
    ("L1_attn_a_bv", "L1_attn_a_bv", (16, 64)),
    ("L1_attn_a_bproj", "L1_attn_a_bproj", False),
    ("L1_attn_b_Wq", "L1_attn_b_Wq", False),
    ("L1_attn_b_Wk", "L1_attn_b_Wk", False),
    ("L1_attn_b_Wv", "L1_attn_b_Wv", False),
    ("L1_attn_b_Wg1_t", "L1_attn_b_Wg1", True),
    ("L1_attn_b_Wg2", "L1_attn_b_Wg2", False),
    ("L1_attn_b_bg2", "L1_attn_b_bg2", (1, D)),
    ("L1_attn_b_Wg", "L1_attn_b_Wg", False),
    ("L1_attn_b_g_norm_w", "L1_attn_b_g_norm_w", False),
    ("L1_attn_b_Wo", "L1_attn_b_Wo", False),
    ("L1_ffn_router_ln_scale", "L1_ffn_router_ln_scale", (1, D)),
    ("L1_ffn_router_ln_bias", "L1_ffn_router_ln_bias", (1, D)),
    ("L1_ffn_router_w_t", "L1_ffn_router_w", True),
    ("L1_ffn_router_b", "L1_ffn_router_b", False),
    ("L1_ffn_expert_ln_scale_t", "L1_ffn_expert_ln_scale", True),
    ("L1_ffn_expert_ln_bias_t", "L1_ffn_expert_ln_bias", True),
    ("L1_ffn_w1_t", "L1_ffn_w1", True),
    ("L1_ffn_b1_t", "L1_ffn_b1", (EXPERTS * HC, P)),
    ("L1_ffn_w2_t", "L1_ffn_w2", True),
    ("L1_ffn_b2_t", "L1_ffn_b2", True),
]


def laid_out(inputs):
    import numpy as np

    arrays = {}
    for name, source, swapped in _LAYOUT:
        v = np.asarray(inputs[source])
        if isinstance(swapped, tuple):
            v = v.reshape(swapped)
        arrays[name] = np.ascontiguousarray(np.swapaxes(v, -1, -2) if swapped else v)
    return arrays


def kernel(**inputs):
    import concourse.bacc as bacc
    from concourse.bass_utils import run_bass_kernel_spmd

    nc = bacc.Bacc("TRN2", target_bir_lowering=False, num_devices=1)
    arrays = laid_out(inputs)
    a = {n: nc.dram_tensor(n, v.shape, mybir.dt.from_np(v.dtype), kind="ExternalInput").ap()
         for n, v in arrays.items()}
    out = nc.dram_tensor("out", (B, T, D), F32, kind="ExternalOutput").ap()
    program(nc, a, out)
    return run_bass_kernel_spmd(nc, [arrays], core_ids=[0]).results[0]["out"]
```
